# Optimizing a Trainium2 kernel written in Bass

```python
import numpy as np
import jax
import jax.numpy as jnp

def _softmax(x, axis=-1):
    return jax.nn.softmax(x, axis=axis)

def _gelu(x):
    return jax.nn.gelu(x, approximate=True)

def _silu(x):
    return jax.nn.silu(x)

def _sigmoid(x):
    return jax.nn.sigmoid(x)

def _layernorm(x, axis=-1, eps=1e-05):
    m = jnp.mean(x, axis=axis, keepdims=True)
    v = jnp.var(x, axis=axis, keepdims=True)
    return (x - m) / jnp.sqrt(v + eps)

def _scatter_add(tgt, idx, src, axis=0):
    return tgt.at[idx].add(src)

def _segment_sum(src, seg, n):
    return jax.ops.segment_sum(src, seg, n)
kernel_name = 'mk_prb_d2_jaxref_r4_b6464d'

def setup_inputs(seed: int=0):
    np.random.seed(seed)
    _w = jnp.asarray

    def _L0_attn_setup():
        import jax, jax.numpy as jnp
        import numpy as np
        H = 16
        SPLAT_RATIO = 0.4
        STD_RATIO = 1.0 - SPLAT_RATIO
        key = jax.random.key(seed)
        ks = jax.random.split(key, 12)
        B, N, D, S = (2, 256, 256, 64)
        Db = D // 2
        f32 = jnp.float32
        n = lambda k, shape, s: jax.random.normal(k, shape, dtype=f32) * s
        return {'x': n(ks[0], (B, N, D), 1.0), 'Wq': n(ks[1], (D, D), 0.02), 'Wk': n(ks[2], (D, D), 0.02), 'Wv': n(ks[3], (D, D), 0.02), 'Wo': n(ks[4], (D, D), 0.02), 'splat_positions': n(ks[5], (S, D), 0.02), 'splat_scales': jnp.ones((S,), f32), 'splat_importance': jnp.ones((S,), f32), 'We': n(ks[6], (D, Db), 0.02), 'be': jnp.zeros((Db,), f32), 'Wt': n(ks[7], (S, Db, Db), 0.02), 'bt': jnp.zeros((S, Db), f32), 'Wd': n(ks[8], (Db, D), 0.02), 'bd': jnp.zeros((D,), f32), 'Wg': n(ks[9], (D, D), 0.02), 'bg': jnp.zeros((D,), f32)}
    _L0_attn_in = _L0_attn_setup()

    def _L0_ffn_setup():
        import math
        import jax, jax.numpy as jnp
        import numpy as np
        B, S, D, F, E = (8, 512, 256, 1024, 8)
        CAPACITY_FACTOR = 1.0
        key = jax.random.key(seed)
        k1, k2, k3, k4 = jax.random.split(key, 4)
        x = jax.random.normal(k1, (B, S, D), dtype=jnp.float32)
        Wr = jax.random.normal(k2, (D, E), dtype=jnp.float32) * (1.0 / math.sqrt(D))
        W1 = jax.random.normal(k3, (E, D, F), dtype=jnp.float32) * (1.0 / math.sqrt(D))
        W2 = jax.random.normal(k4, (E, F, D), dtype=jnp.float32) * (1.0 / math.sqrt(F))
        return {'x': x, 'Wr': Wr, 'W1': W1, 'W2': W2}
    _L0_ffn_in = _L0_ffn_setup()

    def _L1_attn_setup():
        import jax, jax.numpy as jnp
        import numpy as np
        B, N, D = (4, 512, 256)
        H, HD = (8, 64)
        FF = 1024
        ETA = 0.1
        DT = 0.01
        GAMMA_FLOOR = 0.1
        EPS = 1e-05

        def layernorm(x, g, b):
            m = jnp.mean(x, -1, keepdims=True)
            v = jnp.var(x, -1, keepdims=True)
            return (x - m) * jax.lax.rsqrt(v + EPS) * g + b

        def _cf_scan(d):
            dT = jnp.swapaxes(d, 0, 1)

            def step(c, di):
                a = di - 1.0 / c
                return (a, a)
            _, rest = jax.lax.scan(step, dT[0], dT[1:])
            return jnp.swapaxes(jnp.concatenate([dT[:1], rest], 0), 0, 1)

        def bk_core_diag(V, gamma):
            d = jax.lax.complex(V + 2.0, -gamma)
            a = _cf_scan(d)
            b = _cf_scan(d[:, ::-1])[:, ::-1]
            G = 1.0 / (a + b - d)
            return jnp.stack([G.real, G.imag], axis=-1)

        def hebbian_scan(q, k, v, gamma):
            qT = jnp.transpose(q, (1, 0, 2, 3))
            kT = jnp.transpose(k, (1, 0, 2, 3))
            vT = jnp.transpose(v, (1, 0, 2, 3))
            gT = jnp.swapaxes(gamma, 0, 1)
            W0 = jnp.zeros((q.shape[0], H, HD, HD), dtype=q.dtype)

            def step(W, inp):
                q_t, k_t, v_t, g_t = inp
                decay = jnp.exp(-g_t * DT)[:, None, None, None]
                W = decay * W + ETA * (k_t[..., :, None] * v_t[..., None, :])
                o = jnp.einsum('bhd,bhde->bhe', q_t, W)
                return (W, o)
            _, outs = jax.lax.scan(step, W0, (qT, kT, vT, gT))
            return jnp.transpose(outs, (1, 0, 2, 3)).reshape(q.shape[0], q.shape[1], H * HD)
        key = jax.random.key(seed)
        ks = jax.random.split(key, 12)
        s = lambda fan: 1.0 / np.sqrt(fan)
        return {'x': jax.random.normal(ks[0], (B, N, D), jnp.float32), 'ln1_g': jnp.ones((D,), jnp.float32), 'ln1_b': jnp.zeros((D,), jnp.float32), 'ln2_g': jnp.ones((D,), jnp.float32), 'ln2_b': jnp.zeros((D,), jnp.float32), 'ln3_g': jnp.ones((D,), jnp.float32), 'ln3_b': jnp.zeros((D,), jnp.float32), 'w_pot': jax.random.normal(ks[1], (D, 2), jnp.float32) * s(D), 'b_pot': jnp.zeros((2,), jnp.float32), 'w_bk': jax.random.normal(ks[2], (2, D), jnp.float32) * s(2), 'b_bk': jnp.zeros((D,), jnp.float32), 'w_qkv': jax.random.normal(ks[3], (D, 3 * H * HD), jnp.float32) * s(D), 'b_qkv': jnp.zeros((3 * H * HD,), jnp.float32), 'w_out': jax.random.normal(ks[4], (H * HD, D), jnp.float32) * s(H * HD), 'b_out': jnp.zeros((D,), jnp.float32), 'w_ff1': jax.random.normal(ks[5], (D, FF), jnp.float32) * s(D), 'b_ff1': jnp.zeros((FF,), jnp.float32), 'w_ff2': jax.random.normal(ks[6], (FF, D), jnp.float32) * s(FF), 'b_ff2': jnp.zeros((D,), jnp.float32)}
    _L1_attn_in = _L1_attn_setup()

    def _L1_ffn_setup():
        import jax, jax.numpy as jnp
        import numpy as np
        B, L, D = (2, 256, 256)
        HID, E, K = (512, 8, 2)
        key = jax.random.key(seed)
        ks = jax.random.split(key, 4)
        std = 0.02
        return {'x': jax.random.normal(ks[0], (B, L, D), dtype=jnp.float32), 'router_scale': jnp.ones((D,), dtype=jnp.float32), 'router_w': jax.random.normal(ks[1], (D, E), dtype=jnp.float32) * std, 'gating_w': jax.random.normal(ks[2], (E, 2, HID, D), dtype=jnp.float32) * std, 'linear_w': jax.random.normal(ks[3], (E, HID, D), dtype=jnp.float32) * std, 'per_expert_scale': jnp.ones((E,), dtype=jnp.float32)}
    _L1_ffn_in = _L1_ffn_setup()
    _d = {'L0_attn_x': _L0_attn_in['x'], 'L0_attn_Wq': _L0_attn_in['Wq'], 'L0_attn_Wk': _L0_attn_in['Wk'], 'L0_attn_Wv': _L0_attn_in['Wv'], 'L0_attn_Wo': _L0_attn_in['Wo'], 'L0_attn_splat_positions': _L0_attn_in['splat_positions'], 'L0_attn_splat_scales': _L0_attn_in['splat_scales'], 'L0_attn_splat_importance': _L0_attn_in['splat_importance'], 'L0_attn_We': _L0_attn_in['We'], 'L0_attn_be': _L0_attn_in['be'], 'L0_attn_Wt': _L0_attn_in['Wt'], 'L0_attn_bt': _L0_attn_in['bt'], 'L0_attn_Wd': _L0_attn_in['Wd'], 'L0_attn_bd': _L0_attn_in['bd'], 'L0_attn_Wg': _L0_attn_in['Wg'], 'L0_attn_bg': _L0_attn_in['bg'], 'L0_ffn_Wr': _L0_ffn_in['Wr'], 'L0_ffn_W1': _L0_ffn_in['W1'], 'L0_ffn_W2': _L0_ffn_in['W2'], 'L1_attn_ln1_g': _L1_attn_in['ln1_g'], 'L1_attn_ln1_b': _L1_attn_in['ln1_b'], 'L1_attn_ln2_g': _L1_attn_in['ln2_g'], 'L1_attn_ln2_b': _L1_attn_in['ln2_b'], 'L1_attn_ln3_g': _L1_attn_in['ln3_g'], 'L1_attn_ln3_b': _L1_attn_in['ln3_b'], 'L1_attn_w_pot': _L1_attn_in['w_pot'], 'L1_attn_b_pot': _L1_attn_in['b_pot'], 'L1_attn_w_bk': _L1_attn_in['w_bk'], 'L1_attn_b_bk': _L1_attn_in['b_bk'], 'L1_attn_w_qkv': _L1_attn_in['w_qkv'], 'L1_attn_b_qkv': _L1_attn_in['b_qkv'], 'L1_attn_w_out': _L1_attn_in['w_out'], 'L1_attn_b_out': _L1_attn_in['b_out'], 'L1_attn_w_ff1': _L1_attn_in['w_ff1'], 'L1_attn_b_ff1': _L1_attn_in['b_ff1'], 'L1_attn_w_ff2': _L1_attn_in['w_ff2'], 'L1_attn_b_ff2': _L1_attn_in['b_ff2'], 'L1_ffn_router_scale': _L1_ffn_in['router_scale'], 'L1_ffn_router_w': _L1_ffn_in['router_w'], 'L1_ffn_gating_w': _L1_ffn_in['gating_w'], 'L1_ffn_linear_w': _L1_ffn_in['linear_w'], 'L1_ffn_per_expert_scale': _L1_ffn_in['per_expert_scale']}
    _x0 = _d['L0_attn_x']
    _d['L0_attn_x'] = jax.random.normal(jax.random.fold_in(jax.random.key(seed), 1), (8, 512, 256), dtype=_x0.dtype)
    del _x0
    return _d

def reference(L0_attn_x, L0_attn_Wq, L0_attn_Wk, L0_attn_Wv, L0_attn_Wo, L0_attn_splat_positions, L0_attn_splat_scales, L0_attn_splat_importance, L0_attn_We, L0_attn_be, L0_attn_Wt, L0_attn_bt, L0_attn_Wd, L0_attn_bd, L0_attn_Wg, L0_attn_bg, L0_ffn_Wr, L0_ffn_W1, L0_ffn_W2, L1_attn_ln1_g, L1_attn_ln1_b, L1_attn_ln2_g, L1_attn_ln2_b, L1_attn_ln3_g, L1_attn_ln3_b, L1_attn_w_pot, L1_attn_b_pot, L1_attn_w_bk, L1_attn_b_bk, L1_attn_w_qkv, L1_attn_b_qkv, L1_attn_w_out, L1_attn_b_out, L1_attn_w_ff1, L1_attn_b_ff1, L1_attn_w_ff2, L1_attn_b_ff2, L1_ffn_router_scale, L1_ffn_router_w, L1_ffn_gating_w, L1_ffn_linear_w, L1_ffn_per_expert_scale):

    def _L0_attn_ref(x, Wq, Wk, Wv, Wo, splat_positions, splat_scales, splat_importance, We, be, Wt, bt, Wd, bd, Wg, bg):
        import jax, jax.numpy as jnp
        import numpy as np
        H = 16
        SPLAT_RATIO = 0.4
        STD_RATIO = 1.0 - SPLAT_RATIO
        B, N, D = x.shape
        Dh = D // H
        q = (x @ Wq).reshape(B, N, H, Dh)
        k = (x @ Wk).reshape(B, N, H, Dh)
        v = (x @ Wv).reshape(B, N, H, Dh)
        scores = jnp.einsum('bqhd,bkhd->bhqk', q, k) * Dh ** (-0.5)
        attn = jax.nn.softmax(scores, axis=-1)
        std_out = jnp.einsum('bhqk,bkhd->bqhd', attn, v).reshape(B, N, D)
        x2 = jnp.sum(x * x, axis=-1, keepdims=True)
        s2 = jnp.sum(splat_positions * splat_positions, axis=-1)
        d2 = jnp.maximum(x2 + s2[None, None, :] - 2.0 * jnp.einsum('bnd,sd->bns', x, splat_positions), 0.0)
        scales = jnp.maximum(jnp.abs(splat_scales), 1e-06)
        infl = jnp.exp(-0.5 * d2 / (scales * scales)) * jnp.abs(splat_importance)
        total = jnp.maximum(jnp.sum(infl, axis=1), 1e-08)
        gathered = jnp.einsum('bns,bnd->bsd', infl, x) / total[..., None]
        enc = jax.nn.relu(gathered @ We + be)
        trans = jnp.einsum('bsd,sde->bse', enc, Wt) + bt
        dec = trans @ Wd + bd
        flow = jnp.einsum('bns,bsd->bnd', infl, dec)
        flow = flow * jax.nn.sigmoid(x @ Wg + bg)
        out = (STD_RATIO * std_out + SPLAT_RATIO * flow) @ Wo
        return out

    def _L0_ffn_ref(x, Wr, W1, W2):
        import math
        import jax, jax.numpy as jnp
        import numpy as np
        B, S, D, F, E = (8, 512, 256, 1024, 8)
        CAPACITY_FACTOR = 1.0
        b, s, d = x.shape
        t = b * s
        cap = max(math.ceil(t * CAPACITY_FACTOR / E), 1)
        xf = x.reshape(t, d)
        probs = jax.nn.softmax(xf.astype(jnp.float32) @ Wr, axis=-1)
        eidx = jnp.argmax(probs, axis=-1)
        p_tok = jnp.take_along_axis(probs, eidx[:, None], axis=1)[:, 0]
        onehot = jax.nn.one_hot(eidx, E, dtype=jnp.int32)
        rank_all = jnp.cumsum(onehot, axis=0) - onehot
        rank = jnp.take_along_axis(rank_all, eidx[:, None], axis=1)[:, 0]
        keep = rank < cap
        slot = jnp.where(keep, rank, cap)
        dispatch = jnp.zeros((E, cap + 1), dtype=jnp.int32).at[eidx, slot].set(jnp.arange(t, dtype=jnp.int32))
        valid = jnp.zeros((E, cap + 1), dtype=bool).at[eidx, slot].set(keep)
        dispatch = dispatch[:, :cap]
        valid = valid[:, :cap]
        xe = xf[dispatch]
        h = jnp.maximum(jnp.einsum('ecd,edf->ecf', xe, W1), 0.0)
        ye = jnp.einsum('ecf,efd->ecd', h, W2)
        pe = p_tok[dispatch]
        ye = ye * (pe * valid.astype(ye.dtype))[:, :, None]
        y = jnp.zeros((t, d), dtype=x.dtype).at[dispatch.reshape(-1)].add(ye.reshape(E * cap, d).astype(x.dtype))
        return y.reshape(b, s, d)

    def _L1_attn_ref(x, ln1_g, ln1_b, ln2_g, ln2_b, ln3_g, ln3_b, w_pot, b_pot, w_bk, b_bk, w_qkv, b_qkv, w_out, b_out, w_ff1, b_ff1, w_ff2, b_ff2):
        import jax, jax.numpy as jnp
        import numpy as np
        B, N, D = (4, 512, 256)
        H, HD = (8, 64)
        FF = 1024
        ETA = 0.1
        DT = 0.01
        GAMMA_FLOOR = 0.1
        EPS = 1e-05

        def layernorm(x, g, b):
            m = jnp.mean(x, -1, keepdims=True)
            v = jnp.var(x, -1, keepdims=True)
            return (x - m) * jax.lax.rsqrt(v + EPS) * g + b

        def _cf_scan(d):
            dT = jnp.swapaxes(d, 0, 1)

            def step(c, di):
                a = di - 1.0 / c
                return (a, a)
            _, rest = jax.lax.scan(step, dT[0], dT[1:])
            return jnp.swapaxes(jnp.concatenate([dT[:1], rest], 0), 0, 1)

        def bk_core_diag(V, gamma):
            d = jax.lax.complex(V + 2.0, -gamma)
            a = _cf_scan(d)
            b = _cf_scan(d[:, ::-1])[:, ::-1]
            G = 1.0 / (a + b - d)
            return jnp.stack([G.real, G.imag], axis=-1)

        def hebbian_scan(q, k, v, gamma):
            qT = jnp.transpose(q, (1, 0, 2, 3))
            kT = jnp.transpose(k, (1, 0, 2, 3))
            vT = jnp.transpose(v, (1, 0, 2, 3))
            gT = jnp.swapaxes(gamma, 0, 1)
            W0 = jnp.zeros((q.shape[0], H, HD, HD), dtype=q.dtype)

            def step(W, inp):
                q_t, k_t, v_t, g_t = inp
                decay = jnp.exp(-g_t * DT)[:, None, None, None]
                W = decay * W + ETA * (k_t[..., :, None] * v_t[..., None, :])
                o = jnp.einsum('bhd,bhde->bhe', q_t, W)
                return (W, o)
            _, outs = jax.lax.scan(step, W0, (qT, kT, vT, gT))
            return jnp.transpose(outs, (1, 0, 2, 3)).reshape(q.shape[0], q.shape[1], H * HD)
        b, n, d = x.shape
        xn1 = layernorm(x, ln1_g, ln1_b)
        pot = xn1 @ w_pot + b_pot
        V = pot[..., 0]
        gamma = jax.nn.softplus(pot[..., 1]) + GAMMA_FLOOR
        bk_features = bk_core_diag(V, gamma)
        x = x + bk_features @ w_bk + b_bk
        xn2 = layernorm(x, ln2_g, ln2_b)
        qkv = (xn2 @ w_qkv + b_qkv).reshape(b, n, 3, H, HD)
        q, k, v = (qkv[:, :, 0], qkv[:, :, 1], qkv[:, :, 2])
        heb = hebbian_scan(q, k, v, gamma)
        x = x + heb @ w_out + b_out
        xn3 = layernorm(x, ln3_g, ln3_b)
        x = x + jax.nn.gelu(xn3 @ w_ff1 + b_ff1) @ w_ff2 + b_ff2
        return x

    def _L1_ffn_ref(x, router_scale, router_w, gating_w, linear_w, per_expert_scale):
        import jax, jax.numpy as jnp
        import numpy as np
        B, L, D = (2, 256, 256)
        HID, E, K = (512, 8, 2)
        d = x.shape[-1]
        var = jnp.mean(jnp.square(x), axis=-1, keepdims=True)
        r_in = x * jax.lax.rsqrt(var + 1e-06)
        r_in = r_in * jax.lax.rsqrt(jnp.array(d, dtype=r_in.dtype)) * router_scale
        logits = jnp.dot(r_in, router_w).astype(jnp.float32)
        probs = jax.nn.softmax(logits, axis=-1)
        _, top_k_idx = jax.lax.top_k(logits, K)
        indicator = jax.nn.one_hot(top_k_idx, probs.shape[-1], dtype=probs.dtype)
        gate_weights = indicator.sum(axis=-2) * probs
        renorm = jnp.sum(gate_weights, axis=-1, keepdims=True)
        renorm = jnp.where(renorm > 0.0, renorm, 1.0)
        weights = probs / renorm
        top_k_w = jnp.take_along_axis(weights, top_k_idx, axis=-1)
        combine = jnp.einsum('blke,blk->ble', indicator, top_k_w)
        combine = combine * per_expert_scale
        gate0 = jnp.einsum('bld,ehd->bleh', x, gating_w[:, 0])
        gate1 = jnp.einsum('bld,ehd->bleh', x, gating_w[:, 1])
        act = jax.nn.gelu(gate0) * gate1
        out = jnp.einsum('bleh,ehd,ble->bld', act, linear_w, combine)
        return out.astype(x.dtype)
    x = L0_attn_x
    xn = _layernorm(x, axis=-1)
    x = x + _L0_attn_ref(xn, L0_attn_Wq, L0_attn_Wk, L0_attn_Wv, L0_attn_Wo, L0_attn_splat_positions, L0_attn_splat_scales, L0_attn_splat_importance, L0_attn_We, L0_attn_be, L0_attn_Wt, L0_attn_bt, L0_attn_Wd, L0_attn_bd, L0_attn_Wg, L0_attn_bg) + _L0_ffn_ref(xn, L0_ffn_Wr, L0_ffn_W1, L0_ffn_W2)
    xn = _layernorm(x, axis=-1)
    x = x + _L1_attn_ref(xn, L1_attn_ln1_g, L1_attn_ln1_b, L1_attn_ln2_g, L1_attn_ln2_b, L1_attn_ln3_g, L1_attn_ln3_b, L1_attn_w_pot, L1_attn_b_pot, L1_attn_w_bk, L1_attn_b_bk, L1_attn_w_qkv, L1_attn_b_qkv, L1_attn_w_out, L1_attn_b_out, L1_attn_w_ff1, L1_attn_b_ff1, L1_attn_w_ff2, L1_attn_b_ff2) + _L1_ffn_ref(xn, L1_ffn_router_scale, L1_ffn_router_w, L1_ffn_gating_w, L1_ffn_linear_w, L1_ffn_per_expert_scale)
    return x

_drawn_inputs = setup_inputs


def setup_inputs(seed=0):
    import zlib

    import numpy as np

    out = dict(_drawn_inputs(seed))
    spreads = {'L0_attn_splat_scales': (1.0, 0.2),
     'L0_attn_splat_importance': (1.0, 0.2),
     'L0_attn_be': (0.0, 0.1),
     'L0_attn_bt': (0.0, 0.1),
     'L0_attn_bd': (0.0, 0.1),
     'L0_attn_bg': (0.0, 0.1),
     'L1_attn_ln1_g': (1.0, 0.2),
     'L1_attn_ln1_b': (0.0, 0.1),
     'L1_attn_ln2_g': (1.0, 0.2),
     'L1_attn_ln2_b': (0.0, 0.1),
     'L1_attn_ln3_g': (1.0, 0.6),
     'L1_attn_ln3_b': (0.0, 2.0),
     'L1_attn_b_pot': (0.0, 0.28),
     'L1_attn_b_bk': (0.0, 0.1),
     'L1_attn_b_qkv': (0.0, 0.1),
     'L1_attn_b_out': (0.0, 0.8),
     'L1_attn_b_ff1': (0.0, 2.0),
     'L1_attn_b_ff2': (0.0, 0.8),
     'L1_ffn_router_scale': (1.0, 0.6),
     'L1_ffn_per_expert_scale': (1.0, 0.6)}
    factors = {'L0_attn_Wq': 8.0,
     'L0_attn_Wk': 8.0,
     'L0_attn_Wv': 7.328,
     'L0_attn_Wo': 7.114,
     'L1_ffn_router_w': 8.0,
     'L1_ffn_gating_w': 8.0,
     'L1_ffn_linear_w': 8.0}
    for name, (base, spread) in spreads.items():
        noise = np.random.default_rng([zlib.crc32(name.encode()), seed]).standard_normal(out[name].shape)
        drawn = base * np.exp(spread * noise) if base else spread * noise
        out[name] = jnp.asarray(drawn.astype(out[name].dtype))
    for name, factor in factors.items():
        out[name] = (out[name] * factor).astype(out[name].dtype)
    return out
```

```python
from contextlib import ExitStack

import concourse.bass as bass
from concourse import mybir

F32 = mybir.dt.float32
BF16 = mybir.dt.bfloat16
I32 = mybir.dt.int32
ALU = mybir.AluOpType
ACT = mybir.ActivationFunctionType
AX = mybir.AxisListType
ds = bass.ds

P = 128
ZROW = 2304


class Steps:

    def __init__(self, eng, sem, settled=None):
        self.eng, self.sem, self.total, self.i, self.per, self.k = eng, sem, 0, None, 0, 0
        self.settled = settled

    def enter(self, i, per):
        self.i, self.per, self.k = i, per, 0

    def leave(self, trips):
        assert self.k == self.per, f"steps in the loop: {self.k}, said {self.per}"
        self.total += trips * self.per
        self.i = None

    def link(self, instruction, apart=False):
        instruction.then_inc(self.sem, 1)
        if self.i is None:
            self.total += 1
            self.eng.wait_ge(self.sem, self.total)
        else:
            self.k += 1
            value = self.i * self.per + (self.total + self.k)
            if apart:
                wait_apart(self.eng, self.sem, value, self.settled)
            else:
                self.eng.wait_ge(self.sem, value)


def wait_apart(eng, sem, value, settled):
    if not isinstance(value, int):
        eng.lower_val(value)
        eng.wait_ge(*settled)
    eng.wait_ge(sem, value)


def last_dim(ap, n):
    return ap.unsqueeze(2).to_broadcast([ap.shape[0], ap.shape[1], n])


def mid_dim(ap, n):
    return ap.unsqueeze(1).to_broadcast([ap.shape[0], n, ap.shape[1]])


def row_of(vector, n):
    return vector.unsqueeze(0).to_broadcast([n, vector.shape[0]])


def column(vector):
    return vector.rearrange("(s a) -> s a", a=1)


def loop(eng, trips, body, steps=None, per=0):
    with eng.Fori(0, trips - 1) as i:
        if steps:
            steps.enter(i, per)
        body(i, False)
    if steps:
        steps.leave(trips - 1)
    body(trips - 1, True)


def clear(nc, semaphores):
    with nc.Block() as block:
        @block.sync
        def _(sp):
            for s in semaphores:
                sp.sem_clear(s)


def build_program(nc, T, out):
    ctx = ExitStack()
    with ctx:
        B, N, D = T["x"].shape
        NT = B * N // P
        G = {"nc": nc}

        def sb(name, shape, dt=F32, into=ctx):
            G[name] = into.enter_context(nc.sbuf_tensor(name, shape, dt))

        def sem(name):
            G[name] = ctx.enter_context(nc.semaphore(name))

        sb("x_all", [P, NT, D])
        sb("ident", [P, P])
        sb("ones", [P, P])
        sb("mhalf", [P, NT])
        sb("strict", [P, P])
        sb("slot0", [P, NT], I32)
        sb("take0", [P, NT], I32)
        sb("pkeep0", [P, NT])
        sem("dram_zeroed")
        sem("scattered0")
        phase_norm_route0(nc, T, G)
        phase_attention0_experts0(nc, T, G)
        E1, HID = T["lin"].shape[0], T["lin"].shape[1]
        sb("y_all", [P, NT, D])
        sb("dcol", [P, 2, NT])
        sb("ccol", [P, NT])
        sb("slot1", [P, 2, NT], I32)
        sb("weight1", [P, 2, NT])
        sb("tile_expert", [1, T["xs"].shape[0] // P], I32)
        sb("anti", [P, P])
        sb("decay_mask", [P, N])
        sem("moe_w_in")
        HW, F1 = T["w_out"].shape[0], T["w_ff1"].shape[1]
        sb("Wqkv", [P, D // P, 3 * HW])
        sb("cols", [P, D // P, 4])
        sb("bqk", [P, 2 * HW // P])
        sb("bf1", [P, F1 // P])
        sb("bv", [P, HW])
        sb("wbk", [P, 2, D])
        sb("bout", [P, D])
        sb("bf2", [P, D])
        with ExitStack() as weights:
            sb("gate", [P, D // P, E1, 2 * HID], into=weights)
            sb("lin", [P, E1, HID // P, D], into=weights)
            phase_middle(nc, T, G)
            phase_experts1_scan(nc, T, G)
        phase_attention1(nc, T, G, out)


def phase_norm_route0(nc, T, G):
    B, N, D = T["x"].shape
    S = T["splat"].shape[0]
    E = T["Wr"].shape[1]
    C, J = D // P, N // P
    NT = B * J
    CAP = B * N // E
    x_all, ident, ones, strict = G["x_all"], G["ident"], G["ones"], G["strict"]
    slot0, take0, pkeep0 = G["slot0"], G["take0"], G["pkeep0"]
    mhalf = G["mhalf"]
    dram_zeroed, scattered0 = G["dram_zeroed"], G["scattered0"]
    with ExitStack() as ctx:
        used = []

        def sb(name, shape, dt=F32):
            return ctx.enter_context(nc.sbuf_tensor(name, shape, dt))

        def psum(name, shape):
            return ctx.enter_context(nc.psum_tensor(name, shape, F32))

        def sem(name):
            used.append(ctx.enter_context(nc.semaphore(name)))
            return used[-1]

        Wr = sb("Wr", [P, C, E])
        We = sb("We", [P, C, P])
        Wd = sb("Wd", [P, D])
        Wt = sb("Wt", [P, S, P])
        splat = sb("splat", [S, D])
        splT = sb("splT", [P, C, S])
        svec = sb("svec", [S, 8])
        be = sb("be", [P, 1])
        btT = sb("btT", [P, S])
        bdb = sb("bdb", [S, D])
        zeros = sb("zeros", [P, ZROW])
        xn = sb("xn", [P, J, D])
        xn_all = sb("xn_all", [P, NT, D])
        stats = sb("stats", [P, J, 6])
        mv = sb("mv", [P, J, 2])
        rstd = sb("rstd", [P, J])
        xnTc = sb("xnTc", [P, C, N])
        sqT = sb("sqT", [P, C, N])
        lg = sb("lg", [P, NT, E])
        d2 = sb("d2", [S, N])
        ex = sb("ex", [S, N])
        infl = sb("infl", [S, N])
        dec = sb("dec", [S, B, D])
        tot = sb("tot", [S, 3])
        gathered = sb("gathered0", [S, B, D])
        inN = sb("inN", [P, J, S])
        gT = sb("gT", [P, C, B, S])
        encT = sb("encT", [P, S, B])
        trT = sb("trT", [P, S, B])
        ra = sb("ra", [P, NT, E])
        rb = sb("rb", [P, NT, E])
        oh = sb("oh", [P, NT, E])
        r1 = sb("r1", [P, NT])
        r2 = sb("r2", [P, NT])
        ptok = sb("ptok", [P, NT])
        wgt = sb("wgt", [P, E])
        eno = sb("eno", [P, E])
        tp = psum("tp", [P, C, N])
        lgp = psum("lgp", [P, 512])
        d2p = psum("d2p", [P, N])
        inp = psum("inp", [P, 512])
        gap = psum("gap", [P, 512])
        enp = psum("enp", [P, 512])
        dcp = psum("dcp", [P, 512])
        lgv = lgp[:, 0:J * E].rearrange("p (j e) -> p j e", e=E)
        inv = inp[:, 0:J * S].rearrange("p (j s) -> p j s", s=S)
        gav = gap[0:S, 0:D]

        x_loaded, w_loaded, wt_loaded = sem("x_loaded"), sem("w_loaded"), sem("wt_loaded")
        consts, z_ready = sem("consts"), sem("z_ready")
        var_ready, rstd_ready = sem("var_ready"), sem("rstd_ready")
        xn_ready, xn_copied = sem("xn_ready"), sem("xn_copied")
        tp_ready, xnTc_ready, sq_ready, xnT_out = sem("tp_ready"), sem("xnTc_ready"), sem("sq_ready"), sem("xnT_out")
        infl_out, dec_out = sem("infl_out"), sem("dec_out")
        lg_done, lg_copied = sem("lg_done"), sem("lg_copied")
        d2_done, d2_ready, ex_ready = sem("d2_done"), sem("d2_ready"), sem("ex_ready")
        infl_ready, in_turned, inN_ready = sem("infl_ready"), sem("in_turned"), sem("inN_ready")
        gath_done, gath_taken, g_turned, gT_ready, enc_done, enc_ready = sem("gath_done"), sem("gath_taken"), sem("g_turned"), sem("gT_ready"), sem("enc_done"), sem("enc_ready")
        tr_done, tr_ready, dec_done, dec_copied = sem("tr_done"), sem("tr_ready"), sem("dec_done"), sem("dec_copied")
        r_sub, r_exp, oh_ready, rank_done, slots_ready = sem("r_sub"), sem("r_exp"), sem("oh_ready"), sem("rank_done"), sem("slots_ready")
        spl_turned, spl_ready = sem("spl_turned"), sem("spl_ready")
        v_step, p_step = sem("v_step"), sem("p_step")
        NW = 9

        with nc.Block() as block:
            @block.sync
            def _(sp):
                with sp.Fori(0, B) as b:
                    sp.dma_start(x_all[:, ds(b * J, J), :],
                                 T["x"].rearrange("b (j p) d -> p (b j) d", p=P)[:, ds(b * J, J), :]).then_inc(x_loaded, 16)
                sp.dma_start(splat[:, :], T["splat"]).then_inc(w_loaded, 16)
                sp.dma_start(svec[:, 0:1], column(T["sscale"])).then_inc(w_loaded, 16)
                sp.dma_start(svec[:, 1:2], column(T["simp"])).then_inc(w_loaded, 16)
                sp.dma_start(Wr[:, :, :], T["Wr"].rearrange("(c p) e -> p c e", p=P)).then_inc(w_loaded, 16)
                sp.dma_start(We[:, :, :], T["We"].rearrange("(c p) e -> p c e", p=P)).then_inc(w_loaded, 16)
                sp.dma_start(Wd[:, :], T["Wd"]).then_inc(w_loaded, 16)
                sp.dma_start(be[:, :], column(T["be"])).then_inc(w_loaded, 16)
                sp.dma_start(btT[:, :], T["btT"]).then_inc(w_loaded, 16)
                sp.dma_start(bdb[:, :], row_of(T["bd"], S)).then_inc(w_loaded, 16)
                sp.sem_inc(xnT_out, 16)
                sp.sem_inc(infl_out, 16)
                sp.wait_ge(z_ready, 1)
                with sp.Fori(0, B) as b:
                    sp.wait_ge(xnTc_ready, b + 2)
                    sp.dma_start(T["xnT"][ds(b, 1), :, :, :].squeeze(0), xnTc[:, :, :]).then_inc(xnT_out, 16)
                    sp.wait_ge(infl_ready, b + 1)
                    sp.dma_start(T["inflT"][ds(b, 1), :, :].squeeze(0), infl[:, :]).then_inc(infl_out, 16)
                    sp.dma_start(Wt[:, ds(b * (S // B), S // B), :],
                                 T["Wt"].rearrange("s d e -> d s e")[:, ds(b * (S // B), S // B), :]).then_inc(wt_loaded, 16)
                    for name in ("xe", "xs"):
                        rows = T[name].shape[0] // B
                        sp.dma_start(T[name][ds(b * rows, rows), :].rearrange("(p r) d -> p (r d)", p=P),
                                     zeros[:, 0:rows // P * D]).then_inc(dram_zeroed, 16)
                sp.wait_ge(dec_copied, B)
                sp.dma_start(T["dec"].rearrange("b s d -> s b d"), dec[:, :, :]).then_inc(dec_out, 16)
                sp.wait_ge(xnT_out, 16 * (B + 1))
                sp.wait_ge(infl_out, 16 * (B + 1))
                sp.wait_ge(dec_out, 16)

            @block.gpsimd
            def _(pool):
                st = Steps(pool, p_step)
                st.link(nc.gpsimd.memset(ident[:, :], 0.0))
                st.link(nc.gpsimd.memset(strict[:, :], 0.0))
                st.link(nc.gpsimd.memset(mhalf[:, :], -0.5))
                nc.gpsimd.affine_select(out=ident[:, :], in_=ident[:, :], compare_op=ALU.not_equal, fill=1.0,
                                        base=0, pattern=[[-1, P]], channel_multiplier=1).then_inc(consts, 1)
                nc.gpsimd.affine_select(out=strict[:, :], in_=strict[:, :], compare_op=ALU.is_ge, fill=1.0,
                                        base=0, pattern=[[-1, P]], channel_multiplier=1).then_inc(consts, 1)
                nc.gpsimd.iota(wgt[:, :], pattern=[[-1, E]], base=E, channel_multiplier=0,
                               allow_small_or_imprecise_dtypes=True).then_inc(consts, 1)
                nc.gpsimd.iota(eno[:, :], pattern=[[1, E]], base=0, channel_multiplier=0,
                               allow_small_or_imprecise_dtypes=True).then_inc(consts, 1)
                nc.gpsimd.memset(zeros[:, :], 0.0).then_inc(z_ready, 1)
                with pool.Fori(0, B) as b:
                    pool.wait_ge(var_ready, b + 1)
                    nc.gpsimd.tensor_tensor(rstd[:, :], rstd[:, :], mhalf[:, 0:J], ALU.pow).then_inc(rstd_ready, 1)
                pool.wait_ge(xn_copied, B + 1)
                pool.wait_ge(slots_ready, 1)
                pool.wait_ge(dram_zeroed, 16 * 2 * B)
                for t in range(NT):
                    nc.gpsimd.indirect_dma_start(
                        out=T["xe"], out_offset=bass.IndirectOffsetOnAxis(ap=slot0[:, t:t + 1], axis=0),
                        in_=xn_all[:, t, :], in_offset=None, bounds_check=B * N - 1, oob_is_err=False,
                    ).then_inc(scattered0, 16)
                pool.wait_ge(scattered0, 16 * NT)

            @block.scalar
            def _(act):
                act.wait_ge(spl_turned, 1)
                nc.scalar.activation(splT[:, :, :], tp[:, :, 0:S], ACT.Copy, scale=-2.0).then_inc(spl_ready, 1)
                act.sem_inc(xnTc_ready, 1)
                act.sem_inc(xn_copied, 1)

                def ahead(b):
                    act.wait_ge(tp_ready, b + 2)
                    act.wait_ge(d2_done, b + 1)
                    act.wait_ge(xnT_out, b * 16 + 16)
                    nc.scalar.activation(xnTc[:, :, :], tp[:, :, :], ACT.Copy).then_inc(xnTc_ready, 1)

                def kept(b):
                    nc.scalar.activation(sqT[:, :, :], tp[:, :, :], ACT.Square).then_inc(sq_ready, 1)
                    nc.scalar.activation(xn_all[:, ds(b * J, J), :], xn[:, :, :], ACT.Copy).then_inc(xn_copied, 1)

                def body(b, last):
                    if not last:
                        ahead(b + 1)
                    act.wait_ge(d2_ready, b + 1)
                    nc.scalar.activation(ex[:, :], d2[:, :], ACT.Exp, scale=svec[:, 4:5]).then_inc(ex_ready, 1)
                    if not last:
                        kept(b + 1)
                    act.wait_ge(in_turned, b + 2)
                    nc.scalar.activation(inN[:, :, :], inv, ACT.Copy).then_inc(inN_ready, 1)
                ahead(0)
                kept(0)
                loop(act, B, body)
                act.wait_ge(g_turned, 1)
                nc.scalar.activation(gT[:, :, :, :].rearrange("p c b s -> p c (b s)"), tp[:, :, :], ACT.Copy).then_inc(gT_ready, 1)
                act.wait_ge(r_sub, 1)
                nc.scalar.activation(rb[:, :, :], ra[:, :, :], ACT.Exp).then_inc(r_exp, 1)

            @block.tensor
            def _(pe):
                pe.wait_ge(consts, 4)
                pe.wait_ge(w_loaded, 16 * NW)
                for c in range(C):
                    last = nc.tensor.transpose(tp[:, c, 0:S], splat[:, c * P:(c + 1) * P], ident[0:S, 0:S])
                last.then_inc(spl_turned, 1)
                pe.wait_ge(spl_ready, 1)
                pe.sem_inc(d2_done, 1)
                pe.sem_inc(tp_ready, 1)
                pe.sem_inc(in_turned, 1)

                def turn(b):
                    pe.wait_ge(xn_ready, b + 1)
                    if not (isinstance(b, int) and b == 0):
                        pe.wait_ge(sq_ready, b)
                    for j in range(J):
                        for c in range(C):
                            mm = nc.tensor.transpose(tp[:, c, j * P:(j + 1) * P], xn[:, j, c * P:(c + 1) * P], ident[:, :])
                    mm.then_inc(tp_ready, 1)

                def logits(b):
                    pe.wait_ge(xnTc_ready, b + 2)
                    pe.wait_ge(lg_copied, b + 1)
                    for j in range(J):
                        for c in range(C):
                            mm = nc.tensor.matmul(lgv[:, j, :], xnTc[:, c, j * P:(j + 1) * P], Wr[:, c, :],
                                                  start=(c == 0), stop=(c == C - 1))
                    mm.then_inc(lg_done, 1)

                def distances(b):
                    pe.wait_ge(sq_ready, b + 1)
                    if not (isinstance(b, int) and b == 0):
                        pe.wait_ge(d2_ready, b)
                    for c in range(C):
                        nc.tensor.matmul(d2p[0:S, :], ones[:, 0:S], sqT[:, c, :], start=(c == 0), stop=False)
                        mm = nc.tensor.matmul(d2p[0:S, :], splT[:, c, :], xnTc[:, c, :], start=False, stop=(c == C - 1))
                    mm.then_inc(d2_done, 1)

                turn(0)
                logits(0)
                distances(0)

                def body(b, last):
                    if not last:
                        turn(b + 1)
                        logits(b + 1)
                    wait_apart(pe, infl_ready, b + 1, (consts, 4))
                    for j in range(J):
                        mm = nc.tensor.transpose(inv[:, j, :], infl[:, j * P:(j + 1) * P], ident[0:S, 0:S])
                    mm.then_inc(in_turned, 1)
                    if not last:
                        distances(b + 1)
                    pe.wait_ge(inN_ready, b + 1)
                    pe.wait_ge(xn_copied, b + 2)
                    pe.wait_ge(gath_taken, b + 1)
                    for j in range(J):
                        mm = nc.tensor.matmul(gav, inN[:, j, :], xn_all[:, ds(b * J + j, 1), :].squeeze(1), start=(j == 0), stop=(j == J - 1))
                    mm.then_inc(gath_done, 1)
                loop(pe, B, body)
                pe.wait_ge(gath_taken, B + 1)
                for c in range(C):
                    for b in range(B):
                        mm = nc.tensor.transpose(tp[:, c, b * S:(b + 1) * S], gathered[:, b, c * P:(c + 1) * P], ident[0:S, 0:S])
                mm.then_inc(g_turned, 1)
                pe.wait_ge(gT_ready, 1)
                for c in range(C):
                    last = nc.tensor.matmul(enp[:, 0:B * S], We[:, c, :], gT[:, c, :, :].rearrange("p b s -> p (b s)"), start=(c == 0), stop=(c == C - 1))
                last.then_inc(enc_done, 1)
                pe.wait_ge(oh_ready, 1)
                ohf = oh[:, :, :].rearrange("p t e -> p (t e)")
                nc.tensor.matmul(tp[:, 0, 0:NT * E], strict[:, :], ohf, start=True, stop=True)
                nc.tensor.matmul(tp[:, 1, 0:NT * E], ones[:, :], ohf, start=True, stop=True).then_inc(rank_done, 1)
                pe.wait_ge(enc_ready, 1)
                pe.wait_ge(wt_loaded, 16 * B)
                for s in range(S):
                    last = nc.tensor.matmul(d2p[:, s * B:(s + 1) * B], Wt[:, s, :], encT[:, s, :], start=True, stop=True)
                last.then_inc(tr_done, 1)
                pe.wait_ge(tr_ready, 1)
                for b in range(B):
                    if b:
                        pe.wait_ge(dec_copied, b)
                    nc.tensor.matmul(dcp[0:S, 0:D], trT[:, :, b], Wd[:, :], start=True, stop=True).then_inc(dec_done, 1)

            @block.vector
            def _(ve):
                st = Steps(ve, v_step, (consts, 4))
                link = st.link
                V = nc.vector
                link(V.memset(ones[:, :], 1.0))
                ve.wait_ge(consts, 4)
                ve.wait_ge(w_loaded, 16 * NW)
                link(V.tensor_scalar(svec[:, 7:8], svec[:, 1:2], -1.0, None, ALU.mult))
                link(V.tensor_tensor(svec[:, 2:3], svec[:, 1:2], svec[:, 7:8], ALU.max))
                link(V.tensor_tensor(d2[:, 0:D], splat[:, :], splat[:, :], ALU.mult))
                link(V.tensor_reduce(svec[:, 3:4], d2[:, 0:D], AX.X, ALU.add))
                link(V.tensor_scalar(svec[:, 7:8], svec[:, 0:1], -1.0, 1e-6, ALU.mult, ALU.max))
                link(V.tensor_tensor(svec[:, 5:6], svec[:, 0:1], svec[:, 7:8], ALU.max))
                link(V.tensor_tensor(svec[:, 6:7], svec[:, 5:6], svec[:, 5:6], ALU.mult))
                link(V.reciprocal(svec[:, 7:8], svec[:, 6:7]))
                link(V.tensor_scalar(svec[:, 4:5], svec[:, 7:8], -0.5, None, ALU.mult))
                for s in (lg_copied, gath_taken):
                    ve.sem_inc(s, 1)

                def moments(b):
                    ve.wait_ge(x_loaded, b * 16 + 16)
                    for j in range(J):
                        la = V.bn_stats(stats[:, j, :], x_all[:, b * J + j, :])
                    link(la, apart=True)
                    for j in range(J):
                        la = V.bn_aggr(mv[:, j, :], stats[:, j, :])
                    link(la)
                    V.tensor_scalar(rstd[:, :], mv[:, :, 1], 1e-5, None, ALU.add).then_inc(var_ready, 1)

                def normed(b):
                    ve.wait_ge(rstd_ready, b + 1)
                    ve.wait_ge(xn_copied, b + 1)
                    for j in range(J):
                        la = V.tensor_scalar(xn[:, j, :], x_all[:, b * J + j, :], mv[:, j, 0:1], rstd[:, j:j + 1],
                                             ALU.subtract, ALU.mult)
                    la.then_inc(xn_ready, 1)

                def logits(b):
                    ve.wait_ge(lg_done, b + 1)
                    V.tensor_copy(lg[:, ds(b * J, J), :], lgv).then_inc(lg_copied, 1)

                moments(0)
                normed(0)
                logits(0)

                def body(b, last):
                    if not last:
                        moments(b + 1)
                        normed(b + 1)
                    ve.wait_ge(d2_done, b + 2)
                    V.tensor_scalar(d2[:, :], d2p[0:S, :], svec[:, 3:4], 0.0, ALU.add, ALU.max).then_inc(d2_ready, 1)
                    ve.wait_ge(ex_ready, b + 1)
                    ve.wait_ge(in_turned, b + 1)
                    ve.wait_ge(infl_out, b * 16 + 16)
                    V.tensor_scalar(infl[:, :], ex[:, :], svec[:, 2:3], None, ALU.mult).then_inc(infl_ready, 1)
                    ve.wait_ge(infl_ready, b + 1)
                    link(V.tensor_reduce(tot[:, 0:1], infl[:, :], AX.X, ALU.add))
                    link(V.tensor_scalar(tot[:, 1:2], tot[:, 0:1], 1e-8, None, ALU.max))
                    link(V.reciprocal(tot[:, 2:3], tot[:, 1:2]))
                    if not last:
                        logits(b + 1)
                    ve.wait_ge(gath_done, b + 1)
                    V.tensor_scalar(gathered[:, ds(b, 1), :].squeeze(1), gav, tot[:, 2:3], None, ALU.mult).then_inc(gath_taken, 1)
                loop(ve, B, body, st, 5)
                ve.wait_ge(lg_copied, B + 1)
                link(V.tensor_reduce(r1[:, :], lg[:, :, :], AX.X, ALU.max))
                V.tensor_tensor(ra[:, :, :], lg[:, :, :], last_dim(r1[:, :], E), ALU.subtract).then_inc(r_sub, 1)
                ve.wait_ge(r_exp, 1)
                link(V.tensor_reduce(r1[:, :], rb[:, :, :], AX.X, ALU.add))
                link(V.reciprocal(r2[:, :], r1[:, :]))
                link(V.tensor_tensor(ra[:, :, :], rb[:, :, :], last_dim(r2[:, :], E), ALU.mult))
                link(V.tensor_reduce(ptok[:, :], ra[:, :, :], AX.X, ALU.max))
                link(V.tensor_tensor(rb[:, :, :], ra[:, :, :], last_dim(ptok[:, :], E), ALU.is_equal))
                link(V.tensor_tensor(ra[:, :, :], rb[:, :, :], mid_dim(wgt[:, :], NT), ALU.mult))
                link(V.tensor_reduce(r1[:, :], ra[:, :, :], AX.X, ALU.max))
                V.tensor_tensor(oh[:, :, :], ra[:, :, :], last_dim(r1[:, :], E), ALU.is_equal).then_inc(oh_ready, 1)
                ve.wait_ge(oh_ready, 1)
                ve.wait_ge(rank_done, 1)
                before = tp[:, 0, 0:NT * E].rearrange("p (t e) -> p t e", e=E)
                count = tp[:, 1, 0:NT * E].rearrange("p (t e) -> p t e", e=E)
                link(V.tensor_copy(ra[:, :, :], count))
                a, z, k = ra, rb, 1
                while k < NT:
                    link(V.tensor_copy(z[:, 0:k, :], a[:, 0:k, :]))
                    link(V.tensor_tensor(z[:, k:NT, :], a[:, k:NT, :], a[:, 0:NT - k, :], ALU.add))
                    a, z, k = z, a, 2 * k
                link(V.tensor_tensor(z[:, :, :], a[:, :, :], count, ALU.subtract))
                link(V.tensor_tensor(a[:, :, :], z[:, :, :], before, ALU.add))
                link(V.tensor_tensor(z[:, :, :], a[:, :, :], oh[:, :, :], ALU.mult))
                link(V.tensor_reduce(r1[:, :], z[:, :, :], AX.X, ALU.add))
                link(V.tensor_tensor(z[:, :, :], oh[:, :, :], mid_dim(eno[:, :], NT), ALU.mult))
                link(V.tensor_reduce(r2[:, :], z[:, :, :], AX.X, ALU.add))
                link(V.tensor_scalar(ra[:, :, 0], r1[:, :], float(CAP), None, ALU.is_ge))
                link(V.scalar_tensor_tensor(out=ra[:, :, 1], in0=r2[:, :], scalar=float(CAP), in1=r1[:, :],
                                            op0=ALU.mult, op1=ALU.add))
                link(V.scalar_tensor_tensor(out=ra[:, :, 2], in0=ra[:, :, 0], scalar=2.0 * B * N, in1=ra[:, :, 1],
                                            op0=ALU.mult, op1=ALU.add))
                link(V.tensor_scalar(ra[:, :, 3], ra[:, :, 1], float(B * N - 1), None, ALU.min))
                link(V.tensor_copy(take0[:, :], ra[:, :, 3]))
                link(V.tensor_scalar(ra[:, :, 4], ra[:, :, 0], -1.0, 1.0, ALU.mult, ALU.add))
                link(V.tensor_tensor(pkeep0[:, :], ra[:, :, 4], ptok[:, :], ALU.mult))
                V.tensor_copy(slot0[:, :], ra[:, :, 2]).then_inc(slots_ready, 1)
                ve.wait_ge(enc_done, 1)
                V.tensor_scalar(encT[:, :, :].rearrange("p s b -> p b s"), enp[:, 0:B * S].rearrange("p (b s) -> p b s", s=S),
                                be[:, 0:1], 0.0, ALU.add, ALU.max).then_inc(enc_ready, 1)
                ve.wait_ge(tr_done, 1)
                V.tensor_tensor(trT[:, :, :], d2p[:, :].rearrange("p (s b) -> p s b", b=B), last_dim(btT[:, :], B),
                                ALU.add).then_inc(tr_ready, 1)
                for b in range(B):
                    ve.wait_ge(dec_done, b + 1)
                    V.tensor_tensor(dec[:, b, :], dcp[0:S, 0:D], bdb[:, :], ALU.add).then_inc(dec_copied, 1)
        clear(nc, used)


def phase_attention0_experts0(nc, T, G):
    B, N, D = T["x"].shape
    H = 16
    DH = D // H
    S = T["splat"].shape[0]
    C, J = D // P, N // P
    F = T["W1"].shape[2]
    FT = F // P
    CAP = B * N // T["W1"].shape[0]
    assert CAP == N
    QH = 4
    NG = H // QH
    R = 6 * DH
    PAIRS = ((0, 0), (0, 1), (0, 2), (1, 0), (1, 1), (2, 0))
    x_all, ident = G["x_all"], G["ident"]
    with ExitStack() as ctx:
        used = []

        def sb(name, shape, dt=F32):
            return ctx.enter_context(nc.sbuf_tensor(name, shape, dt))

        def sem(name):
            used.append(ctx.enter_context(nc.semaphore(name)))
            return used[-1]

        Wq, Wk, Wv, Wo, Wg = (sb(n, [P, C, D]) for n in ("Wq", "Wk", "Wv", "Wo", "Wg"))
        W1 = sb("W1", [P, C, F])
        W2 = sb("W2", [P, FT, D])
        nbg = sb("nbg", [P, C])
        xe = sb("xe", [P, J, D])
        xeT = sb("xeT", [P, C, N])
        hT = sb("hT", [P, FT, N])
        ysb = sb("ysb", [P, J, D])
        xnTb = sb("xnTb", [P, C, N])
        inflb = sb("inflb", [S, N])
        decb = sb("decb", [S, D])
        rest = sb("rest", [P, 2, C, N])
        parts = sb("parts", [P, 2, 3, C, N], BF16)
        Qs = sb("Qs", [R + 3, H, N], BF16)
        Ks = sb("Ks", [R + 3, H, N], BF16)
        V = sb("V", [P, J, H, 32])
        nm = sb("nm", [P, H * J])
        nmr = sb("nmr", [H * J, P])
        nmp = sb("nmp", [H * J, 3, P], BF16)
        gx = sb("gx", [P, C, N])
        fl = sb("fl", [P, C, N])
        PT = sb("PT", [P, 2, QH, N])
        OT = sb("OT", [P, 2, N])
        rec = sb("rec", [P, 2, J * QH])
        O = sb("O", [P, J, D])
        comb = sb("comb", [P, C, N])
        PA = ctx.enter_context(nc.psum_tensor("PA", [P, 2, 512], F32))
        PB = ctx.enter_context(nc.psum_tensor("PB", [P, 4, 512], F32))
        PC = ctx.enter_context(nc.psum_tensor("PC", [P, 2, 512], F32))

        w_in, nbg_ready, ones_ready = sem("w_in"), sem("nbg_ready"), sem("ones_ready")
        in_loaded, ex_loaded = sem("in_loaded"), sem("ex_loaded")
        qk_done, v_done = sem("qk_done"), sem("v_done")
        part1_ready, rest_ready, part2_ready, part3_ready = (sem(f"part{k}_ready") if k else sem("rest_ready") for k in (1, 0, 2, 3))
        v_ready, parts_out, stacked = sem("v_ready"), sem("parts_out"), sem("stacked")
        xt_done, xt_ready, h_done, h_ready = sem("xt_done"), sem("xt_ready"), sem("h_done"), sem("h_ready")
        y_done, y_ready, y_out = sem("y_done"), sem("y_ready"), sem("y_out")
        max_done, max_taken, nmT_done, nmp_ready, nm_placed = (sem(n) for n in ("max_done", "max_taken", "nmT_done", "nmp_ready", "nm_placed"))
        gate_done, flow_done, gx_ready, fl_ready = sem("gate_done"), sem("flow_done"), sem("gx_ready"), sem("fl_ready")
        s_done, e_done, pt_used, av_done, ot_ready = (sem(n) for n in ("s_done", "e_done", "pt_used", "av_done", "ot_ready"))
        ot_turned, rec_ready, o_taken = sem("ot_turned"), sem("rec_ready"), sem("o_taken")
        ot_done, comb_ready, wo_done, x_added = (sem(n) for n in ("ot_done", "comb_ready", "wo_done", "x_added"))
        v2_step = sem("v2_step")
        NSTACK = 2 * len(PAIRS)
        NU = NG * J

        with nc.Block() as block:
            @block.sync
            def _(sp):
                for name, t in (("Wq", Wq), ("Wk", Wk), ("Wv", Wv), ("Wo", Wo), ("Wg", Wg)):
                    sp.dma_start(t[:, :, :], T[name].rearrange("(c p) n -> p c n", p=P)).then_inc(w_in, 16)
                for c in range(C):
                    sp.dma_start(nbg[:, c:c + 1], column(T["bg"][c * P:(c + 1) * P])).then_inc(w_in, 16)

                def load(b):
                    sp.dma_start(xnTb[:, :, :], T["xnT"][ds(b, 1), :, :, :].squeeze(0)).then_inc(in_loaded, 16)
                    sp.dma_start(inflb[:, :], T["inflT"][ds(b, 1), :, :].squeeze(0)).then_inc(in_loaded, 16)
                    sp.dma_start(decb[:, :], T["dec"][ds(b, 1), :, :].squeeze(0)).then_inc(in_loaded, 16)

                def stack(b):
                    def out(k, ready):
                        for w in range(2):
                            sp.wait_ge(ready, b * 2 + w + 1)
                            sp.dma_start(T["parts"][w, k].rearrange("(c p) n -> p c n", p=P), parts[:, w, k, :, :]).then_inc(parts_out, 16)

                    def back(k):
                        for n, pair in enumerate(PAIRS):
                            for w, st in ((0, Qs), (1, Ks)):
                                if pair[w] == k:
                                    sp.dma_start(st[n * DH:(n + 1) * DH, :, :],
                                                 T["parts"][w, k].rearrange("(h d) n -> d h n", d=DH)).then_inc(stacked, 16)

                    out(0, part1_ready)
                    sp.wait_ge(parts_out, b * 96 + 32)
                    back(0)
                    out(1, part2_ready)
                    out(2, part3_ready)
                    sp.wait_ge(parts_out, b * 96 + 96)
                    back(1)
                    back(2)

                load(0)
                stack(0)

                def body(i, last):
                    sp.wait_ge(nmp_ready, i + 1)
                    for k in range(3):
                        sp.dma_start(Qs[R + k:R + k + 1, :, :].rearrange("o h (j n) -> o (h j) n", n=P), nmp[:, k, :]).then_inc(nm_placed, 16)
                    if not last:
                        sp.wait_ge(flow_done, i + 1)
                        load(i + 1)
                        sp.wait_ge(s_done, i * 2 * NU + 2 * NU)
                        stack(i + 1)
                loop(sp, B, body)

            @block.gpsimd
            def _(pool):
                def load(e):
                    nc.gpsimd.dma_start(W1[:, :, :], T["W1"][ds(e, 1)].squeeze(0).rearrange("(c p) n -> p c n", p=P)).then_inc(ex_loaded, 16)
                    nc.gpsimd.dma_start(W2[:, :, :], T["W2"][ds(e, 1)].squeeze(0).rearrange("(c p) n -> p c n", p=P)).then_inc(ex_loaded, 16)
                    nc.gpsimd.dma_start(xe[:, :, :], T["xe"][ds(e * N, N), :].rearrange("(j p) d -> p j d", p=P)).then_inc(ex_loaded, 16)

                def third_part(b):
                    for w in range(2):
                        pool.wait_ge(part2_ready, b * 2 + w + 1)
                        nc.gpsimd.tensor_tensor(parts[:, w, 2, :, :], rest[:, w, :, :], parts[:, w, 1, :, :],
                                                ALU.subtract).then_inc(part3_ready, 1)

                load(0)
                third_part(0)

                def body(i, last):
                    if not last:
                        wait_apart(pool, y_done, i * J + J, (ones_ready, 2))
                        load(i + 1)
                        third_part(i + 1)
                loop(pool, B, body)

            @block.scalar
            def _(act):
                A = nc.scalar.activation

                def first_parts(b):
                    for w in range(2):
                        act.wait_ge(qk_done, b * 2 + w + 1)
                        if not (isinstance(b, int) and b == 0):
                            act.wait_ge(parts_out, b * 96)
                        A(parts[:, w, 0, :, :], PB[:, 2 * w:2 * w + 2, :], ACT.Copy, scale=DH ** -0.5 if w == 0 else 1.0).then_inc(part1_ready, 1)
                    for j in range(J):
                        if j % 2 == 0:
                            act.wait_ge(v_done, b * 2 + j // 2 + 1)
                        A(V[:, j, :, 0:DH], PC[:, j // 2, j % 2 * D:(j % 2 + 1) * D].rearrange("p (h d) -> p h d", d=DH),
                          ACT.Copy).then_inc(v_ready, 1)
                    for w in range(2):
                        act.wait_ge(rest_ready, b * 2 + w + 1)
                        A(parts[:, w, 1, :, :], rest[:, w, :, :], ACT.Copy).then_inc(part2_ready, 1)

                act.wait_ge(ones_ready, 1)
                act.wait_ge(w_in, 16 * (5 + C))
                A(nbg[:, :], nbg[:, :], ACT.Copy, scale=-1.0).then_inc(nbg_ready, 1)
                act.wait_ge(nbg_ready, 1)
                first_parts(0)
                act.sem_inc(y_out, 16)

                def exps(i, u):
                    for g in range(2):
                        if g == 0:
                            act.wait_ge(pt_used, i * NU + (u + 1))
                        act.wait_ge(s_done, i * 2 * NU + (2 * u + g + 1))
                        A(PT[:, u % 2, 2 * g:2 * g + 2, :], PB[:, 2 * g:2 * g + 2, :], ACT.Exp).then_inc(e_done, 1)

                def body(i, last):
                    act.wait_ge(xt_done, i + 1)
                    A(xeT[:, :, :], PB[:, 0:2, :], ACT.Copy).then_inc(xt_ready, 1)
                    for f in range(FT):
                        act.wait_ge(h_done, i * FT + (f + 1))
                        A(hT[:, f, :], PB[:, f % 4, :], ACT.Relu).then_inc(h_ready, 1)
                    act.wait_ge(y_out, i * 16 + 16)
                    for j in range(J):
                        act.wait_ge(y_done, i * J + (j + 1))
                        A(ysb[:, j, :], PB[:, j, 0:D], ACT.Copy).then_inc(y_ready, 1)
                    act.wait_ge(y_ready, i * J + J)
                    act.dma_start(T["ye"][ds(i * N, N), :].rearrange("(j p) d -> p j d", p=P), ysb[:, :, :]).then_inc(y_out, 16)
                    act.wait_ge(gate_done, i + 1)
                    for c in range(C):
                        last_i = A(gx[:, c, :], PB[:, c, :], ACT.Exp, scale=-1.0, bias=nbg[:, c:c + 1])
                    last_i.then_inc(gx_ready, 1)
                    for u in range(NU):
                        exps(i, u)
                    if not last:
                        first_parts(i + 1)
                loop(act, B, body)
                act.wait_ge(y_out, 16 * (B + 1))

            @block.tensor
            def _(pe):
                M = nc.tensor.matmul

                def project(b):
                    pe.wait_ge(in_loaded, b * 48 + 48)
                    for w, W in ((0, Wq), (1, Wk)):
                        for m in range(C):
                            for c in range(C):
                                last = M(PB[:, 2 * w + m, :], W[:, c, m * P:(m + 1) * P], xnTb[:, c, :], start=(c == 0), stop=(c == C - 1))
                        last.then_inc(qk_done, 1)
                    for j in range(J):
                        for c in range(C):
                            last = M(PC[:, j // 2, j % 2 * D:(j % 2 + 1) * D], xnTb[:, c, j * P:(j + 1) * P], Wv[:, c, :],
                                     start=(c == 0), stop=(c == C - 1))
                        if j % 2:
                            last.then_inc(v_done, 1)

                def scores(i, u):
                    hg, c = divmod(u, J)
                    for g in range(2):
                        if u == 0:
                            pe.wait_ge((gx_ready, fl_ready)[g], i + 1)
                        else:
                            pe.wait_ge(e_done, i * 2 * NU + (2 * u + g - 1))
                        for q in (2 * g, 2 * g + 1):
                            h = hg * QH + q
                            mm = M(PB[:, q, :], Ks[:, h, c * P:(c + 1) * P], Qs[:, h, :], start=True, stop=True)
                        mm.then_inc(s_done, 1)

                def values(i, u):
                    hg, c = divmod(u, J)
                    pe.wait_ge(e_done, i * 2 * NU + (2 * u + 2))
                    for q in range(QH):
                        mm = M(PC[32 * q:32 * q + 32, 0, :], V[:, c, hg * QH + q, :], PT[:, u % 2, q, :],
                               start=(c == 0), stop=(c == J - 1))
                    mm.then_inc(pt_used, 1)

                def turn_values(i, hg):
                    pe.wait_ge(ot_ready, i * NG + (hg + 1))
                    pe.wait_ge(o_taken, i * NG + (hg + 1))
                    for j in range(J):
                        mm = nc.tensor.transpose(PC[:, 1, j * P:(j + 1) * P], OT[:, hg % 2, j * P:(j + 1) * P], ident[:, :])
                    mm.then_inc(ot_turned, 1)

                pe.wait_ge(w_in, 16 * (5 + C))
                pe.sem_inc(pt_used, 2)
                project(0)

                def body(i, last):
                    pe.wait_ge(ex_loaded, i * 48 + 48)
                    pe.wait_ge(rest_ready, i * 2 + 2)
                    for j in range(J):
                        for c in range(C):
                            mm = nc.tensor.transpose(PB[:, c, j * P:(j + 1) * P], xe[:, j, c * P:(c + 1) * P], ident[:, :])
                    mm.then_inc(xt_done, 1)
                    n_max = [0]

                    def maxima(count):
                        for n in range(n_max[0], min(n_max[0] + count, H * J)):
                            h, j = divmod(n, J)
                            if n == 0:
                                pe.wait_ge(stacked, i * 16 * NSTACK + 16 * NSTACK)
                                pe.wait_ge(x_added, i * 2 + 2)
                            if n >= 2:
                                pe.wait_ge(max_taken, i * H * J + (n - 1))
                            M(PA[:, n % 2, :], Qs[0:R, h, j * P:(j + 1) * P], Ks[0:R, h, :], start=True, stop=True).then_inc(max_done, 1)
                        n_max[0] += count

                    for f in range(FT):
                        if f == 0:
                            pe.wait_ge(xt_ready, i + 1)
                        if f >= 4:
                            pe.wait_ge(h_ready, i * FT + (f - 3))
                        for c in range(C):
                            mm = M(PB[:, f % 4, :], W1[:, c, f * P:(f + 1) * P], xeT[:, c, :], start=(c == 0), stop=(c == C - 1))
                            if c == C - 1:
                                mm.then_inc(h_done, 1)
                            if f >= 3:
                                maxima(2)
                    pe.wait_ge(h_ready, i * FT + FT)
                    for j in range(J):
                        for f in range(FT):
                            mm = M(PB[:, j, 0:D], hT[:, f, j * P:(j + 1) * P], W2[:, f, :], start=(f == 0), stop=(f == FT - 1))
                            if f == FT - 1:
                                mm.then_inc(y_done, 1)
                            maxima(1 if f % 4 else 2)
                    maxima(H * J)
                    wait_apart(pe, max_taken, i * H * J + H * J, (w_in, 16))
                    nc.tensor.transpose(PC[0:H * J, 0, 0:P], nm[:, :], ident[:, :]).then_inc(nmT_done, 1)
                    pe.wait_ge(y_ready, i * J + J)
                    for m in range(C):
                        for c in range(C):
                            mm = M(PB[:, m, :], Wg[:, c, m * P:(m + 1) * P], xnTb[:, c, :], start=(c == 0), stop=(c == C - 1))
                    mm.then_inc(gate_done, 1)
                    for m in range(C):
                        mm = M(PB[:, 2 + m, :], decb[:, m * P:(m + 1) * P], inflb[:, :], start=True, stop=True)
                    mm.then_inc(flow_done, 1)
                    pe.wait_ge(ones_ready, 2)
                    pe.wait_ge(nm_placed, i * 48 + 48)
                    pe.wait_ge(v_ready, i * J + J)
                    scores(i, 0)
                    for u in range(NU):
                        if u + 1 < NU:
                            scores(i, u + 1)
                        if u % J == 0 and u:
                            pe.wait_ge(ot_ready, i * NG + u // J)
                        values(i, u)
                        if u % J == 1 and u > J:
                            turn_values(i, u // J - 1)
                    if not last:
                        pe.wait_ge(e_done, i * 2 * NU + 2 * NU)
                    turn_values(i, NG - 1)
                    pe.wait_ge(o_taken, i * NG + (NG + 1))
                    if not last:
                        project(i + 1)
                        pe.wait_ge(v_ready, i * J + 2 * J)
                    for c in range(C):
                        for j in range(J):
                            mm = nc.tensor.transpose(PC[:, c, j * P:(j + 1) * P], O[:, j, c * P:(c + 1) * P], ident[:, :])
                    mm.then_inc(ot_done, 1)
                    pe.wait_ge(comb_ready, i + 1)
                    for j in range(J):
                        for c in range(C):
                            mm = M(PA[:, j // 2, j % 2 * D:(j % 2 + 1) * D], comb[:, c, j * P:(j + 1) * P], Wo[:, c, :],
                                   start=(c == 0), stop=(c == C - 1))
                        if j % 2:
                            mm.then_inc(wo_done, 1)
                loop(pe, B, body)

            @block.vector
            def _(ve):
                v = nc.vector
                st = Steps(ve, v2_step, (ones_ready, 1))

                def rests(b):
                    for w in range(2):
                        ve.wait_ge(part1_ready, b * 2 + w + 1)
                        if not (isinstance(b, int) and b == 0):
                            ve.wait_ge(part3_ready, b * 2)
                        v.scalar_tensor_tensor(out=rest[:, w, :, :], in0=PB[:, 2 * w:2 * w + 2, :], scalar=DH ** -0.5 if w == 0 else 1.0,
                                               in1=parts[:, w, 0, :, :], op0=ALU.mult, op1=ALU.subtract).then_inc(rest_ready, 1)

                v.memset(V[:, :, :, :], 1.0).then_inc(ones_ready, 1)
                v.memset(Ks[R:R + 3, :, :], 1.0).then_inc(ones_ready, 1)
                rests(0)
                ve.sem_inc(x_added, 2)
                ve.sem_inc(o_taken, 1)

                def body(i, last):
                    for n in range(H * J):
                        ve.wait_ge(max_done, i * H * J + (n + 1))
                        v.tensor_reduce(nm[:, n:n + 1], PA[:, n % 2, :], AX.X, ALU.max, negate=True).then_inc(max_taken, 1)
                    ve.wait_ge(nmT_done, i + 1)
                    rows = PC[0:H * J, 0, 0:P]
                    st.link(v.tensor_copy(nmp[:, 0, :], rows))
                    st.link(v.tensor_tensor(nmr[:, :], rows, nmp[:, 0, :], ALU.subtract))
                    st.link(v.tensor_copy(nmp[:, 1, :], nmr[:, :]))
                    v.tensor_tensor(nmp[:, 2, :], nmr[:, :], nmp[:, 1, :], ALU.subtract).then_inc(nmp_ready, 1)
                    ve.wait_ge(flow_done, i + 1)
                    v.tensor_scalar(fl[:, :, :], PB[:, 2:4, :], 0.4, None, ALU.mult).then_inc(fl_ready, 1)
                    ve.wait_ge(gx_ready, i + 1)
                    st.link(v.tensor_scalar(gx[:, :, :], gx[:, :, :], 1.0, None, ALU.add))
                    st.link(v.reciprocal(gx[:, :, :], gx[:, :, :]))
                    ve.wait_ge(fl_ready, i + 1)
                    v.tensor_tensor(fl[:, :, :], fl[:, :, :], gx[:, :, :], ALU.mult)
                    for hg in range(NG):
                        ve.wait_ge(pt_used, i * NU + ((hg + 1) * J + 2))
                        v.tensor_copy(OT[:, hg % 2, :], PC[:, 0, :]).then_inc(ot_ready, 1)
                        ve.wait_ge(ot_turned, i * NG + (hg + 1))
                        o = PC[:, 1, :].rearrange("p (j q d) -> p j q d", j=J, q=QH)
                        r = rec[:, hg % 2, :].rearrange("p (j q) -> p j q", j=J)
                        v.reciprocal(r, o[:, :, :, DH]).then_inc(rec_ready, 1)
                        ve.wait_ge(rec_ready, i * NG + (hg + 1))
                        v.tensor_tensor(O[:, :, hg * QH * DH:(hg + 1) * QH * DH].rearrange("p j (q d) -> p j q d", q=QH), o[:, :, :, 0:DH],
                                        r.unsqueeze(3).to_broadcast([P, J, QH, DH]), ALU.mult).then_inc(o_taken, 1)
                    if not last:
                        rests(i + 1)
                    ve.wait_ge(ot_done, i + 1)
                    v.scalar_tensor_tensor(out=comb[:, :, :], in0=PC[:, :, :], scalar=0.6, in1=fl[:, :, :],
                                           op0=ALU.mult, op1=ALU.add).then_inc(comb_ready, 1)
                    for q in range(2):
                        ve.wait_ge(wo_done, i * 2 + (q + 1))
                        xs = x_all[:, ds(i * J + 2 * q, 2), :]
                        v.tensor_tensor(xs, PA[:, q, :].rearrange("p (j d) -> p j d", j=2), xs, ALU.add).then_inc(x_added, 1)
                loop(ve, B, body, st, 5)
        clear(nc, used)


def phase_middle(nc, T, G):
    B, N, D = T["x"].shape
    E = T["rw"].shape[1]
    C, J = D // P, N // P
    NT = B * J
    NS = T["xs"].shape[0] // P
    RING = 2 * J
    DT = 0.01
    GAMMA_FLOOR = 0.1
    x_all, y_all, ident, ones, strict, mhalf = (G[n] for n in ("x_all", "y_all", "ident", "ones", "strict", "mhalf"))
    take0, pkeep0, slot1, weight1, tile_expert = (G[n] for n in ("take0", "pkeep0", "slot1", "weight1", "tile_expert"))
    dcol, ccol, gate, lin, decay_mask = (G[n] for n in ("dcol", "ccol", "gate", "lin", "decay_mask"))
    anti, moe_w_in = G["anti"], G["moe_w_in"]
    with ExitStack() as ctx:
        used = []

        def sb(name, shape, dt=F32):
            return ctx.enter_context(nc.sbuf_tensor(name, shape, dt))

        def sem(name):
            used.append(ctx.enter_context(nc.semaphore(name)))
            return used[-1]

        incl = sb("incl", [P, P])
        pref = sb("pref", [P, E])
        steps128 = sb("steps128", [P, NT])
        tile_no = sb("tile_no", [P, NS])
        spare = G["Wqkv"][:, :, :].rearrange("p c n -> p (c n)")
        back = spare[:, 0:RING * D].rearrange("p (t d) -> p t d", d=D)
        yT = spare[:, RING * D:RING * D + C * N].rearrange("p (c n) -> p c n", n=N)
        stats = sb("stats3", [P, J, 6])
        mvb = sb("mvb", [P, J, 2])
        mv = sb("mv3", [P, NT, 2])
        var2 = sb("var2", [P, 2, NT])
        rs = sb("rs", [P, 2, NT])
        proj = sb("proj", [P, C, E + 2])
        pv = sb("pv", [P, C, 4])
        lb = sb("lb", [P, C, P])
        wpot = sb("wpot", [P, C, 2])
        consts2 = sb("consts2", [P, 4])
        psc = sb("psc", [P, E])
        bpot = sb("bpot", [P, 2])
        y = sb("y", [P, J, D])
        lg = sb("lg3", [P, NT, E + 2])
        ra, rb, oh1, oh2, oh12 = (sb(n, [P, NT, E]) for n in ("ra1", "rb1", "oh1", "oh2", "oh12"))
        pot = sb("pot", [P, 3, NT])
        gam = sb("gam", [P, NT])
        small = sb("small3", [P, 8, NT])
        base = sb("base3", [P, 4, E])
        tcmp = sb("tcmp", [1, NS, E])
        turned = sb("turned", [3 * NT, 2, P])
        tp = ctx.enter_context(nc.psum_tensor("tp3", [P, C, N], F32))
        lgp = ctx.enter_context(nc.psum_tensor("lgp3", [P, 512], F32))
        rkp = ctx.enter_context(nc.psum_tensor("rkp3", [P, 2, 512], F32))
        cp = ctx.enter_context(nc.psum_tensor("cp3", [P, 2, 512], F32))
        lgv = lgp[:, 0:J * (E + 2)].rearrange("p (j e) -> p j e", e=E + 2)

        c_ready, w_in, gathered, x1_ready = sem("c3_ready"), sem("w3_in"), [sem("gathered_even"), sem("gathered_odd")], sem("x1_ready")
        var_ready, rs_ready, y_ready = sem("var3_ready"), sem("rs3_ready"), sem("yl_ready")
        tp_ready, yT_ready, lg_done, lg_copied = sem("tp3_ready"), sem("yT_ready"), sem("lg3_done"), sem("lg3_copied")
        proj_ready, sums_done, y_kept = sem("proj_ready"), sem("sums_done"), sem("y_kept")
        r_sub, r_exp, oh_ready, rank_done, slots_ready = (sem(n) for n in ("r3_sub", "r3_exp", "oh3_ready", "rank3_done", "slots3_ready"))
        sp_in, sp_exp, sp_1p, sp_ln, gam_ready, cum_done, cols_ready = (
            sem(n) for n in ("sp_in", "sp_exp", "sp_1p", "sp_ln", "gam_ready", "cum_done", "cols_ready"))
        rows_done, rows_ready, rows_out = sem("rows_done"), sem("rows_ready"), sem("rows_out")
        v_step, p_step = sem("v3_step"), sem("p3_step")
        NW = C * 4 + 3

        with nc.Block() as block:
            @block.sync
            def _(sp):
                for c in range(C):
                    part = slice(c * P, (c + 1) * P)
                    sp.dma_start(pv[:, c, 0:1], column(T["rscale"][part])).then_inc(w_in, 16)
                    sp.dma_start(pv[:, c, 1:2], column(T["ln1_g"][part])).then_inc(w_in, 16)
                    sp.dma_start(pv[:, c, 2:3], column(T["ln1_b"][part])).then_inc(w_in, 16)
                    sp.dma_start(proj[:, c, 0:E], T["rw"][part, :]).then_inc(w_in, 16)
                sp.dma_start(wpot[:, :, :], T["w_pot"].rearrange("(c p) n -> p c n", p=P)).then_inc(w_in, 16)
                sp.dma_start(psc[:, :], row_of(T["pscale"], P)).then_inc(w_in, 16)
                sp.dma_start(bpot[:, :], row_of(T["b_pot"], P)).then_inc(w_in, 16)
                sp.wait_ge(x1_ready, B)
                for e in range(E):
                    for c in range(C):
                        sp.dma_start(gate[:, c, e, :], T["gate"][e, c * P:(c + 1) * P].rearrange("p g h -> p (g h)")).then_inc(moe_w_in, 16)
                    sp.dma_start(lin[:, e, :, :], T["lin"][e].rearrange("(f p) d -> p f d", p=P)).then_inc(moe_w_in, 16)
                sp.wait_ge(rows_ready, 2)
                for k in range(2):
                    sp.dma_start(T["drow"][k].rearrange("c b (j n) -> (c b j) n", n=P), turned[0:2 * NT, k, :]).then_inc(rows_out, 16)
                sp.dma_start(T["crow"].rearrange("b (j n) -> (b j) n", n=P), turned[2 * NT:3 * NT, 0, :]).then_inc(rows_out, 16)
                sp.wait_ge(rows_out, 48)

            @block.gpsimd
            def _(pool):
                st = Steps(pool, p_step)
                for t in range(RING):
                    nc.gpsimd.indirect_dma_start(
                        out=back[:, t % RING, :], out_offset=None, in_=T["ye"],
                        in_offset=bass.IndirectOffsetOnAxis(ap=take0[:, t:t + 1], axis=0),
                        bounds_check=B * N - 1, oob_is_err=False).then_inc(gathered[t // J % 2], 16)
                pool.wait_ge(w_in, 16 * NW)
                st.link(nc.gpsimd.memset(incl[:, :], 0.0))
                st.link(nc.gpsimd.memset(anti[:, :], 0.0))
                st.link(nc.gpsimd.memset(decay_mask[:, :], 0.1))
                nc.gpsimd.affine_select(out=incl[:, :], in_=incl[:, :], compare_op=ALU.is_ge, fill=1.0,
                                        base=-1, pattern=[[-1, P]], channel_multiplier=1).then_inc(c_ready, 1)
                nc.gpsimd.affine_select(out=anti[:, :], in_=anti[:, :], compare_op=ALU.not_equal, fill=1.0,
                                        base=1 - P, pattern=[[1, P]], channel_multiplier=1).then_inc(c_ready, 1)
                nc.gpsimd.affine_select(out=decay_mask[:, :], in_=decay_mask[:, :], compare_op=ALU.is_ge, fill=0.0,
                                        base=0, pattern=[[1, N]], channel_multiplier=-1).then_inc(c_ready, 1)
                for tile, pattern, first in ((pref, [[-1, E]], E), (steps128, [[P, NT]], 0), (tile_no, [[1, NS]], 0)):
                    nc.gpsimd.iota(tile[:, :], pattern=pattern, base=first, channel_multiplier=0,
                                   allow_small_or_imprecise_dtypes=True).then_inc(c_ready, 1)
                for t in range(RING, NT):
                    if t % J == 0:
                        pool.wait_ge(x1_ready, t // J - RING // J + 1)
                    nc.gpsimd.indirect_dma_start(
                        out=back[:, t % RING, :], out_offset=None, in_=T["ye"],
                        in_offset=bass.IndirectOffsetOnAxis(ap=take0[:, t:t + 1], axis=0),
                        bounds_check=B * N - 1, oob_is_err=False).then_inc(gathered[t // J % 2], 16)
                pool.wait_ge(var_ready, 1)
                nc.gpsimd.tensor_tensor(rs[:, 0, :], var2[:, 0, :], mhalf[:, :], ALU.pow).then_inc(rs_ready, 1)
                pool.wait_ge(var_ready, 2)
                nc.gpsimd.tensor_tensor(rs[:, 0, :], var2[:, 0, :], mhalf[:, :], ALU.pow).then_inc(rs_ready, 1)
                nc.gpsimd.tensor_tensor(rs[:, 1, :], var2[:, 1, :], mhalf[:, :], ALU.pow).then_inc(rs_ready, 1)

            @block.scalar
            def _(act):
                A = nc.scalar.activation
                act.sem_inc(yT_ready, 1)
                act.sem_inc(lg_copied, 1)
                act.sem_inc(y_kept, 1)
                with act.Fori(0, B) as b:
                    act.wait_ge(y_ready, b + 1)
                    A(y_all[:, ds(b * J, J), :], y[:, :, :], ACT.Copy).then_inc(y_kept, 1)
                    act.wait_ge(tp_ready, b + 2)
                    act.wait_ge(lg_done, b + 1)
                    A(yT[:, :, :], tp[:, :, :], ACT.Copy).then_inc(yT_ready, 1)
                    act.wait_ge(lg_done, b + 2)
                    A(lg[:, ds(b * J, J), :], lgv, ACT.Copy).then_inc(lg_copied, 1)
                act.wait_ge(r_sub, 1)
                A(rb[:, :, :], ra[:, :, :], ACT.Exp).then_inc(r_exp, 1)
                act.wait_ge(sp_in, 1)
                A(small[:, 1, :], small[:, 0, :], ACT.Exp, scale=-1.0).then_inc(sp_exp, 1)
                act.wait_ge(sp_exp, 1)
                A(small[:, 2, :], small[:, 1, :], ACT.Ln, bias=1.0).then_inc(sp_ln, 1)
                act.wait_ge(rows_done, 1)
                A(turned[:, 0, :], cp[0:3 * NT, 0, 0:P], ACT.Copy).then_inc(rows_ready, 1)
                A(turned[0:2 * NT, 1, :], cp[0:2 * NT, 1, 0:P], ACT.Copy).then_inc(rows_ready, 1)

            @block.tensor
            def _(pe):
                M = nc.tensor.matmul
                pe.wait_ge(proj_ready, 2)
                for c in range(C):
                    M(cp[:, 0, 0:2], ones[:, :], proj[:, c, E:E + 2], start=(c == 0), stop=(c == C - 1))
                for c in range(C):
                    last = M(cp[:, 0, 2:4], lb[:, c, :], wpot[:, c, :], start=(c == 0), stop=(c == C - 1))
                last.then_inc(sums_done, 1)
                pe.sem_inc(lg_done, 1)
                pe.sem_inc(tp_ready, 1)
                with pe.Fori(0, B) as b:
                    pe.wait_ge(y_ready, b + 1)
                    pe.wait_ge(yT_ready, b + 1)
                    for j in range(J):
                        for c in range(C):
                            last = nc.tensor.transpose(tp[:, c, j * P:(j + 1) * P], y[:, j, c * P:(c + 1) * P], ident[:, :])
                    last.then_inc(tp_ready, 1)
                    pe.wait_ge(yT_ready, b + 2)
                    pe.wait_ge(lg_copied, b + 1)
                    for j in range(J):
                        for c in range(C):
                            last = M(lgv[:, j, :], yT[:, c, j * P:(j + 1) * P], proj[:, c, :], start=(c == 0), stop=(c == C - 1))
                    last.then_inc(lg_done, 1)
                pe.wait_ge(gam_ready, 1)
                M(cp[:, 0, 0:NT], incl[:, :], gam[:, :], start=True, stop=True)
                M(cp[:, 1, 0:NT], ones[:, :], gam[:, :], start=True, stop=True).then_inc(cum_done, 1)
                pe.wait_ge(oh_ready, 3)
                ohf = oh12[:, :, :].rearrange("p t e -> p (t e)")
                M(rkp[:, 0, 0:NT * E], strict[:, :], ohf, start=True, stop=True)
                M(rkp[:, 1, 0:NT * E], ones[:, :], ohf, start=True, stop=True).then_inc(rank_done, 1)
                pe.wait_ge(cols_ready, 1)
                M(cp[0:3 * NT, 0, 0:P], pot[:, :, :].rearrange("p c t -> p (c t)"), ident[:, :], start=True, stop=True)
                M(cp[0:2 * NT, 1, 0:P], pot[:, 0:2, :].rearrange("p c t -> p (c t)"), anti[:, :], start=True, stop=True).then_inc(rows_done, 1)

            @block.vector
            def _(ve):
                st = Steps(ve, v_step, (c_ready, 6))
                link = st.link
                V = nc.vector
                ve.wait_ge(w_in, 16 * NW)
                ve.wait_ge(c_ready, 6)
                for c in range(C):
                    V.tensor_scalar(proj[:, c, E:E + 2], wpot[:, c, :], pv[:, c, 1:2], None, ALU.mult)
                    V.tensor_scalar(lb[:, c, :], ones[:, :], pv[:, c, 2:3], None, ALU.mult)
                    last = V.tensor_scalar(proj[:, c, 0:E], proj[:, c, 0:E], pv[:, c, 0:1], None, ALU.mult)
                    last.then_inc(proj_ready, 1)
                ve.wait_ge(sums_done, 1)
                V.tensor_copy(consts2[:, 0:2], cp[:, 0, 0:2])
                link(V.tensor_tensor(consts2[:, 2:4], cp[:, 0, 2:4], bpot[:, :], ALU.add))
                with ve.Fori(0, B // 2) as pair:
                    st.enter(pair, 6)
                    for half in range(2):
                        b = pair * 2 + half
                        ve.wait_ge(gathered[half], pair * 16 * J + 16 * J)
                        for j in range(J):
                            x = x_all[:, ds(b * J + j, 1), :].squeeze(1)
                            last = V.scalar_tensor_tensor(out=x, in0=back[:, half * J + j, :], scalar=pkeep0[:, ds(b * J + j, 1)], in1=x,
                                                          op0=ALU.mult, op1=ALU.add)
                        last.then_inc(x1_ready, 1)
                        wait_apart(ve, x1_ready, b + 1, (c_ready, 6))
                        for j in range(J):
                            last = V.bn_stats(stats[:, j, :], x_all[:, b * J + j, :])
                        link(last, apart=True)
                        for j in range(J):
                            last = V.bn_aggr(mvb[:, j, :], stats[:, j, :])
                        link(last, apart=True)
                        link(V.tensor_copy(mv[:, ds(b * J, J), :], mvb[:, :, :]))
                st.leave(B // 2)
                V.tensor_scalar(var2[:, 0, :], mv[:, :, 1], 1e-5, None, ALU.add).then_inc(var_ready, 1)
                ve.wait_ge(rs_ready, 1)
                with ve.Fori(0, B) as b:
                    st.enter(b, 3)
                    ve.wait_ge(tp_ready, b + 1)
                    wait_apart(ve, y_kept, b + 1, (c_ready, 6))
                    for j in range(J):
                        last = V.tensor_scalar(y[:, j, :], x_all[:, ds(b * J + j, 1), :].squeeze(1), mv[:, ds(b * J + j, 1), 0:1].squeeze(1),
                                               rs[:, 0, ds(b * J + j, 1)], ALU.subtract, ALU.mult)
                    last.then_inc(y_ready, 1)
                    wait_apart(ve, y_ready, b + 1, (c_ready, 6))
                    for j in range(J):
                        last = V.bn_stats(stats[:, j, :], y[:, j, :])
                    link(last, apart=True)
                    for j in range(J):
                        last = V.bn_aggr(mvb[:, j, :], stats[:, j, :])
                    link(last, apart=True)
                    link(V.tensor_copy(mv[:, ds(b * J, J), :], mvb[:, :, :]))
                st.leave(B)
                mean, var = mv[:, :, 0], mv[:, :, 1]
                link(V.tensor_tensor(small[:, 0, :], mean, mean, ALU.mult))
                V.tensor_scalar(var2[:, 0, :], var, 1e-5, None, ALU.add)
                V.scalar_tensor_tensor(out=var2[:, 1, :], in0=small[:, 0, :], scalar=1e-6, in1=var, op0=ALU.add, op1=ALU.add).then_inc(var_ready, 1)
                ve.wait_ge(rs_ready, 3)
                ve.wait_ge(lg_copied, B + 1)
                for k in range(2):
                    link(V.scalar_tensor_tensor(out=small[:, 1 + k, :], in0=mean, scalar=consts2[:, k:k + 1], in1=lg[:, :, E + k],
                                                op0=ALU.mult, op1=ALU.subtract))
                    link(V.tensor_tensor(small[:, 3 + k, :], small[:, 1 + k, :], rs[:, 0, :], ALU.mult))
                    link(V.tensor_scalar(small[:, 5 + k, :], small[:, 3 + k, :], -1.0, consts2[:, 2 + k:3 + k], ALU.mult, ALU.add))
                V.tensor_scalar(pot[:, 0, :], small[:, 5, :], 2.0, None, ALU.add)
                link(V.tensor_scalar(small[:, 7, :], small[:, 6, :], -1.0, None, ALU.mult))
                V.tensor_tensor(small[:, 0, :], small[:, 6, :], small[:, 7, :], ALU.max).then_inc(sp_in, 1)
                link(V.tensor_scalar(small[:, 3, :], small[:, 6, :], 0.0, GAMMA_FLOOR, ALU.max, ALU.add))
                link(V.tensor_scalar(small[:, 4, :], rs[:, 1, :], D ** -0.5, None, ALU.mult))
                link(V.tensor_tensor(lg[:, :, 0:E], lg[:, :, 0:E], last_dim(small[:, 4, :], E), ALU.mult))
                link(V.tensor_reduce(small[:, 5, :], lg[:, :, 0:E], AX.X, ALU.max))
                V.tensor_tensor(ra[:, :, :], lg[:, :, 0:E], last_dim(small[:, 5, :], E), ALU.subtract).then_inc(r_sub, 1)
                ve.wait_ge(sp_ln, 1)
                V.tensor_tensor(gam[:, :], small[:, 2, :], small[:, 3, :], ALU.add).then_inc(gam_ready, 1)
                ve.wait_ge(gam_ready, 1)
                V.tensor_scalar(pot[:, 1, :], gam[:, :], -1.0, None, ALU.mult)
                ve.wait_ge(cum_done, 1)
                link(V.tensor_copy(small[:, 0, :], cp[:, 0, 0:NT]))
                link(V.tensor_copy(small[:, 1, :], cp[:, 1, 0:NT]))
                own, whole = (small[:, k, :].rearrange("p (b j) -> p b j", j=J) for k in (0, 1))
                for k in range(1, J):
                    for j in range(J - 1, k - 1, -1):
                        link(V.tensor_tensor(own[:, :, j], own[:, :, j], whole[:, :, j - k], ALU.add))
                link(V.tensor_scalar(ccol[:, :], small[:, 0, :], DT, None, ALU.mult))
                link(V.tensor_copy(dcol[:, :, :], pot[:, 0:2, :]))
                V.tensor_copy(pot[:, 2, :], ccol[:, :]).then_inc(cols_ready, 1)
                ve.wait_ge(r_exp, 1)
                link(V.tensor_reduce(small[:, 0, :], rb[:, :, :], AX.X, ALU.add))
                link(V.reciprocal(small[:, 1, :], small[:, 0, :]))
                link(V.tensor_tensor(rb[:, :, :], rb[:, :, :], last_dim(small[:, 1, :], E), ALU.mult))
                for k, oh in ((0, oh1), (1, oh2)):
                    if k == 1:
                        link(V.scalar_tensor_tensor(out=lg[:, :, 0:E], in0=oh1[:, :, :], scalar=-3e38, in1=lg[:, :, 0:E], op0=ALU.mult, op1=ALU.add))
                        link(V.tensor_reduce(small[:, 5, :], lg[:, :, 0:E], AX.X, ALU.max))
                    link(V.tensor_tensor(ra[:, :, :], lg[:, :, 0:E], last_dim(small[:, 5, :], E), ALU.is_equal))
                    link(V.tensor_tensor(oh12[:, :, :], ra[:, :, :], mid_dim(pref[:, :], NT), ALU.mult))
                    link(V.tensor_reduce(small[:, 6, :], oh12[:, :, :], AX.X, ALU.max))
                    V.tensor_tensor(oh[:, :, :], oh12[:, :, :], last_dim(small[:, 6, :], E), ALU.is_equal).then_inc(oh_ready, 1)
                    ve.wait_ge(oh_ready, k + 1)
                V.tensor_tensor(oh12[:, :, :], oh1[:, :, :], oh2[:, :, :], ALU.add).then_inc(oh_ready, 1)
                for k, oh in ((0, oh1), (1, oh2)):
                    link(V.tensor_tensor(ra[:, :, :], rb[:, :, :], oh[:, :, :], ALU.mult))
                    link(V.tensor_reduce(small[:, k, :], ra[:, :, :], AX.X, ALU.add))
                    link(V.tensor_tensor(ra[:, :, :], oh[:, :, :], mid_dim(psc[:, :], NT), ALU.mult))
                    link(V.tensor_reduce(small[:, 2 + k, :], ra[:, :, :], AX.X, ALU.add))
                link(V.tensor_tensor(small[:, 4, :], small[:, 0, :], small[:, 1, :], ALU.add))
                link(V.scalar_tensor_tensor(out=small[:, 5, :], in0=small[:, 4, :], scalar=0.0, in1=small[:, 4, :], op0=ALU.is_le, op1=ALU.add))
                link(V.reciprocal(small[:, 6, :], small[:, 5, :]))
                for k in range(2):
                    link(V.tensor_tensor(small[:, k, :], small[:, k, :], small[:, 6, :], ALU.mult))
                    link(V.tensor_tensor(weight1[:, k, :], small[:, k, :], small[:, 2 + k, :], ALU.mult))
                ve.wait_ge(rank_done, 1)
                before = rkp[:, 0, 0:NT * E].rearrange("p (t e) -> p t e", e=E)
                count = rkp[:, 1, 0:NT * E].rearrange("p (t e) -> p t e", e=E)
                link(V.tensor_copy(ra[:, :, :], count))
                a, z, k = ra, rb, 1
                while k < NT:
                    link(V.tensor_copy(z[:, 0:k, :], a[:, 0:k, :]))
                    link(V.tensor_tensor(z[:, k:NT, :], a[:, k:NT, :], a[:, 0:NT - k, :], ALU.add))
                    a, z, k = z, a, 2 * k
                total = base[:, 0, :]
                link(V.tensor_copy(total, a[:, NT - 1, :]))
                lgt = lg[:, :, 0:E]
                link(V.tensor_tensor(lgt, mid_dim(total, NT), last_dim(steps128[:, :], E), ALU.is_gt))
                link(V.tensor_reduce(base[:, 1, :], lgt.rearrange("p t e -> p e t"), AX.X, ALU.add))
                link(V.tensor_copy(base[:, 2, :], base[:, 1, :]))
                for e in range(1, E):
                    link(V.tensor_tensor(base[:, 2, e:e + 1], base[:, 2, e:e + 1], base[:, 2, e - 1:e], ALU.add))
                link(V.tensor_tensor(base[:, 3, :], base[:, 2, :], base[:, 1, :], ALU.subtract))
                link(V.tensor_scalar(base[:, 3, :], base[:, 3, :], float(P), None, ALU.mult))
                link(V.tensor_tensor(z[:, :, :], a[:, :, :], count, ALU.subtract))
                link(V.tensor_tensor(a[:, :, :], z[:, :, :], before, ALU.add))
                link(V.tensor_tensor(z[:, :, :], a[:, :, :], mid_dim(base[:, 3, :], NT), ALU.add))
                for k, oh in ((0, oh1), (1, oh2)):
                    link(V.tensor_tensor(a[:, :, :], z[:, :, :], oh[:, :, :], ALU.mult))
                    link(V.tensor_reduce(small[:, 6 + k, :], a[:, :, :], AX.X, ALU.add))
                    V.tensor_copy(slot1[:, k, :], small[:, 6 + k, :]).then_inc(slots_ready, 1)
                link(V.tensor_tensor(tcmp[:, :, :], last_dim(tile_no[0:1, :], E), mid_dim(base[0:1, 2, :], NS), ALU.is_ge))
                link(V.tensor_reduce(tile_no[0:1, :], tcmp[:, :, :], AX.X, ALU.add))
                link(V.tensor_scalar(tile_expert[0:1, :], tile_no[0:1, :], float(E - 1), None, ALU.min))
        clear(nc, used)


def phase_experts1_scan(nc, T, G):
    B, N, D = T["x"].shape
    E, HID = T["lin"].shape[0], T["lin"].shape[1]
    C, J, FT = D // P, N // P, HID // P
    NS = T["xs"].shape[0] // P
    NT = B * J
    HW, F = T["w_out"].shape[0], T["w_ff1"].shape[1]
    y_all, ident, gate, lin, tile_expert, slot1 = (G[n] for n in ("y_all", "ident", "gate", "lin", "tile_expert", "slot1"))
    SCAN = 6
    SCAN_TRIPS = NS - 2
    AHEAD = N - SCAN * SCAN_TRIPS
    with ExitStack() as ctx:
        used = []

        def sb(name, shape, dt=F32):
            return ctx.enter_context(nc.sbuf_tensor(name, shape, dt))

        def sem(name):
            used.append(ctx.enter_context(nc.semaphore(name)))
            return used[-1]

        def bank(name, shape):
            return ctx.enter_context(nc.psum_tensor(name, shape, F32))

        xt = sb("xt4", [P, D])
        xT = sb("xT4", [P, C, P])
        gl = sb("gl", [P, HID])
        hid = sb("hid", [P, HID])
        hidT = sb("hidT", [P, FT, P])
        ysb = sb("ysb4", [P, D])
        bbk = sb("bbk", [P, D])
        dz = sb("dz", [2 * B, 2, N])
        z = sb("z", [2 * B, 2, N])
        sgn = sb("sgn", [2 * B, N // 2, 2])
        sq = sb("sq", [2 * B, 2])
        nrm = sb("nrm", [2 * B, 2])
        txp = bank("txp", [P, 4, P])
        gp = bank("gp", [P, 2, HID])
        htp = bank("htp", [P, FT, P])
        yp = bank("yp", [P, 512])

        xs_loaded, tx_done, xT_ready, g_done, gelu_ready, hid_ready = (
            sem(n) for n in ("xs_loaded", "tx_done", "xT4_ready", "g_done", "gelu_ready", "hid_ready"))
        ht_done, hidT_ready, y_done, y_copied, ys_out = (sem(n) for n in ("ht_done", "hidT_ready", "y4_done", "y4_copied", "ys_out"))
        scattered, next_in = sem("scattered1"), sem("next_in")
        d_in, z_ready, z_out, cf_step, b_in, b_added = (sem(n) for n in ("d_in", "zed_ready", "z_out", "cf_step", "bbk_in", "bbk_added"))

        with nc.Block() as block:
            @block.sync
            def _(sp):
                def load(i):
                    sp.dma_start(xt[:, :], T["xs"][ds(i * P, P), :]).then_inc(xs_loaded, 16)

                def store(i):
                    sp.wait_ge(y_copied, i + 2)
                    sp.dma_start(T["ys"][ds(i * P, P), :], ysb[:, :]).then_inc(ys_out, 16)

                sp.dma_start(bbk[:, :], row_of(T["b_bk"], P)).then_inc(b_in, 16)
                sp.dma_start(dz[0:B, :, :], T["drow"][0].rearrange("c b n -> b c n")).then_inc(d_in, 16)
                for j in range(J):
                    sp.dma_start(dz[B:2 * B, :, (J - 1 - j) * P:(J - j) * P],
                                 T["drow"][1].rearrange("c b n -> b c n")[:, :, j * P:(j + 1) * P]).then_inc(d_in, 16)
                for k in range(2):
                    sp.dma_start(G["wbk"][:, k, :], row_of(T["w_bk"][k], P)).then_inc(next_in, 16)
                for c in range(C):
                    for k, name in enumerate(("ln2_g", "ln2_b", "ln3_g", "ln3_b")):
                        sp.dma_start(G["cols"][:, c, k:k + 1], column(T[name][c * P:(c + 1) * P])).then_inc(next_in, 16)
                sp.dma_start(G["Wqkv"][:, :, :], T["w_qkv"].rearrange("(c p) n -> p c n", p=P)).then_inc(next_in, 16)
                for m in range(2 * HW // P):
                    sp.dma_start(G["bqk"][:, m:m + 1], column(T["b_qkv"][m * P:(m + 1) * P])).then_inc(next_in, 16)
                for f in range(F // P):
                    sp.dma_start(G["bf1"][:, f:f + 1], column(T["b_ff1"][f * P:(f + 1) * P])).then_inc(next_in, 16)
                for t, vector in ((G["bv"], T["b_qkv"][2 * HW:3 * HW]), (G["bout"], T["b_out"]), (G["bf2"], T["b_ff2"])):
                    sp.dma_start(t[:, :], row_of(vector, P)).then_inc(next_in, 16)
                sp.sem_inc(ys_out, 16)
                sp.wait_ge(scattered, 16 * 2 * NT)
                load(0)
                sp.wait_ge(tx_done, 1)
                load(1)
                sp.wait_ge(tx_done, 2)
                load(2)
                with sp.Fori(0, NS - 3) as k:
                    store(k)
                    sp.wait_ge(tx_done, k + 3)
                    load(k + 3)
                for i in range(NS - 3, NS):
                    store(i)
                sp.wait_ge(z_ready, 1)
                for way in range(2):
                    for c in range(2):
                        sp.dma_start(T["cf"][way, c], z[way * B:(way + 1) * B, c, :]).then_inc(z_out, 16)
                sp.wait_ge(z_out, 64)
                sp.wait_ge(next_in, 16 * (2 + 4 * C + 1 + 2 * HW // P + F // P + 3))
                sp.wait_ge(ys_out, 16 * (NS + 1))

            @block.gpsimd
            def _(pool):
                for t in range(NT):
                    for k in range(2):
                        nc.gpsimd.indirect_dma_start(
                            out=T["xs"], out_offset=bass.IndirectOffsetOnAxis(ap=slot1[:, k, t:t + 1], axis=0),
                            in_=y_all[:, t, :], in_offset=None, bounds_check=NS * P - 1, oob_is_err=False,
                        ).then_inc(scattered, 16)
                pool.wait_ge(b_in, 16)
                pool.wait_ge(scattered, 16 * 2 * NT)
                with pool.Fori(0, B) as b:
                    own = y_all[:, ds(b * J, J), :]
                    nc.gpsimd.tensor_tensor(own, own, mid_dim(bbk[:, :], J), ALU.add).then_inc(b_added, 1)
                pool.wait_ge(b_added, B)

            @block.scalar
            def _(act):
                A = nc.scalar.activation

                def turned_in():
                    A(xT[:, :, :], txp[:, 0:C, :], ACT.Copy).then_inc(xT_ready, 1)

                def outputs(i):
                    act.wait_ge(y_done, i + 1)
                    act.wait_ge(ys_out, i * 16 + 16)
                    A(ysb[:, :], yp[:, 0:D], ACT.Copy).then_inc(y_copied, 1)

                def body(i, first=False, last=False):
                    act.wait_ge(g_done, i * 2 + 1)
                    A(gl[:, :], gp[:, 0, :], ACT.Gelu_apprx_tanh).then_inc(gelu_ready, 1)
                    if not last:
                        act.wait_ge(tx_done, i + 2)
                        turned_in()
                    if not first:
                        outputs(i - 1)
                    act.wait_ge(ht_done, i + 1)
                    A(hidT[:, :, :], htp[:, :, :], ACT.Copy).then_inc(hidT_ready, 1)

                act.sem_inc(y_copied, 1)
                act.wait_ge(tx_done, 1)
                turned_in()
                body(0, first=True)
                with act.Fori(0, NS - 2) as k:
                    body(k + 1)
                body(NS - 1, last=True)
                outputs(NS - 1)

            @block.tensor
            def _(pe):
                M = nc.tensor.matmul

                def turn_in(i):
                    pe.wait_ge(xs_loaded, i * 16 + 16)
                    for c in range(C):
                        mm = nc.tensor.transpose(txp[:, c, :], xt[:, c * P:(c + 1) * P], ident[:, :])
                    mm.then_inc(tx_done, 1)

                def turn_hidden(i):
                    pe.wait_ge(hid_ready, i + 1)
                    pe.wait_ge(hidT_ready, i + 1)
                    for f in range(FT):
                        mm = nc.tensor.transpose(htp[:, f, :], hid[:, f * P:(f + 1) * P], ident[:, :])
                    mm.then_inc(ht_done, 1)

                def gates(i, e):
                    pe.wait_ge(xT_ready, i + 1)
                    for g in range(2):
                        for c in range(C):
                            mm = M(gp[:, g, :], xT[:, c, :], gate[:, c, ds(e, 1), g * HID:(g + 1) * HID].squeeze(1), start=(c == 0), stop=(c == C - 1))
                        mm.then_inc(g_done, 1)

                def outputs(i, e):
                    pe.wait_ge(hidT_ready, i + 2)
                    pe.wait_ge(y_copied, i + 1)
                    for f in range(FT):
                        mm = M(yp[:, 0:D], hidT[:, f, :], lin[:, ds(e, 1), f, :].squeeze(1), start=(f == 0), stop=(f == FT - 1))
                    mm.then_inc(y_done, 1)

                def expert(i):
                    return pe.value_load(tile_expert[0:1, ds(i, 1)], min_val=0, max_val=E - 1)

                pe.wait_ge(G["moe_w_in"], 16 * E * (C + 1))
                turn_in(0)
                pe.sem_inc(hidT_ready, 1)
                gates(0, expert(0))
                turn_in(1)
                with pe.Fori(0, NS - 2) as k:
                    e, e_next = expert(k), expert(k + 1)
                    turn_hidden(k)
                    gates(k + 1, e_next)
                    turn_in(k + 2)
                    outputs(k, e)
                turn_hidden(NS - 2)
                gates(NS - 1, expert(NS - 1))
                outputs(NS - 2, expert(NS - 2))
                turn_hidden(NS - 1)
                outputs(NS - 1, expert(NS - 1))

            @block.vector
            def _(ve):
                V = nc.vector
                st = Steps(ve, cf_step, (d_in, 16))
                link = st.link

                def scan(t):
                    last = z[:, :, ds(t - 1, 1)].squeeze(2)
                    link(V.scalar_tensor_tensor(out=sq[:, :], in0=last, scalar=-1.0, in1=last, op0=ALU.mult, op1=ALU.mult, accum_out=nrm[:, 0:1]))
                    link(V.reciprocal(nrm[:, 1:2], nrm[:, 0:1]))
                    link(V.scalar_tensor_tensor(out=z[:, :, ds(t, 1)].squeeze(2), in0=last, scalar=nrm[:, 1:2], in1=dz[:, :, ds(t, 1)].squeeze(2),
                                                op0=ALU.mult, op1=ALU.add))

                def product(i):
                    ve.wait_ge(gelu_ready, i + 1)
                    ve.wait_ge(g_done, i * 2 + 2)
                    V.tensor_tensor(hid[:, :], gl[:, :], gp[:, 1, :], ALU.mult).then_inc(hid_ready, 1)

                link(V.memset(sgn[:, :, 0:1], 1.0))
                link(V.memset(sgn[:, :, 1:2], -1.0))
                sign = sgn[:, :, :].rearrange("p n s -> p (n s)")
                ve.wait_ge(d_in, 16 * (1 + J))
                link(V.tensor_tensor(dz[:, 1, :], dz[:, 1, :], sign, ALU.mult))
                link(V.tensor_copy(z[:, :, 0], dz[:, :, 0]))
                for t in range(1, AHEAD % SCAN):
                    scan(t)
                with ve.Fori(0, AHEAD // SCAN) as i:
                    st.enter(i, 3 * SCAN)
                    for s in range(SCAN):
                        scan(i * SCAN + (AHEAD % SCAN + s))
                st.leave(AHEAD // SCAN)
                with ve.Fori(0, SCAN_TRIPS) as i:
                    st.enter(i, 3 * SCAN)
                    product(i)
                    for s in range(SCAN):
                        scan(i * SCAN + (AHEAD + s))
                st.leave(SCAN_TRIPS)
                V.tensor_tensor(z[:, 1, :], z[:, 1, :], sign, ALU.mult).then_inc(z_ready, 1)
                with ve.Fori(0, NS - SCAN_TRIPS) as k:
                    product(k + SCAN_TRIPS)
        clear(nc, used)


def phase_attention1(nc, T, G, out):
    B, N, D = T["x"].shape
    E = T["rw"].shape[1]
    C, J = D // P, N // P
    NT = B * J
    HW = T["w_out"].shape[0]
    HP = HW // P
    DH = P // 2
    F = T["w_ff1"].shape[1]
    FT = F // P
    NU = HP * J
    x_all, y_all, ident, anti = G["x_all"], G["y_all"], G["ident"], G["anti"]
    Wqkv, cols, bqk, bf1, bv, wbk, bout, bf2 = (G[n] for n in ("Wqkv", "cols", "bqk", "bf1", "bv", "wbk", "bout", "bf2"))
    mhalf, dcol, ccol, slot1, weight1, decay_mask = (G[n] for n in ("mhalf", "dcol", "ccol", "slot1", "weight1", "decay_mask"))
    with ExitStack() as ctx:
        def sb(name, shape, dt=F32):
            return ctx.enter_context(nc.sbuf_tensor(name, shape, dt))

        def sem(name):
            return ctx.enter_context(nc.semaphore(name))

        Wout = sb("Wout", [P, HP, D])
        Wf1 = sb("Wf1", [P, C, F])
        Wf2 = sb("Wf2", [P, FT, D])
        cbc = sb("cbc", [P, N])
        wd = sb("wd", [P, J, N])
        xh2, xh3 = sb("xh2", [P, J, D]), sb("xh3", [P, J, D])
        xT2, xT3 = sb("xT2", [P, C, N]), sb("xT3", [P, C, N])
        stats5 = sb("stats5", [P, J, 6])
        mv5 = sb("mv5", [P, J, 2])
        rv = sb("rv", [P, 2, J])
        qkT = sb("qkT", [P, 2 * HP, N])
        vt = sb("vt", [P, J, HW])
        pm = sb("pm", [P, 2, 2, N])
        hebT = sb("hebT", [P, HP, N])
        hT = sb("hT5", [P, FT, N])
        gt = sb("gt", [P, 2, J, D])
        ost = sb("ost", [P, J, D])
        fr = sb("fr", [2 * NT, 2, P])
        fb = sb("fb", [P, 2 * NT])
        gf = sb("gf", [P, 8, NT])
        gcol = sb("gcol", [P, 2, NT])
        PA = ctx.enter_context(nc.psum_tensor("PA5", [P, 2, 512], F32))
        PS = ctx.enter_context(nc.psum_tensor("PS5", [P, 4, 512], F32))
        PO = ctx.enter_context(nc.psum_tensor("PO5", [P, 2, 512], F32))

        w_in, c_in, f_in = sem("w5_in"), sem("cbc_in"), sem("f_in")
        f_turned, fb_ready, fb_turned, g_ready = (sem(n) for n in ("f_turned", "fb_ready", "fb_turned", "gcol_ready"))
        diff_ready, wexp_ready, wd_ready = (sem(n) for n in ("diff_ready", "wexp_ready", "wd_ready"))
        var_ready, rs_ready, xh2_ready, xh3_ready = (sem(n) for n in ("var5_ready", "rs5_ready", "xh2_ready", "xh3_ready"))
        t2_done, xT2_ready, t3_done, xT3_ready = (sem(n) for n in ("t2_done", "xT2_ready", "t3_done", "xT3_ready"))
        qk_done, qk_ready, v_done, v_ready = (sem(n) for n in ("qk5_done", "qk5_ready", "v5_done", "v5_ready"))
        s_done, p_ready, av_done, heb_ready = (sem(n) for n in ("s5_done", "p5_ready", "av5_done", "heb_ready"))
        wo_done, x3_ready, bout_added, h_done, h_ready, f_done, moved = (
            sem(n) for n in ("wo5_done", "x3_ready", "bout_added", "h5_done", "h5_ready", "f5_done", "out_ready"))
        res_ready, gathered, moe_added, o_out = (sem(n) for n in ("res_ready", "gathered5", "moe_added", "o_out"))
        v_step, p_step = sem("v5_step"), sem("p5_step")
        NW = 3

        with nc.Block() as block:
            @block.sync
            def _(sp):
                def load_c(b):
                    sp.dma_start(cbc[:, :], T["crow"][ds(b, 1), :].to_broadcast([P, N])).then_inc(c_in, 16)

                for k in range(2):
                    sp.dma_start(fr[:, k, :], T["cf"][k].rearrange("c b (j n) -> (c b j) n", n=P)).then_inc(f_in, 16)
                load_c(0)
                sp.dma_start(Wout[:, :, :], T["w_out"].rearrange("(c p) n -> p c n", p=P)).then_inc(w_in, 16)
                sp.dma_start(Wf1[:, :, :], T["w_ff1"].rearrange("(c p) n -> p c n", p=P)).then_inc(w_in, 16)
                sp.dma_start(Wf2[:, :, :], T["w_ff2"].rearrange("(c p) n -> p c n", p=P)).then_inc(w_in, 16)

                def body(b, last):
                    if not last:
                        sp.wait_ge(diff_ready, b + 1)
                        load_c(b + 1)
                    for j in range(J):
                        sp.wait_ge(moved, b * J + (j + 2))
                        sp.dma_start(out[ds(b, 1), j * P:(j + 1) * P, :].squeeze(0), ost[:, j, :]).then_inc(o_out, 16)
                sp.sem_inc(o_out, 16 * J)
                loop(sp, B, body)
                sp.wait_ge(o_out, 16 * (B * J + J))

            @block.gpsimd
            def _(pool):
                st = Steps(pool, p_step)
                Q = nc.gpsimd

                def gather(b):
                    for j in range(J):
                        for k in range(2):
                            t = b * J + j
                            Q.indirect_dma_start(out=gt[:, k, j, :], out_offset=None, in_=T["ys"],
                                                 in_offset=bass.IndirectOffsetOnAxis(ap=slot1[:, k, t:t + 1], axis=0),
                                                 bounds_check=T["ys"].shape[0] - 1, oob_is_err=False).then_inc(gathered, 16)

                def power(n):
                    pool.wait_ge(var_ready, n + 1)
                    Q.tensor_tensor(rv[:, 1, :], rv[:, 0, :], mhalf[:, 0:J], ALU.pow).then_inc(rs_ready, 1)

                def ahead(b):
                    power(2 * b - 1 if b else 0)
                    for c in range(J):
                        if c == 0:
                            pool.wait_ge(wexp_ready, b + 1)
                        Q.tensor_tensor(wd[:, c, 0:N - c * P], wd[:, c, 0:N - c * P], decay_mask[:, 0:N - c * P], ALU.mult).then_inc(wd_ready, 1)
                    pool.wait_ge(xh2_ready, b + 1)
                    own = y_all[:, b * J:(b + 1) * J, :]
                    Q.tensor_tensor(own, own, mid_dim(bout[:, :], J), ALU.add).then_inc(bout_added, 1)

                gather(0)
                ahead(0)
                for b in range(B):
                    if b + 1 < B:
                        ahead(b + 1)
                    power(2 * b + 2 if b + 1 < B else 2 * b + 1)
                    pool.wait_ge(xh3_ready, b + 1)
                    own = y_all[:, b * J:(b + 1) * J, :]
                    st.link(Q.tensor_tensor(own, own, mid_dim(bf2[:, :], J), ALU.add))
                    Q.tensor_tensor(own, own, x_all[:, b * J:(b + 1) * J, :], ALU.add).then_inc(res_ready, 1)
                    if b + 1 < B:
                        pool.wait_ge(moe_added, b + 1)
                        gather(b + 1)

            @block.scalar
            def _(act):
                A = nc.scalar.activation

                def decays(b):
                    act.wait_ge(diff_ready, b + 1)
                    for c in range(J):
                        last = A(wd[:, c, 0:N - c * P], wd[:, c, 0:N - c * P], ACT.Exp, scale=-1.0)
                    last.then_inc(wexp_ready, 1)

                def project(b):
                    act.wait_ge(t2_done, b + 1)
                    for c in range(C):
                        last = A(xT2[:, c, :], PA[:, c, :], ACT.Identity, scale=cols[:, c, 0:1], bias=cols[:, c, 1:2])
                    last.then_inc(xT2_ready, 1)
                    for m in range(2 * HP):
                        act.wait_ge(qk_done, b * 2 * HP + (m + 1))
                        A(qkT[:, m, :], PS[:, m % 4, :], ACT.Identity, bias=bqk[:, m:m + 1]).then_inc(qk_ready, 1)

                act.wait_ge(f_turned, 1)
                A(fb[:, :], PS[:, 1, 0:2 * NT], ACT.Copy).then_inc(fb_ready, 1)
                decays(0)
                project(0)

                def body(b, last):
                    for hp in range(HP):
                        act.wait_ge(av_done, b * NU + ((hp + 1) * J + 2))
                        A(hebT[:, hp, :], PO[:, hp % 2, :], ACT.Copy).then_inc(heb_ready, 1)
                    if not last:
                        decays(b + 1)
                        project(b + 1)
                    act.wait_ge(t3_done, b + 1)
                    for c in range(C):
                        la = A(xT3[:, c, :], PA[:, c, :], ACT.Identity, scale=cols[:, c, 2:3], bias=cols[:, c, 3:4])
                    la.then_inc(xT3_ready, 1)
                    for f in range(FT):
                        act.wait_ge(h_done, b * FT + (f + 1))
                        A(hT[:, f, :], PS[:, f % 4, :], ACT.Gelu_apprx_tanh, bias=bf1[:, f:f + 1]).then_inc(h_ready, 1)
                loop(act, B, body)

            @block.tensor
            def _(pe):
                M = nc.tensor.matmul

                def turn(xh, done):
                    for c in range(C):
                        for j in range(J):
                            mm = nc.tensor.transpose(PA[:, c, j * P:(j + 1) * P], xh[:, j, c * P:(c + 1) * P], ident[:, :])
                    mm.then_inc(done, 1)

                def project(b):
                    pe.wait_ge(xh2_ready, b + 1)
                    turn(xh2, t2_done)
                    pe.wait_ge(xT2_ready, b + 1)
                    for m in range(2 * HP):
                        if m < 4:
                            if not (isinstance(b, int) and b == 0):
                                pe.wait_ge(x3_ready, (b - 1) * J + (m + 1))
                        else:
                            pe.wait_ge(qk_ready, b * 2 * HP + (m - 3))
                        for c in range(C):
                            mm = M(PS[:, m % 4, :], Wqkv[:, c, m * P:(m + 1) * P], xT2[:, c, :], start=(c == 0), stop=(c == C - 1))
                        mm.then_inc(qk_done, 1)
                    for j in range(J):
                        pe.wait_ge(qk_ready, b * 2 * HP + (2 * HP - J + j + 1))
                        for c in range(C):
                            mm = M(PS[:, j, 0:HW], xT2[:, c, j * P:(j + 1) * P], Wqkv[:, c, 2 * HW:3 * HW], start=(c == 0), stop=(c == C - 1))
                        mm.then_inc(v_done, 1)

                def scores(b, u):
                    hp, c = divmod(u, J)
                    if u == 0:
                        pe.wait_ge(v_ready, b * J + J)
                        pe.wait_ge(moved, b * J + 1)
                    elif u >= 2:
                        pe.wait_ge(p_ready, b * NU + (u - 1))
                    for e in range(2):
                        half = slice(e * DH, (e + 1) * DH)
                        mm = M(PS[:, 2 * (u % 2) + e, 0:N - c * P], qkT[half, HP + hp, c * P:(c + 1) * P], qkT[half, hp, c * P:N],
                               start=True, stop=True)
                    mm.then_inc(s_done, 1)

                def values(b, u):
                    hp, c = divmod(u, J)
                    if c == 0:
                        pe.wait_ge(heb_ready, b * HP + (hp + 1))
                    pe.wait_ge(p_ready, b * NU + (u + 1))
                    for e in range(2):
                        mm = M(PO[e * DH:(e + 1) * DH, hp % 2, c * P:N], vt[:, c, (2 * hp + e) * DH:(2 * hp + e + 1) * DH], pm[:, u % 2, e, 0:N - c * P],
                               start=(c == 0), stop=(c == J - 1))
                    mm.then_inc(av_done, 1)

                pe.wait_ge(f_in, 32)
                nc.tensor.transpose(PS[:, 0, 0:2 * NT], fr[:, 0, :], ident[0:2 * NT, 0:2 * NT])
                nc.tensor.transpose(PS[:, 1, 0:2 * NT], fr[:, 1, :], ident[0:2 * NT, 0:2 * NT]).then_inc(f_turned, 1)
                pe.wait_ge(fb_ready, 1)
                M(PS[:, 2, 0:2 * NT], anti[:, :], fb[:, :], start=True, stop=True).then_inc(fb_turned, 1)
                pe.sem_inc(heb_ready, 2)
                pe.sem_inc(moved, 1)
                pe.sem_inc(av_done, 2)
                project(0)
                pe.wait_ge(w_in, 16 * NW)

                def body(b, last):
                    pe.wait_ge(qk_ready, b * 2 * HP + 2 * HP)
                    pe.wait_ge(v_ready, b * J + J)
                    scores(b, 0)
                    for u in range(NU):
                        if u + 1 < NU:
                            scores(b, u + 1)
                        values(b, u)
                    pe.wait_ge(heb_ready, b * HP + (HP + 2))
                    for j in range(J):
                        for hp in range(HP):
                            mm = M(PS[:, j, 0:D], hebT[:, hp, j * P:(j + 1) * P], Wout[:, hp, :], start=(hp == 0), stop=(hp == HP - 1))
                        mm.then_inc(wo_done, 1)
                    if not last:
                        project(b + 1)
                    pe.wait_ge(xh3_ready, b + 1)
                    turn(xh3, t3_done)
                    pe.wait_ge(xT3_ready, b + 1)
                    for f in range(FT):
                        if f >= 4:
                            pe.wait_ge(h_ready, b * FT + (f - 3))
                        elif not last:
                            pe.wait_ge(v_ready, b * J + (J + f + 1))
                        for c in range(C):
                            mm = M(PS[:, f % 4, :], Wf1[:, c, f * P:(f + 1) * P], xT3[:, c, :], start=(c == 0), stop=(c == C - 1))
                        mm.then_inc(h_done, 1)
                    pe.wait_ge(h_ready, b * FT + FT)
                    for j in range(J):
                        for f in range(FT):
                            mm = M(PS[:, j, 0:D], hT[:, f, j * P:(j + 1) * P], Wf2[:, f, :], start=(f == 0), stop=(f == FT - 1))
                        mm.then_inc(f_done, 1)
                loop(pe, B, body)

            @block.vector
            def _(ve):
                V = nc.vector
                st = Steps(ve, v_step, (fb_turned, 1))
                link = st.link

                def tile(t):
                    return y_all[:, ds(t, 1), :].squeeze(1)

                def norm(b, n, xh, done):
                    for j in range(J):
                        la = V.bn_stats(stats5[:, j, :], tile(b * J + j))
                    link(la, apart=True)
                    for j in range(J):
                        la = V.bn_aggr(mv5[:, j, :], stats5[:, j, :])
                    link(la)
                    V.tensor_scalar(rv[:, 0, :], mv5[:, :, 1], 1e-5, None, ALU.add).then_inc(var_ready, 1)
                    ve.wait_ge(rs_ready, n + 1)
                    for j in range(J):
                        la = V.tensor_scalar(xh[:, j, :], tile(b * J + j), mv5[:, j, 0:1], rv[:, 1, j:j + 1], ALU.subtract, ALU.mult)
                    la.then_inc(done, 1)

                def ahead(b, n):
                    ve.wait_ge(c_in, b * 16 + 16)
                    for c in range(J):
                        la = V.tensor_scalar(wd[:, c, 0:N - c * P], cbc[:, c * P:N], ccol[:, ds(b * J + c, 1)], 0.0, ALU.subtract, ALU.max)
                    la.then_inc(diff_ready, 1)
                    for k in range(2):
                        for j in range(J):
                            la = V.scalar_tensor_tensor(out=tile(b * J + j), in0=wbk[:, k, :], scalar=gcol[:, k, ds(b * J + j, 1)], in1=tile(b * J + j),
                                                        op0=ALU.mult, op1=ALU.add)
                        link(la, apart=True)
                    norm(b, n, xh2, xh2_ready)

                def values_in(b):
                    for j in range(J):
                        ve.wait_ge(v_done, b * J + (j + 1))
                        V.tensor_tensor(vt[:, j, :], PS[:, j, 0:HW], bv[:, :], ALU.add).then_inc(v_ready, 1)

                ve.wait_ge(fb_turned, 1)
                fwd = PS[:, 0, 0:2 * NT].rearrange("p (c b j) -> p c b j", c=2, j=J)
                bwd = PS[:, 2, 0:2 * NT].rearrange("p (c b j) -> p c b j", c=2, j=J)
                link(V.tensor_tensor(gf[:, 0:2, :], PS[:, 0, 0:2 * NT].rearrange("p (c t) -> p c t", c=2), dcol[:, :, :], ALU.subtract))
                for c in range(2):
                    own = gf[:, c, :].rearrange("p (b j) -> p b j", j=J)
                    for j in range(J):
                        la = V.tensor_tensor(own[:, :, j], bwd[:, c, :, J - 1 - j], own[:, :, j], ALU.add)
                link(la)
                link(V.tensor_tensor(gf[:, 2:4, :], gf[:, 0:2, :], gf[:, 0:2, :], ALU.mult))
                link(V.tensor_tensor(gf[:, 4, :], gf[:, 2, :], gf[:, 3, :], ALU.add))
                link(V.reciprocal(gf[:, 5, :], gf[:, 4, :]))
                V.tensor_tensor(gcol[:, 0, :], gf[:, 0, :], gf[:, 5, :], ALU.mult)
                link(V.scalar_tensor_tensor(out=gcol[:, 1, :], in0=gf[:, 1, :], scalar=-1.0, in1=gf[:, 5, :], op0=ALU.mult, op1=ALU.mult))
                ahead(0, 0)
                values_in(0)

                def body(b, last):
                    for u in range(NU):
                        c = u % J
                        n = N - c * P
                        if u == 0:
                            ve.wait_ge(wd_ready, b * J + J)
                        ve.wait_ge(av_done, b * NU + (u + 1))
                        ve.wait_ge(s_done, b * NU + (u + 1))
                        V.tensor_tensor(pm[:, u % 2, :, 0:n], PS[:, 2 * (u % 2):2 * (u % 2) + 2, 0:n], mid_dim(wd[:, c, 0:n], 2), ALU.mult).then_inc(p_ready, 1)
                    if not last:
                        ve.wait_ge(p_ready, b * NU + NU)
                        ahead(b + 1, 2 * b + 1)
                    ve.wait_ge(bout_added, b + 1)
                    for j in range(J):
                        ve.wait_ge(wo_done, b * J + (j + 1))
                        V.tensor_tensor(tile(b * J + j), PS[:, j, 0:D], tile(b * J + j), ALU.add).then_inc(x3_ready, 1)
                    wait_apart(ve, x3_ready, b * J + J, (fb_turned, 1))
                    norm(b, 2 * b + (1 if last else 2), xh3, xh3_ready)
                    if not last:
                        values_in(b + 1)
                    ve.wait_ge(res_ready, b + 1)
                    ve.wait_ge(gathered, b * 16 * 2 * J + 16 * 2 * J)
                    for k in range(2):
                        for j in range(J):
                            la = V.scalar_tensor_tensor(out=tile(b * J + j), in0=gt[:, k, j, :], scalar=weight1[:, k, ds(b * J + j, 1)], in1=tile(b * J + j),
                                                        op0=ALU.mult, op1=ALU.add)
                        if k == 1:
                            la.then_inc(moe_added, 1)
                            ve.wait_ge(moe_added, b + 1)
                        else:
                            link(la, apart=True)
                    for j in range(J):
                        if j == 0:
                            ve.wait_ge(o_out, b * 16 * J + 16 * J)
                        ve.wait_ge(f_done, b * J + (j + 1))
                        V.tensor_tensor(ost[:, j, :], PS[:, j, 0:D], tile(b * J + j), ALU.add).then_inc(moved, 1)
                loop(ve, B, body, st, 7)


_NAMES = {"x": "L0_attn_x", "Wq": "L0_attn_Wq", "Wk": "L0_attn_Wk", "Wv": "L0_attn_Wv", "Wo": "L0_attn_Wo",
          "splat": "L0_attn_splat_positions", "sscale": "L0_attn_splat_scales", "simp": "L0_attn_splat_importance",
          "We": "L0_attn_We", "be": "L0_attn_be", "Wt": "L0_attn_Wt", "Wd": "L0_attn_Wd",
          "bd": "L0_attn_bd", "Wg": "L0_attn_Wg", "bg": "L0_attn_bg", "Wr": "L0_ffn_Wr", "W1": "L0_ffn_W1",
          "W2": "L0_ffn_W2", "ln1_g": "L1_attn_ln1_g", "ln1_b": "L1_attn_ln1_b", "ln2_g": "L1_attn_ln2_g",
          "ln2_b": "L1_attn_ln2_b", "ln3_g": "L1_attn_ln3_g", "ln3_b": "L1_attn_ln3_b", "w_pot": "L1_attn_w_pot",
          "b_pot": "L1_attn_b_pot", "w_bk": "L1_attn_w_bk", "b_bk": "L1_attn_b_bk", "w_qkv": "L1_attn_w_qkv",
          "b_qkv": "L1_attn_b_qkv", "w_out": "L1_attn_w_out", "b_out": "L1_attn_b_out", "w_ff1": "L1_attn_w_ff1",
          "b_ff1": "L1_attn_b_ff1", "w_ff2": "L1_attn_w_ff2", "b_ff2": "L1_attn_b_ff2",
          "rscale": "L1_ffn_router_scale", "rw": "L1_ffn_router_w", "lin": "L1_ffn_linear_w",
          "pscale": "L1_ffn_per_expert_scale"}


def kernel(**inputs):
    import numpy as _np
    import concourse.bacc as _bacc
    from concourse import mybir as _mybir
    from concourse.bass_utils import run_bass_kernel_spmd as _run

    nc = _bacc.Bacc("TRN2", target_bir_lowering=False, num_devices=1)
    laid = {short: _np.asarray(inputs[name]) for short, name in _NAMES.items()}
    laid["btT"] = _np.asarray(inputs["L0_attn_bt"]).T
    laid["gate"] = _np.asarray(inputs["L1_ffn_gating_w"]).transpose(0, 3, 1, 2)
    arrays, T = {}, {}
    for short, a in laid.items():
        a = _np.ascontiguousarray(a)
        arrays[f"in_{short}"] = a
        T[short] = nc.dram_tensor(f"in_{short}", a.shape, _mybir.dt.from_np(a.dtype), kind="ExternalInput").ap()
    shape = laid["x"].shape
    tokens, width = shape[0] * shape[1], shape[2]
    experts = laid["rw"].shape[1]
    rows2 = 2 * tokens + experts * P
    for name, rows in (("xe", tokens), ("ye", tokens), ("xs", rows2), ("ys", rows2)):
        T[name] = nc.dram_tensor(f"scratch_{name}", (rows, width), F32, kind="Internal").ap()
    T["xnT"] = nc.dram_tensor("scratch_xnT", (shape[0], P, width // P, shape[1]), F32, kind="Internal").ap()
    T["inflT"] = nc.dram_tensor("scratch_inflT", (shape[0], laid["splat"].shape[0], shape[1]), F32, kind="Internal").ap()
    T["dec"] = nc.dram_tensor("scratch_dec", (shape[0], laid["splat"].shape[0], width), F32, kind="Internal").ap()
    T["parts"] = nc.dram_tensor("scratch_parts", (2, 3, width, shape[1]), BF16, kind="Internal").ap()
    T["drow"] = nc.dram_tensor("scratch_drow", (2, 2, shape[0], shape[1]), F32, kind="Internal").ap()
    T["crow"] = nc.dram_tensor("scratch_crow", (shape[0], shape[1]), F32, kind="Internal").ap()
    T["cf"] = nc.dram_tensor("scratch_cf", (2, 2, shape[0], shape[1]), F32, kind="Internal").ap()
    out = nc.dram_tensor("out_dram", shape, F32, kind="ExternalOutput").ap()
    build_program(nc, T, out)
    r = _run(nc, [arrays], core_ids=[0])
    return r.results[0]["out_dram"]
```

```python
from contextlib import ExitStack

import concourse.bass as bass
from concourse import mybir

F32 = mybir.dt.float32
F32R = mybir.dt.float32r
BF16 = mybir.dt.bfloat16
I32 = mybir.dt.int32
ALU = mybir.AluOpType
ACT = mybir.ActivationFunctionType
AX = mybir.AxisListType
ds = bass.ds

P = 128
ZROW = 2304


class Steps:

    def __init__(self, eng, sem, settled=None):
        self.eng, self.sem, self.total, self.i, self.per, self.k = eng, sem, 0, None, 0, 0
        self.settled = settled

    def enter(self, i, per):
        self.i, self.per, self.k = i, per, 0

    def leave(self, trips):
        assert self.k == self.per, f"steps in the loop: {self.k}, said {self.per}"
        self.total += trips * self.per
        self.i = None

    def link(self, instruction, apart=False):
        instruction.then_inc(self.sem, 1)
        if self.i is None:
            self.total += 1
            self.eng.wait_ge(self.sem, self.total)
        else:
            self.k += 1
            value = self.i * self.per + (self.total + self.k)
            if apart:
                wait_apart(self.eng, self.sem, value, self.settled)
            else:
                self.eng.wait_ge(self.sem, value)


def wait_apart(eng, sem, value, settled):
    if not isinstance(value, int):
        eng.lower_val(value)
        eng.wait_ge(*settled)
    eng.wait_ge(sem, value)


def last_dim(ap, n):
    return ap.unsqueeze(2).to_broadcast([ap.shape[0], ap.shape[1], n])


def mid_dim(ap, n):
    return ap.unsqueeze(1).to_broadcast([ap.shape[0], n, ap.shape[1]])


def row_of(vector, n):
    return vector.unsqueeze(0).to_broadcast([n, vector.shape[0]])


def column(vector):
    return vector.rearrange("(s a) -> s a", a=1)


def loop(eng, trips, body, steps=None, per=0):
    with eng.Fori(0, trips - 1) as i:
        if steps:
            steps.enter(i, per)
        body(i, False)
    if steps:
        steps.leave(trips - 1)
    body(trips - 1, True)


def clear(nc, semaphores):
    with nc.Block() as block:
        @block.sync
        def _(sp):
            for s in semaphores:
                sp.sem_clear(s)


def build_program(nc, T, out):
    ctx = ExitStack()
    with ctx:
        B, N, D = T["x"].shape
        NT = B * N // P
        G = {"nc": nc}

        def sb(name, shape, dt=F32, into=ctx):
            G[name] = into.enter_context(nc.sbuf_tensor(name, shape, dt))

        def sem(name):
            G[name] = ctx.enter_context(nc.semaphore(name))

        sb("x_all", [P, NT, D])
        sb("ident", [P, P])
        sb("ones", [P, P])
        sb("mhalf", [P, NT])
        sb("strict", [P, P])
        sb("slot0", [P, NT], I32)
        sb("take0", [P, NT], I32)
        sb("pkeep0", [P, NT])
        sem("dram_zeroed")
        sem("scattered0")
        phase_norm_route0(nc, T, G)
        phase_attention0_experts0(nc, T, G)
        E1, HID = T["lin"].shape[0], T["lin"].shape[1]
        sb("y_all", [P, NT, D])
        sb("dcol", [P, 2, NT])
        sb("ccol", [P, NT])
        sb("slot1", [P, 2, NT], I32)
        sb("weight1", [P, 2, NT])
        sb("tile_expert", [1, T["xs"].shape[0] // P], I32)
        sb("anti", [P, P])
        sb("decay_mask", [P, N])
        sem("moe_w_in")
        HW, F1 = T["w_out"].shape[0], T["w_ff1"].shape[1]
        sb("Wqkv", [P, D // P, 3 * HW])
        sb("cols", [P, D // P, 4])
        sb("bqk", [P, 2 * HW // P])
        sb("bf1", [P, F1 // P])
        sb("bv", [P, HW])
        sb("wbk", [P, 2, D])
        sb("bout", [P, D])
        sb("bf2", [P, D])
        with ExitStack() as weights:
            sb("gate", [P, D // P, E1, 2 * HID], into=weights)
            sb("lin", [P, E1, HID // P, D], into=weights)
            phase_middle(nc, T, G)
            phase_experts1_scan(nc, T, G)
        phase_attention1(nc, T, G, out)


def phase_norm_route0(nc, T, G):
    B, N, D = T["x"].shape
    S = T["splat"].shape[0]
    E = T["Wr"].shape[1]
    C, J = D // P, N // P
    NT = B * J
    CAP = B * N // E
    x_all, ident, ones, strict = G["x_all"], G["ident"], G["ones"], G["strict"]
    slot0, take0, pkeep0 = G["slot0"], G["take0"], G["pkeep0"]
    mhalf = G["mhalf"]
    dram_zeroed, scattered0 = G["dram_zeroed"], G["scattered0"]
    with ExitStack() as ctx:
        used = []

        def sb(name, shape, dt=F32):
            return ctx.enter_context(nc.sbuf_tensor(name, shape, dt))

        def psum(name, shape):
            return ctx.enter_context(nc.psum_tensor(name, shape, F32))

        def sem(name):
            used.append(ctx.enter_context(nc.semaphore(name)))
            return used[-1]

        Wr = sb("Wr", [P, C, E])
        We = sb("We", [P, C, P])
        Wd = sb("Wd", [P, D])
        Wt = sb("Wt", [P, S, P])
        splat = sb("splat", [S, D])
        splT = sb("splT", [P, C, S])
        svec = sb("svec", [S, 8])
        be = sb("be", [P, 1])
        btT = sb("btT", [P, S])
        bdb = sb("bdb", [S, D])
        zeros = sb("zeros", [P, ZROW])
        xn = sb("xn", [P, J, D])
        xn_all = sb("xn_all", [P, NT, D])
        stats = sb("stats", [P, J, 6])
        mv = sb("mv", [P, J, 2])
        rstd = sb("rstd", [P, J])
        xnTc = sb("xnTc", [P, C, N])
        sqT = sb("sqT", [P, C, N])
        lg = sb("lg", [P, NT, E])
        d2 = sb("d2", [S, N])
        ex = sb("ex", [S, N])
        infl = sb("infl", [S, N])
        dec = sb("dec", [S, B, D])
        tot = sb("tot", [S, 3])
        gathered = sb("gathered0", [S, B, D])
        inN = sb("inN", [P, J, S])
        gT = sb("gT", [P, C, B, S])
        encT = sb("encT", [P, S, B])
        trT = sb("trT", [P, S, B])
        ra = sb("ra", [P, NT, E])
        rb = sb("rb", [P, NT, E])
        oh = sb("oh", [P, NT, E])
        r1 = sb("r1", [P, NT])
        r2 = sb("r2", [P, NT])
        ptok = sb("ptok", [P, NT])
        wgt = sb("wgt", [P, E])
        eno = sb("eno", [P, E])
        tp = psum("tp", [P, C, N])
        lgp = psum("lgp", [P, 512])
        d2p = psum("d2p", [P, N])
        inp = psum("inp", [P, 512])
        gap = psum("gap", [P, 512])
        enp = psum("enp", [P, 512])
        dcp = psum("dcp", [P, 512])
        lgv = lgp[:, 0:J * E].rearrange("p (j e) -> p j e", e=E)
        inv = inp[:, 0:J * S].rearrange("p (j s) -> p j s", s=S)
        gav = gap[0:S, 0:D]

        x_first, x_loaded, w_loaded, wt_loaded = sem("x_first"), sem("x_loaded"), sem("w_loaded"), sem("wt_loaded")
        consts, z_ready = sem("consts"), sem("z_ready")
        var_ready, rstd_ready = sem("var_ready"), sem("rstd_ready")
        xn_ready, xn_copied = sem("xn_ready"), sem("xn_copied")
        tp_ready, xnTc_ready, sq_ready, xnT_out = sem("tp_ready"), sem("xnTc_ready"), sem("sq_ready"), sem("xnT_out")
        infl_out, dec_out = sem("infl_out"), sem("dec_out")
        lg_done, lg_copied = sem("lg_done"), sem("lg_copied")
        d2_done, d2_ready, ex_ready = sem("d2_done"), sem("d2_ready"), sem("ex_ready")
        infl_ready, in_turned, inN_ready = sem("infl_ready"), sem("in_turned"), sem("inN_ready")
        gath_done, gath_taken, g_turned, gT_ready, enc_done, enc_ready = sem("gath_done"), sem("gath_taken"), sem("g_turned"), sem("gT_ready"), sem("enc_done"), sem("enc_ready")
        tr_done, tr_ready, dec_done, dec_copied = sem("tr_done"), sem("tr_ready"), sem("dec_done"), sem("dec_copied")
        r_sub, r_exp, oh_ready, rank_done, slots_ready = sem("r_sub"), sem("r_exp"), sem("oh_ready"), sem("rank_done"), sem("slots_ready")
        spl_turned, spl_ready = sem("spl_turned"), sem("spl_ready")
        v_step, p_step = sem("v_step"), sem("p_step")
        NW = 9

        with nc.Block() as block:
            @block.sync
            def _(sp):
                def load(b, loaded):
                    sp.dma_start(x_all[:, ds(b * J, J), :],
                                 T["x"].rearrange("b (j p) d -> p (b j) d", p=P)[:, ds(b * J, J), :]).then_inc(loaded, 16)

                load(0, x_first)
                sp.dma_start(splat[:, :], T["splat"]).then_inc(w_loaded, 16)
                sp.dma_start(svec[:, 0:1], column(T["sscale"])).then_inc(w_loaded, 16)
                sp.dma_start(svec[:, 1:2], column(T["simp"])).then_inc(w_loaded, 16)
                sp.dma_start(Wr[:, :, :], T["Wr"].rearrange("(c p) e -> p c e", p=P)).then_inc(w_loaded, 16)
                sp.dma_start(We[:, :, :], T["We"].rearrange("(c p) e -> p c e", p=P)).then_inc(w_loaded, 16)
                sp.dma_start(Wd[:, :], T["Wd"]).then_inc(w_loaded, 16)
                sp.dma_start(be[:, :], column(T["be"])).then_inc(w_loaded, 16)
                sp.dma_start(btT[:, :], T["btT"]).then_inc(w_loaded, 16)
                sp.dma_start(bdb[:, :], row_of(T["bd"], S)).then_inc(w_loaded, 16)
                with sp.Fori(1, B) as b:
                    load(b, x_loaded)
                sp.sem_inc(xnT_out, 16)
                sp.sem_inc(infl_out, 16)
                sp.wait_ge(z_ready, 1)
                with sp.Fori(0, B) as b:
                    sp.wait_ge(xnTc_ready, b + 2)
                    sp.dma_start(T["xnT"][ds(b, 1), :, :, :].squeeze(0), xnTc[:, :, :]).then_inc(xnT_out, 16)
                    sp.wait_ge(infl_ready, b + 1)
                    sp.dma_start(T["inflT"][ds(b, 1), :, :].squeeze(0), infl[:, :]).then_inc(infl_out, 16)
                    sp.dma_start(Wt[:, ds(b * (S // B), S // B), :],
                                 T["Wt"].rearrange("s d e -> d s e")[:, ds(b * (S // B), S // B), :]).then_inc(wt_loaded, 16)
                    for name in ("xe", "xs"):
                        rows = T[name].shape[0] // B
                        sp.dma_start(T[name][ds(b * rows, rows), :].rearrange("(p r) d -> p (r d)", p=P),
                                     zeros[:, 0:rows // P * D]).then_inc(dram_zeroed, 16)
                sp.wait_ge(dec_copied, B)
                sp.dma_start(T["dec"].rearrange("b s d -> s b d"), dec[:, :, :]).then_inc(dec_out, 16)
                sp.wait_ge(xnT_out, 16 * (B + 1))
                sp.wait_ge(infl_out, 16 * (B + 1))
                sp.wait_ge(dec_out, 16)

            @block.gpsimd
            def _(pool):
                st = Steps(pool, p_step)
                st.link(nc.gpsimd.memset(ident[:, :], 0.0))
                st.link(nc.gpsimd.memset(strict[:, :], 0.0))
                st.link(nc.gpsimd.memset(mhalf[:, :], -0.5))
                nc.gpsimd.affine_select(out=ident[:, :], in_=ident[:, :], compare_op=ALU.not_equal, fill=1.0,
                                        base=0, pattern=[[-1, P]], channel_multiplier=1).then_inc(consts, 1)
                nc.gpsimd.affine_select(out=strict[:, :], in_=strict[:, :], compare_op=ALU.is_ge, fill=1.0,
                                        base=0, pattern=[[-1, P]], channel_multiplier=1).then_inc(consts, 1)
                nc.gpsimd.iota(wgt[:, :], pattern=[[-1, E]], base=E, channel_multiplier=0,
                               allow_small_or_imprecise_dtypes=True).then_inc(consts, 1)
                nc.gpsimd.iota(eno[:, :], pattern=[[1, E]], base=0, channel_multiplier=0,
                               allow_small_or_imprecise_dtypes=True).then_inc(consts, 1)
                nc.gpsimd.memset(zeros[:, :], 0.0).then_inc(z_ready, 1)
                with pool.Fori(0, B) as b:
                    pool.wait_ge(var_ready, b + 1)
                    nc.gpsimd.tensor_tensor(rstd[:, :], rstd[:, :], mhalf[:, 0:J], ALU.pow).then_inc(rstd_ready, 1)
                pool.wait_ge(xn_copied, B + 1)
                pool.wait_ge(slots_ready, 1)
                pool.wait_ge(dram_zeroed, 16 * 2 * B)
                for t in range(NT):
                    nc.gpsimd.indirect_dma_start(
                        out=T["xe"], out_offset=bass.IndirectOffsetOnAxis(ap=slot0[:, t:t + 1], axis=0),
                        in_=xn_all[:, t, :], in_offset=None, bounds_check=B * N - 1, oob_is_err=False,
                    ).then_inc(scattered0, 16)
                pool.wait_ge(scattered0, 16 * NT)

            @block.scalar
            def _(act):
                act.wait_ge(spl_turned, 1)
                nc.scalar.activation(splT[:, :, :], tp[:, :, 0:S], ACT.Copy, scale=-2.0).then_inc(spl_ready, 1)
                act.sem_inc(xnTc_ready, 1)
                act.sem_inc(xn_copied, 1)

                def ahead(b):
                    act.wait_ge(tp_ready, b + 2)
                    act.wait_ge(d2_done, b + 1)
                    act.wait_ge(xnT_out, b * 16 + 16)
                    nc.scalar.activation(xnTc[:, :, :], tp[:, :, :], ACT.Copy).then_inc(xnTc_ready, 1)

                def squares(b):
                    nc.scalar.activation(sqT[:, :, :], tp[:, :, :], ACT.Square).then_inc(sq_ready, 1)

                def kept(b):
                    nc.scalar.activation(xn_all[:, ds(b * J, J), :], xn[:, :, :], ACT.Copy).then_inc(xn_copied, 1)

                def body(b, last):
                    if not last:
                        ahead(b + 1)
                    act.wait_ge(d2_ready, b + 1)
                    nc.scalar.activation(ex[:, :], d2[:, :], ACT.Exp, scale=svec[:, 4:5]).then_inc(ex_ready, 1)
                    if not last:
                        squares(b + 1)
                    act.wait_ge(in_turned, b + 2)
                    nc.scalar.activation(inN[:, :, :], inv, ACT.Copy).then_inc(inN_ready, 1)
                    if not last:
                        kept(b + 1)
                ahead(0)
                squares(0)
                kept(0)
                loop(act, B, body)
                act.wait_ge(g_turned, 1)
                nc.scalar.activation(gT[:, :, :, :].rearrange("p c b s -> p c (b s)"), tp[:, :, :], ACT.Copy).then_inc(gT_ready, 1)
                act.wait_ge(r_sub, 1)
                nc.scalar.activation(rb[:, :, :], ra[:, :, :], ACT.Exp).then_inc(r_exp, 1)

            @block.tensor
            def _(pe):
                pe.wait_ge(consts, 4)
                pe.wait_ge(w_loaded, 16 * NW)
                for c in range(C):
                    last = nc.tensor.transpose(tp[:, c, 0:S], splat[:, c * P:(c + 1) * P], ident[0:S, 0:S])
                last.then_inc(spl_turned, 1)
                pe.wait_ge(spl_ready, 1)
                pe.sem_inc(d2_done, 1)
                pe.sem_inc(tp_ready, 1)
                pe.sem_inc(in_turned, 1)

                def turn(b):
                    pe.wait_ge(xn_ready, b + 1)
                    if not (isinstance(b, int) and b == 0):
                        pe.wait_ge(sq_ready, b)
                    for j in range(J):
                        for c in range(C):
                            mm = nc.tensor.transpose(tp[:, c, j * P:(j + 1) * P], xn[:, j, c * P:(c + 1) * P], ident[:, :])
                    mm.then_inc(tp_ready, 1)

                def logits(b):
                    pe.wait_ge(xnTc_ready, b + 2)
                    pe.wait_ge(lg_copied, b + 1)
                    for j in range(J):
                        for c in range(C):
                            mm = nc.tensor.matmul(lgv[:, j, :], xnTc[:, c, j * P:(j + 1) * P], Wr[:, c, :],
                                                  start=(c == 0), stop=(c == C - 1))
                    mm.then_inc(lg_done, 1)

                def distances(b):
                    pe.wait_ge(sq_ready, b + 1)
                    if not (isinstance(b, int) and b == 0):
                        pe.wait_ge(d2_ready, b)
                    for c in range(C):
                        nc.tensor.matmul(d2p[0:S, :], ones[:, 0:S], sqT[:, c, :], start=(c == 0), stop=False)
                        mm = nc.tensor.matmul(d2p[0:S, :], splT[:, c, :], xnTc[:, c, :], start=False, stop=(c == C - 1))
                    mm.then_inc(d2_done, 1)

                turn(0)
                logits(0)
                distances(0)

                def body(b, last):
                    if not last:
                        turn(b + 1)
                        logits(b + 1)
                    wait_apart(pe, infl_ready, b + 1, (consts, 4))
                    for j in range(J):
                        mm = nc.tensor.transpose(inv[:, j, :], infl[:, j * P:(j + 1) * P], ident[0:S, 0:S])
                    mm.then_inc(in_turned, 1)
                    pe.wait_ge(inN_ready, b + 1)
                    pe.wait_ge(xn_copied, b + 2)
                    pe.wait_ge(gath_taken, b + 1)
                    for j in range(J):
                        mm = nc.tensor.matmul(gav, inN[:, j, :], xn_all[:, ds(b * J + j, 1), :].squeeze(1), start=(j == 0), stop=(j == J - 1))
                    mm.then_inc(gath_done, 1)
                    if not last:
                        distances(b + 1)
                loop(pe, B, body)
                pe.wait_ge(gath_taken, B + 1)
                for c in range(C):
                    for b in range(B):
                        mm = nc.tensor.transpose(tp[:, c, b * S:(b + 1) * S], gathered[:, b, c * P:(c + 1) * P], ident[0:S, 0:S])
                mm.then_inc(g_turned, 1)
                pe.wait_ge(gT_ready, 1)
                for c in range(C):
                    last = nc.tensor.matmul(enp[:, 0:B * S], We[:, c, :], gT[:, c, :, :].rearrange("p b s -> p (b s)"), start=(c == 0), stop=(c == C - 1))
                last.then_inc(enc_done, 1)
                pe.wait_ge(oh_ready, 1)
                ohf = oh[:, :, :].rearrange("p t e -> p (t e)")
                nc.tensor.matmul(tp[:, 0, 0:NT * E], strict[:, :], ohf, start=True, stop=True)
                nc.tensor.matmul(tp[:, 1, 0:NT * E], ones[:, :], ohf, start=True, stop=True).then_inc(rank_done, 1)
                pe.wait_ge(enc_ready, 1)
                pe.wait_ge(wt_loaded, 16 * B)
                for s in range(S):
                    last = nc.tensor.matmul(d2p[:, s * B:(s + 1) * B], Wt[:, s, :], encT[:, s, :], start=True, stop=True)
                last.then_inc(tr_done, 1)
                pe.wait_ge(tr_ready, 1)
                for b in range(B):
                    if b:
                        pe.wait_ge(dec_copied, b)
                    nc.tensor.matmul(dcp[0:S, 0:D], trT[:, :, b], Wd[:, :], start=True, stop=True).then_inc(dec_done, 1)

            @block.vector
            def _(ve):
                st = Steps(ve, v_step, (consts, 4))
                link = st.link
                V = nc.vector
                link(V.memset(ones[:, :], 1.0))

                def moments(b):
                    if isinstance(b, int) and b == 0:
                        ve.wait_ge(x_first, 16)
                    else:
                        ve.wait_ge(x_loaded, 16 * (B - 1))
                    for j in range(J):
                        la = V.bn_stats(stats[:, j, :], x_all[:, b * J + j, :])
                    link(la, apart=True)
                    for j in range(J):
                        la = V.bn_aggr(mv[:, j, :], stats[:, j, :])
                    link(la)
                    V.tensor_scalar(rstd[:, :], mv[:, :, 1], 1e-5, None, ALU.add).then_inc(var_ready, 1)

                def normed(b):
                    ve.wait_ge(rstd_ready, b + 1)
                    ve.wait_ge(xn_copied, b + 1)
                    for j in range(J):
                        la = V.tensor_scalar(xn[:, j, :], x_all[:, b * J + j, :], mv[:, j, 0:1], rstd[:, j:j + 1],
                                             ALU.subtract, ALU.mult)
                    la.then_inc(xn_ready, 1)

                def logits(b):
                    ve.wait_ge(lg_done, b + 1)
                    V.tensor_copy(lg[:, ds(b * J, J), :], lgv).then_inc(lg_copied, 1)

                moments(0)
                normed(0)
                ve.wait_ge(consts, 4)
                ve.wait_ge(w_loaded, 16 * NW)
                link(V.tensor_scalar(svec[:, 7:8], svec[:, 1:2], -1.0, None, ALU.mult))
                link(V.tensor_tensor(svec[:, 2:3], svec[:, 1:2], svec[:, 7:8], ALU.max))
                link(V.tensor_tensor(d2[:, 0:D], splat[:, :], splat[:, :], ALU.mult))
                link(V.tensor_reduce(svec[:, 3:4], d2[:, 0:D], AX.X, ALU.add))
                link(V.tensor_scalar(svec[:, 7:8], svec[:, 0:1], -1.0, 1e-6, ALU.mult, ALU.max))
                link(V.tensor_tensor(svec[:, 5:6], svec[:, 0:1], svec[:, 7:8], ALU.max))
                link(V.tensor_tensor(svec[:, 6:7], svec[:, 5:6], svec[:, 5:6], ALU.mult))
                link(V.reciprocal(svec[:, 7:8], svec[:, 6:7]))
                link(V.tensor_scalar(svec[:, 4:5], svec[:, 7:8], -0.5, None, ALU.mult))
                for s in (lg_copied, gath_taken):
                    ve.sem_inc(s, 1)

                logits(0)

                def body(b, last):
                    if not last:
                        moments(b + 1)
                        normed(b + 1)
                    ve.wait_ge(d2_done, b + 2)
                    V.tensor_scalar(d2[:, :], d2p[0:S, :], svec[:, 3:4], 0.0, ALU.add, ALU.max).then_inc(d2_ready, 1)
                    ve.wait_ge(ex_ready, b + 1)
                    ve.wait_ge(in_turned, b + 1)
                    ve.wait_ge(infl_out, b * 16 + 16)
                    V.tensor_scalar(infl[:, :], ex[:, :], svec[:, 2:3], None, ALU.mult).then_inc(infl_ready, 1)
                    ve.wait_ge(infl_ready, b + 1)
                    link(V.tensor_reduce(tot[:, 0:1], infl[:, :], AX.X, ALU.add))
                    link(V.tensor_scalar(tot[:, 1:2], tot[:, 0:1], 1e-8, None, ALU.max))
                    link(V.reciprocal(tot[:, 2:3], tot[:, 1:2]))
                    if not last:
                        logits(b + 1)
                    ve.wait_ge(gath_done, b + 1)
                    V.tensor_scalar(gathered[:, ds(b, 1), :].squeeze(1), gav, tot[:, 2:3], None, ALU.mult).then_inc(gath_taken, 1)
                loop(ve, B, body, st, 5)
                ve.wait_ge(lg_copied, B + 1)
                link(V.tensor_reduce(r1[:, :], lg[:, :, :], AX.X, ALU.max))
                V.tensor_tensor(ra[:, :, :], lg[:, :, :], last_dim(r1[:, :], E), ALU.subtract).then_inc(r_sub, 1)
                ve.wait_ge(r_exp, 1)
                link(V.tensor_reduce(r1[:, :], rb[:, :, :], AX.X, ALU.add))
                link(V.reciprocal(r2[:, :], r1[:, :]))
                link(V.tensor_tensor(ra[:, :, :], rb[:, :, :], last_dim(r2[:, :], E), ALU.mult))
                link(V.tensor_reduce(ptok[:, :], ra[:, :, :], AX.X, ALU.max))
                link(V.tensor_tensor(rb[:, :, :], ra[:, :, :], last_dim(ptok[:, :], E), ALU.is_equal))
                link(V.tensor_tensor(ra[:, :, :], rb[:, :, :], mid_dim(wgt[:, :], NT), ALU.mult))
                link(V.tensor_reduce(r1[:, :], ra[:, :, :], AX.X, ALU.max))
                V.tensor_tensor(oh[:, :, :], ra[:, :, :], last_dim(r1[:, :], E), ALU.is_equal).then_inc(oh_ready, 1)
                ve.wait_ge(oh_ready, 1)
                ve.wait_ge(rank_done, 1)
                before = tp[:, 0, 0:NT * E].rearrange("p (t e) -> p t e", e=E)
                count = tp[:, 1, 0:NT * E].rearrange("p (t e) -> p t e", e=E)
                link(V.tensor_copy(ra[:, :, :], count))
                a, z, k = ra, rb, 1
                while k < NT:
                    link(V.tensor_copy(z[:, 0:k, :], a[:, 0:k, :]))
                    link(V.tensor_tensor(z[:, k:NT, :], a[:, k:NT, :], a[:, 0:NT - k, :], ALU.add))
                    a, z, k = z, a, 2 * k
                link(V.tensor_tensor(z[:, :, :], a[:, :, :], count, ALU.subtract))
                link(V.tensor_tensor(a[:, :, :], z[:, :, :], before, ALU.add))
                link(V.tensor_tensor(z[:, :, :], a[:, :, :], oh[:, :, :], ALU.mult))
                link(V.tensor_reduce(r1[:, :], z[:, :, :], AX.X, ALU.add))
                link(V.tensor_tensor(z[:, :, :], oh[:, :, :], mid_dim(eno[:, :], NT), ALU.mult))
                link(V.tensor_reduce(r2[:, :], z[:, :, :], AX.X, ALU.add))
                link(V.tensor_scalar(ra[:, :, 0], r1[:, :], float(CAP), None, ALU.is_ge))
                link(V.scalar_tensor_tensor(out=ra[:, :, 1], in0=r2[:, :], scalar=float(CAP), in1=r1[:, :],
                                            op0=ALU.mult, op1=ALU.add))
                link(V.scalar_tensor_tensor(out=ra[:, :, 2], in0=ra[:, :, 0], scalar=2.0 * B * N, in1=ra[:, :, 1],
                                            op0=ALU.mult, op1=ALU.add))
                link(V.tensor_scalar(ra[:, :, 3], ra[:, :, 1], float(B * N - 1), None, ALU.min))
                link(V.tensor_copy(take0[:, :], ra[:, :, 3]))
                link(V.tensor_scalar(ra[:, :, 4], ra[:, :, 0], -1.0, 1.0, ALU.mult, ALU.add))
                link(V.tensor_tensor(pkeep0[:, :], ra[:, :, 4], ptok[:, :], ALU.mult))
                V.tensor_copy(slot0[:, :], ra[:, :, 2]).then_inc(slots_ready, 1)
                ve.wait_ge(enc_done, 1)
                V.tensor_scalar(encT[:, :, :].rearrange("p s b -> p b s"), enp[:, 0:B * S].rearrange("p (b s) -> p b s", s=S),
                                be[:, 0:1], 0.0, ALU.add, ALU.max).then_inc(enc_ready, 1)
                ve.wait_ge(tr_done, 1)
                V.tensor_tensor(trT[:, :, :], d2p[:, :].rearrange("p (s b) -> p s b", b=B), last_dim(btT[:, :], B),
                                ALU.add).then_inc(tr_ready, 1)
                for b in range(B):
                    ve.wait_ge(dec_done, b + 1)
                    V.tensor_tensor(dec[:, b, :], dcp[0:S, 0:D], bdb[:, :], ALU.add).then_inc(dec_copied, 1)
        clear(nc, used)


def phase_attention0_experts0(nc, T, G):
    B, N, D = T["x"].shape
    H = 16
    DH = D // H
    S = T["splat"].shape[0]
    C, J = D // P, N // P
    F = T["W1"].shape[2]
    FT = F // P
    CAP = B * N // T["W1"].shape[0]
    assert CAP == N
    QH = 4
    NG = H // QH
    R = 6 * DH
    PAIRS = ((0, 0), (0, 1), (0, 2), (1, 0), (1, 1), (2, 0))
    x_all, ident, take0, pkeep0 = G["x_all"], G["ident"], G["take0"], G["pkeep0"]
    with ExitStack() as ctx:
        used = []

        def sb(name, shape, dt=F32):
            return ctx.enter_context(nc.sbuf_tensor(name, shape, dt))

        def sem(name):
            used.append(ctx.enter_context(nc.semaphore(name)))
            return used[-1]

        Wq, Wk, Wv, Wo, Wg = (sb(n, [P, C, D]) for n in ("Wq", "Wk", "Wv", "Wo", "Wg"))
        W1 = sb("W1", [P, C, F])
        W2 = sb("W2", [P, FT, D])
        nbg = sb("nbg", [P, C])
        xe = sb("xe", [P, J, D])
        xeT = sb("xeT", [P, C, N])
        hT = sb("hT", [P, FT, N])
        ysb = sb("ysb", [P, J, D])
        xnTb = sb("xnTb", [P, C, N])
        inflb = sb("inflb", [S, N])
        decb = sb("decb", [S, D])
        rest = sb("rest", [P, 2, C, N])
        parts = sb("parts", [P, 2, 3, C, N], BF16)
        Qs = sb("Qs", [R + 3, H, N], BF16)
        Ks = sb("Ks", [R + 3, H, N], BF16)
        V = sb("V", [P, J, H, 32])
        nm = sb("nm", [P, H * J])
        nmr = sb("nmr", [H * J, P])
        nmp = sb("nmp", [H * J, 3, P], BF16)
        gx = sb("gx", [P, C, N])
        fl = sb("fl", [P, C, N])
        PT = sb("PT", [P, 2, QH, N])
        OT = sb("OT", [P, 2, N])
        rec = sb("rec", [P, 2, J * QH])
        O = sb("O", [P, J, D])
        comb = sb("comb", [P, C, N])
        flat = [W1[:, :, :].rearrange("p c n -> p (c n)"), W2[:, :, :].rearrange("p c n -> p (c n)"),
                hT[:, :, :].rearrange("p c n -> p (c n)")]
        back = [f[:, k:k + D] for f in flat for k in range(0, f.shape[1], D)]
        NT = B * J
        assert len(back) >= NT
        PA = ctx.enter_context(nc.psum_tensor("PA", [P, 2, 512], F32))
        PB = ctx.enter_context(nc.psum_tensor("PB", [P, 4, 512], F32))
        PC = ctx.enter_context(nc.psum_tensor("PC", [P, 2, 512], F32))

        w_in, nbg_ready, ones_ready = sem("w_in"), sem("nbg_ready"), sem("ones_ready")
        in_loaded, ex_loaded = sem("in_loaded"), sem("ex_loaded")
        qk_done, v_done = sem("qk_done"), sem("v_done")
        part1_ready, rest_ready, part2_ready, part3_ready = (sem(f"part{k}_ready") if k else sem("rest_ready") for k in (1, 0, 2, 3))
        v_ready, parts_out, stacked = sem("v_ready"), sem("parts_out"), sem("stacked")
        xt_done, xt_ready, h_done, h_ready = sem("xt_done"), sem("xt_ready"), sem("h_done"), sem("h_ready")
        y_done, y_ready, y_out = sem("y_done"), sem("y_ready"), sem("y_out")
        max_done, max_taken, nmT_done, nmp_ready, nm_placed = (sem(n) for n in ("max_done", "max_taken", "nmT_done", "nmp_ready", "nm_placed"))
        gate_done, flow_done, gx_ready, fl_ready = sem("gate_done"), sem("flow_done"), sem("gx_ready"), sem("fl_ready")
        s_done, e_done, pt_used, av_done, ot_ready = (sem(n) for n in ("s_done", "e_done", "pt_used", "av_done", "ot_ready"))
        ot_turned, rec_ready, o_taken = sem("ot_turned"), sem("rec_ready"), sem("o_taken")
        ot_done, comb_ready, wo_done, x_added = (sem(n) for n in ("ot_done", "comb_ready", "wo_done", "x_added"))
        v2_step, moe_added = sem("v2_step"), sem("moe0_added")
        gathered = [sem(f"gathered0_{g}") for g in range(NG)]
        NSTACK = 2 * len(PAIRS)
        NM = H * J // 2
        NU = NG * J

        with nc.Block() as block:
            @block.sync
            def _(sp):
                def load(b):
                    sp.dma_start(xnTb[:, :, :], T["xnT"][ds(b, 1), :, :, :].squeeze(0)).then_inc(in_loaded, 16)
                    sp.dma_start(inflb[:, :], T["inflT"][ds(b, 1), :, :].squeeze(0)).then_inc(in_loaded, 16)
                    sp.dma_start(decb[:, :], T["dec"][ds(b, 1), :, :].squeeze(0)).then_inc(in_loaded, 16)

                load(0)
                for name, t in (("Wq", Wq), ("Wk", Wk), ("Wv", Wv), ("Wo", Wo), ("Wg", Wg)):
                    sp.dma_start(t[:, :, :], T[name].rearrange("(c p) n -> p c n", p=P)).then_inc(w_in, 16)
                for c in range(C):
                    sp.dma_start(nbg[:, c:c + 1], column(T["bg"][c * P:(c + 1) * P])).then_inc(w_in, 16)

                def stack(b):
                    for w in range(2):
                        for k, ready in enumerate((part1_ready, part2_ready, part3_ready)):
                            sp.wait_ge(ready, b * 2 + w + 1)
                            sp.dma_start(T["parts"][w, k].rearrange("(c p) n -> p c n", p=P), parts[:, w, k, :, :]).then_inc(parts_out, 16)
                    if not (isinstance(b, int) and b == 0):
                        sp.wait_ge(s_done, b * 2 * NU)
                    sp.wait_ge(parts_out, b * 96 + 96)
                    for n, pair in enumerate(PAIRS):
                        for w, st in ((0, Qs), (1, Ks)):
                            sp.dma_start(st[n * DH:(n + 1) * DH, :, :],
                                         T["parts"][w, pair[w]].rearrange("(h d) n -> d h n", d=DH)).then_inc(stacked, 16)

                stack(0)

                def body(i, last):
                    sp.wait_ge(nmp_ready, i + 1)
                    for k in range(3):
                        sp.dma_start(Qs[R + k:R + k + 1, :, :].rearrange("o h (j n) -> o (h j) n", n=P), nmp[:, k, :]).then_inc(nm_placed, 16)
                    if not last:
                        sp.wait_ge(flow_done, i + 1)
                        load(i + 1)
                        stack(i + 1)
                loop(sp, B, body)

            @block.gpsimd
            def _(pool):
                def load(e):
                    nc.gpsimd.dma_start(W1[:, :, :], T["W1"][ds(e, 1)].squeeze(0).rearrange("(c p) n -> p c n", p=P)).then_inc(ex_loaded, 16)
                    nc.gpsimd.dma_start(W2[:, :, :], T["W2"][ds(e, 1)].squeeze(0).rearrange("(c p) n -> p c n", p=P)).then_inc(ex_loaded, 16)
                    nc.gpsimd.dma_start(xe[:, :, :], T["xe"][ds(e * N, N), :].rearrange("(j p) d -> p j d", p=P)).then_inc(ex_loaded, 16)

                def third_part(b):
                    for w in range(2):
                        pool.wait_ge(part2_ready, b * 2 + w + 1)
                        nc.gpsimd.tensor_tensor(parts[:, w, 2, :, :], rest[:, w, :, :], parts[:, w, 1, :, :],
                                                ALU.subtract).then_inc(part3_ready, 1)

                pool.wait_ge(w_in, 16 * (5 + C))
                load(0)
                third_part(0)

                def body(i, last):
                    if not last:
                        wait_apart(pool, y_done, i * J + J, (ones_ready, 2))
                        load(i + 1)
                        third_part(i + 1)
                loop(pool, B, body)
                pool.wait_ge(y_out, 16 * (B + 1))
                for t in range(NT):
                    nc.gpsimd.indirect_dma_start(
                        out=back[t], out_offset=None, in_=T["ye"],
                        in_offset=bass.IndirectOffsetOnAxis(ap=take0[:, t:t + 1], axis=0),
                        bounds_check=B * N - 1, oob_is_err=False).then_inc(gathered[t * NG // NT], 16)

            @block.scalar
            def _(act):
                A = nc.scalar.activation

                def values_in(b):
                    if not (isinstance(b, int) and b == 0):
                        act.wait_ge(pt_used, b * NU + 2)
                    for j in range(J):
                        if j % 2 == 0:
                            act.wait_ge(v_done, b * 2 + j // 2 + 1)
                        A(V[:, j, :, 0:DH], PA[:, j // 2, j % 2 * D:(j % 2 + 1) * D].rearrange("p (h d) -> p h d", d=DH),
                          ACT.Copy).then_inc(v_ready, 1)

                act.wait_ge(ones_ready, 1)
                act.wait_ge(w_in, 16 * (5 + C))
                A(nbg[:, :], nbg[:, :], ACT.Copy, scale=-1.0).then_inc(nbg_ready, 1)
                act.wait_ge(nbg_ready, 1)
                values_in(0)
                act.sem_inc(y_out, 16)

                def tokens_in(i):
                    act.wait_ge(xt_done, i + 1)
                    A(xeT[:, :, :], PB[:, 0:2, :], ACT.Copy).then_inc(xt_ready, 1)

                def hidden(i, f):
                    act.wait_ge(h_done, i * FT + (f + 1))
                    A(hT[:, f, :], PB[:, f % 4, :], ACT.Relu).then_inc(h_ready, 1)

                tokens_in(0)
                hidden(0, 0)
                hidden(0, 1)

                def exps(i, u):
                    for g in range(2):
                        if g == 0:
                            act.wait_ge(pt_used, i * NU + (u + 1))
                        act.wait_ge(s_done, i * 2 * NU + (2 * u + g + 1))
                        A(PT[:, u % 2, 2 * g:2 * g + 2, :], PB[:, 2 * g:2 * g + 2, :], ACT.Exp).then_inc(e_done, 1)

                def body(i, last):
                    for f in range(2, FT):
                        hidden(i, f)
                    act.wait_ge(y_out, i * 16 + 16)
                    for j in range(J):
                        act.wait_ge(y_done, i * J + (j + 1))
                        A(ysb[:, j, :], PB[:, j, 0:D], ACT.Copy).then_inc(y_ready, 1)
                    act.wait_ge(y_ready, i * J + J)
                    act.dma_start(T["ye"][ds(i * N, N), :].rearrange("(j p) d -> p j d", p=P), ysb[:, :, :]).then_inc(y_out, 16)
                    act.wait_ge(gate_done, i + 1)
                    for c in range(C):
                        gate_exp = A(gx[:, c, :], PB[:, c, :], ACT.Exp, scale=-1.0, bias=nbg[:, c:c + 1])
                    gate_exp.then_inc(gx_ready, 1)
                    for u in range(NU):
                        exps(i, u)
                    if not last:
                        tokens_in(i + 1)
                        values_in(i + 1)
                        hidden(i + 1, 0)
                        hidden(i + 1, 1)
                loop(act, B, body)
                act.wait_ge(y_out, 16 * (B + 1))

            @block.tensor
            def _(pe):
                M = nc.tensor.matmul

                def project(b, u):
                    w, n = divmod(u, 5)
                    if n == 4:
                        return
                    if u == 0:
                        pe.wait_ge(in_loaded, b * 48 + 48)
                    if w < 2:
                        m, c = divmod(n, C)
                        if n == 0 and w == 1:
                            pe.wait_ge(rest_ready, b * 2 + 1)
                        mm = M(PA[:, m, :], (Wq, Wk)[w][:, c, m * P:(m + 1) * P], xnTb[:, c, :], start=(c == 0), stop=(c == C - 1))
                        if n == 3:
                            mm.then_inc(qk_done, 1)
                    elif w == 2:
                        if n == 0:
                            pe.wait_ge(rest_ready, b * 2 + 2)
                        for c in range(C):
                            mm = M(PA[:, n // 2, n % 2 * D:(n % 2 + 1) * D], xnTb[:, c, n * P:(n + 1) * P], Wv[:, c, :],
                                   start=(c == 0), stop=(c == C - 1))
                        if n % 2:
                            mm.then_inc(v_done, 1)

                def scores(i, u):
                    hg, c = divmod(u, J)
                    for g in range(2):
                        if u == 0:
                            pe.wait_ge((gx_ready, fl_ready)[g], i + 1)
                        else:
                            pe.wait_ge(e_done, i * 2 * NU + (2 * u + g - 1))
                        for q in (2 * g, 2 * g + 1):
                            h = hg * QH + q
                            mm = M(PB[:, q, :], Ks[:, h, c * P:(c + 1) * P], Qs[:, h, :], start=True, stop=True)
                        mm.then_inc(s_done, 1)

                def values(i, u):
                    hg, c = divmod(u, J)
                    pe.wait_ge(e_done, i * 2 * NU + (2 * u + 2))
                    for q in range(QH):
                        mm = M(PC[32 * q:32 * q + 32, 0, :], V[:, c, hg * QH + q, :], PT[:, u % 2, q, :],
                               start=(c == 0), stop=(c == J - 1))
                    mm.then_inc(pt_used, 1)

                def turn_values(i, hg):
                    pe.wait_ge(ot_ready, i * NG + (hg + 1))
                    pe.wait_ge(o_taken, i * NG + (hg + 1))
                    for j in range(J):
                        mm = nc.tensor.transpose(PC[:, 1, j * P:(j + 1) * P], OT[:, hg % 2, j * P:(j + 1) * P], ident[:, :])
                    mm.then_inc(ot_turned, 1)

                pe.wait_ge(w_in, 16 * (5 + C))
                pe.sem_inc(pt_used, 2)
                for u in range(NU):
                    project(0, u)

                def turn_tokens(i):
                    pe.wait_ge(ex_loaded, i * 48 + 48)
                    for j in range(J):
                        for c in range(C):
                            mm = nc.tensor.transpose(PB[:, c, j * P:(j + 1) * P], xe[:, j, c * P:(c + 1) * P], ident[:, :])
                    mm.then_inc(xt_done, 1)

                def hidden(i, f, between=None):
                    if f == 0:
                        pe.wait_ge(xt_ready, i + 1)
                    if f == 2:
                        pe.wait_ge(x_added, i * 2 + 2)
                    if f >= 4:
                        pe.wait_ge(h_ready, i * FT + (f - 3))
                    for c in range(C):
                        mm = M(PB[:, f % 4, :], W1[:, c, f * P:(f + 1) * P], xeT[:, c, :], start=(c == 0), stop=(c == C - 1))
                        if c == C - 1:
                            mm.then_inc(h_done, 1)
                        if between:
                            between()

                turn_tokens(0)
                hidden(0, 0)
                hidden(0, 1)

                def body(i, last):
                    n_max = [0]

                    def maxima(count=1):
                        for n in range(n_max[0], min(n_max[0] + count, NM)):
                            if n == 0:
                                pe.wait_ge(stacked, i * 16 * NSTACK + 16 * NSTACK)
                                pe.wait_ge(v_ready, i * J + J)
                            if n >= 2:
                                pe.wait_ge(max_taken, i * NM + (n - 1))
                            for k in range(2):
                                h, j = divmod(2 * n + k, J)
                                mm = M((PA, PC)[n % 2][:, k, :], Qs[0:R, h, j * P:(j + 1) * P], Ks[0:R, h, :], start=True, stop=True)
                            mm.then_inc(max_done, 1)
                        n_max[0] += count

                    for f in range(2, FT):
                        hidden(i, f, maxima)
                    pe.wait_ge(h_ready, i * FT + FT)
                    for j in range(J):
                        for f in range(FT):
                            mm = M(PB[:, j, 0:D], hT[:, f, j * P:(j + 1) * P], W2[:, f, :], start=(f == 0), stop=(f == FT - 1))
                            if f == FT - 1:
                                mm.then_inc(y_done, 1)
                            if f % 2:
                                maxima()
                    pe.wait_ge(y_ready, i * J + C)
                    for m in range(C):
                        for c in range(C):
                            mm = M(PB[:, m, :], Wg[:, c, m * P:(m + 1) * P], xnTb[:, c, :], start=(c == 0), stop=(c == C - 1))
                            if m == c == C - 1:
                                mm.then_inc(gate_done, 1)
                            maxima()
                    maxima(NM)
                    wait_apart(pe, max_taken, i * NM + NM, (w_in, 16))
                    nc.tensor.transpose(PC[0:H * J, 0, 0:P], nm[:, :], ident[:, :]).then_inc(nmT_done, 1)
                    pe.wait_ge(y_ready, i * J + J)
                    for m in range(C):
                        mm = M(PB[:, 2 + m, :], decb[:, m * P:(m + 1) * P], inflb[:, :], start=True, stop=True)
                    mm.then_inc(flow_done, 1)
                    pe.wait_ge(ones_ready, 2)
                    pe.wait_ge(nm_placed, i * 48 + 48)
                    pe.wait_ge(v_ready, i * J + J)
                    scores(i, 0)
                    for u in range(NU):
                        if u + 1 < NU:
                            scores(i, u + 1)
                        if not last:
                            project(i + 1, u)
                        if u % J == 0 and u:
                            pe.wait_ge(ot_ready, i * NG + u // J)
                        values(i, u)
                        if u % J == 1 and u > J:
                            turn_values(i, u // J - 1)
                    if not last:
                        turn_tokens(i + 1)
                    turn_values(i, NG - 1)
                    if not last:
                        hidden(i + 1, 0)
                    pe.wait_ge(o_taken, i * NG + (NG + 1))
                    for c in range(C):
                        for j in range(J):
                            mm = nc.tensor.transpose(PC[:, c, j * P:(j + 1) * P], O[:, j, c * P:(c + 1) * P], ident[:, :])
                    mm.then_inc(ot_done, 1)
                    if not last:
                        hidden(i + 1, 1)
                    pe.wait_ge(comb_ready, i + 1)
                    for j in range(J):
                        for c in range(C):
                            mm = M(PB[:, 2 + j // 2, j % 2 * D:(j % 2 + 1) * D], comb[:, c, j * P:(j + 1) * P], Wo[:, c, :],
                                   start=(c == 0), stop=(c == C - 1))
                        if j % 2:
                            mm.then_inc(wo_done, 1)
                loop(pe, B, body)

            @block.vector
            def _(ve):
                v = nc.vector
                st = Steps(ve, v2_step, (ones_ready, 1))

                def cut(b, w):
                    ve.wait_ge(qk_done, b * 2 + w + 1)
                    if not (isinstance(b, int) and b == 0):
                        ve.wait_ge(parts_out, b * 96)
                    scale = DH ** -0.5 if w == 0 else 1.0
                    v.tensor_scalar(parts[:, w, 0, :, :], PA[:, :, :], scale, None, ALU.mult).then_inc(part1_ready, 1)
                    ve.wait_ge(part1_ready, b * 2 + w + 1)
                    if not (isinstance(b, int) and b == 0):
                        ve.wait_ge(part3_ready, b * 2)
                    v.scalar_tensor_tensor(out=rest[:, w, :, :], in0=PA[:, :, :], scalar=scale,
                                           in1=parts[:, w, 0, :, :], op0=ALU.mult, op1=ALU.subtract).then_inc(rest_ready, 1)
                    ve.wait_ge(rest_ready, b * 2 + w + 1)
                    v.tensor_copy(parts[:, w, 1, :, :], rest[:, w, :, :]).then_inc(part2_ready, 1)

                v.memset(V[:, :, :, :], 1.0).then_inc(ones_ready, 1)
                v.memset(Ks[R:R + 3, :, :], 1.0).then_inc(ones_ready, 1)
                cut(0, 0)
                cut(0, 1)
                ve.sem_inc(x_added, 2)
                ve.sem_inc(o_taken, 1)

                def experts_in(g):
                    ve.wait_ge(gathered[g], 16 * NT // NG)
                    if g == NG - 1:
                        ve.wait_ge(x_added, 2 * B + 2)
                    for t in range(g * NT // NG, (g + 1) * NT // NG):
                        la = v.scalar_tensor_tensor(out=x_all[:, t, :], in0=back[t], scalar=pkeep0[:, t:t + 1], in1=x_all[:, t, :],
                                                    op0=ALU.mult, op1=ALU.add)
                    la.then_inc(moe_added, 1)

                def body(i, last):
                    for n in range(NM):
                        ve.wait_ge(max_done, i * NM + (n + 1))
                        v.tensor_reduce(nm[:, 2 * n:2 * n + 2], (PA, PC)[n % 2][:, :, :], AX.X, ALU.max, negate=True).then_inc(max_taken, 1)
                    ve.wait_ge(nmT_done, i + 1)
                    rows = PC[0:H * J, 0, 0:P]
                    st.link(v.tensor_copy(nmp[:, 0, :], rows))
                    st.link(v.tensor_tensor(nmr[:, :], rows, nmp[:, 0, :], ALU.subtract))
                    st.link(v.tensor_copy(nmp[:, 1, :], nmr[:, :]))
                    v.tensor_tensor(nmp[:, 2, :], nmr[:, :], nmp[:, 1, :], ALU.subtract).then_inc(nmp_ready, 1)
                    ve.wait_ge(flow_done, i + 1)
                    v.tensor_scalar(fl[:, :, :], PB[:, 2:4, :], 0.4, None, ALU.mult).then_inc(fl_ready, 1)
                    ve.wait_ge(gx_ready, i + 1)
                    st.link(v.tensor_scalar(gx[:, :, :], gx[:, :, :], 1.0, None, ALU.add))
                    st.link(v.reciprocal(gx[:, :, :], gx[:, :, :]))
                    ve.wait_ge(fl_ready, i + 1)
                    v.tensor_tensor(fl[:, :, :], fl[:, :, :], gx[:, :, :], ALU.mult)
                    for hg in range(NG):
                        ve.wait_ge(pt_used, i * NU + ((hg + 1) * J + 2))
                        v.tensor_copy(OT[:, hg % 2, :], PC[:, 0, :]).then_inc(ot_ready, 1)
                        if hg < 2 and not last:
                            cut(i + 1, hg)
                        ve.wait_ge(ot_turned, i * NG + (hg + 1))
                        o = PC[:, 1, :].rearrange("p (j q d) -> p j q d", j=J, q=QH)
                        r = rec[:, hg % 2, :].rearrange("p (j q) -> p j q", j=J)
                        v.reciprocal(r, o[:, :, :, DH]).then_inc(rec_ready, 1)
                        ve.wait_ge(rec_ready, i * NG + (hg + 1))
                        v.tensor_tensor(O[:, :, hg * QH * DH:(hg + 1) * QH * DH].rearrange("p j (q d) -> p j q d", q=QH), o[:, :, :, 0:DH],
                                        r.unsqueeze(3).to_broadcast([P, J, QH, DH]), ALU.mult).then_inc(o_taken, 1)
                        if last and hg:
                            experts_in(hg - 1)
                    ve.wait_ge(ot_done, i + 1)
                    v.scalar_tensor_tensor(out=comb[:, :, :], in0=PC[:, :, :], scalar=0.6, in1=fl[:, :, :],
                                           op0=ALU.mult, op1=ALU.add).then_inc(comb_ready, 1)
                    for q in range(2):
                        ve.wait_ge(wo_done, i * 2 + (q + 1))
                        xs = x_all[:, ds(i * J + 2 * q, 2), :]
                        v.tensor_tensor(xs, PB[:, 2 + q, :].rearrange("p (j d) -> p j d", j=2), xs, ALU.add).then_inc(x_added, 1)
                loop(ve, B, body, st, 5)
                experts_in(NG - 1)
        clear(nc, used)


def phase_middle(nc, T, G):
    B, N, D = T["x"].shape
    E = T["rw"].shape[1]
    C, J = D // P, N // P
    NT = B * J
    NS = 2 * B * N // P + E - 1
    DT = 0.01
    GAMMA_FLOOR = 0.1
    x_all, y_all, ident, ones, strict, mhalf = (G[n] for n in ("x_all", "y_all", "ident", "ones", "strict", "mhalf"))
    slot1, weight1, tile_expert = (G[n] for n in ("slot1", "weight1", "tile_expert"))
    dcol, ccol, gate, lin, decay_mask = (G[n] for n in ("dcol", "ccol", "gate", "lin", "decay_mask"))
    anti, moe_w_in = G["anti"], G["moe_w_in"]
    with ExitStack() as ctx:
        used = []

        def sb(name, shape, dt=F32):
            return ctx.enter_context(nc.sbuf_tensor(name, shape, dt))

        def sem(name):
            used.append(ctx.enter_context(nc.semaphore(name)))
            return used[-1]

        incl = sb("incl", [P, P])
        pref = sb("pref", [P, E])
        steps128 = sb("steps128", [P, NT])
        tile_no = sb("tile_no", [P, NS])
        spare = G["Wqkv"][:, :, :].rearrange("p c n -> p (c n)")
        yT = spare[:, 0:C * N].rearrange("p (c n) -> p c n", n=N)
        stats = sb("stats3", [P, J, 6])
        stats2 = sb("stats32", [P, J, 6])
        mvb = sb("mvb", [P, 2, J, 2])
        vb = sb("vb", [P, J])
        rb1 = sb("rstdx", [P, J])
        mv = sb("mv3", [P, NT, 2])
        msq = sb("msq", [P, J])
        var2 = sb("var2", [P, 2, J])
        rs = sb("rs", [P, 2, NT])
        proj = sb("proj", [P, C, E + 2])
        pv = sb("pv", [P, C, 4])
        lb = sb("lb", [P, C, P])
        wpot = sb("wpot", [P, C, 2])
        consts2 = sb("consts2", [P, 4])
        psc = sb("psc", [P, E])
        bpot = sb("bpot", [P, 2])
        y = sb("y", [P, J, D])
        lg = sb("lg3", [P, NT, E + 2])
        ra, rb, oh1, oh2, oh12 = (sb(n, [P, NT, E]) for n in ("ra1", "rb1", "oh1", "oh2", "oh12"))
        pot = sb("pot", [P, 3, NT])
        gam = sb("gam", [P, NT])
        small = sb("small3", [P, 8, NT])
        base = sb("base3", [P, 4, E])
        tcmp = sb("tcmp", [1, NS, E])
        turned = sb("turned", [3 * NT, 2, P])
        tp = ctx.enter_context(nc.psum_tensor("tp3", [P, C, N], F32))
        lgp = ctx.enter_context(nc.psum_tensor("lgp3", [P, 512], F32))
        rkp = ctx.enter_context(nc.psum_tensor("rkp3", [P, 2, 512], F32))
        cp = ctx.enter_context(nc.psum_tensor("cp3", [P, 2, 512], F32))
        lgv = lgp[:, 0:J * (E + 2)].rearrange("p (j e) -> p j e", e=E + 2)

        c_ready, w_in, var2_ready, rs2_ready = sem("c3_ready"), sem("w3_in"), sem("var2_ready"), sem("rs2_ready")
        var_ready, rs_ready, y_ready = sem("var3_ready"), sem("rs3_ready"), sem("yl_ready")
        tp_ready, yT_ready, lg_done, lg_copied = sem("tp3_ready"), sem("yT_ready"), sem("lg3_done"), sem("lg3_copied")
        proj_ready, sums_done, y_kept = sem("proj_ready"), sem("sums_done"), sem("y_kept")
        r_sub, r_exp, oh_ready, rank_done, slots_ready = (sem(n) for n in ("r3_sub", "r3_exp", "oh3_ready", "rank3_done", "slots3_ready"))
        sp_in, sp_exp, sp_ln, gam_ready, cum_done, cols_ready = (
            sem(n) for n in ("sp_in", "sp_exp", "sp_ln", "gam_ready", "cum_done", "cols_ready"))
        rows_done, rows_ready, rows_out = sem("rows_done"), sem("rows_ready"), sem("rows_out")
        v_step, p_step, x1_out = sem("v3_step"), sem("p3_step"), sem("x1_out")
        NW = C * 4 + 3

        with nc.Block() as block:
            @block.sync
            def _(sp):
                for c in range(C):
                    part = slice(c * P, (c + 1) * P)
                    sp.dma_start(pv[:, c, 0:1], column(T["rscale"][part])).then_inc(w_in, 16)
                    sp.dma_start(pv[:, c, 1:2], column(T["ln1_g"][part])).then_inc(w_in, 16)
                    sp.dma_start(pv[:, c, 2:3], column(T["ln1_b"][part])).then_inc(w_in, 16)
                    sp.dma_start(proj[:, c, 0:E], T["rw"][part, :]).then_inc(w_in, 16)
                sp.dma_start(wpot[:, :, :], T["w_pot"].rearrange("(c p) n -> p c n", p=P)).then_inc(w_in, 16)
                sp.dma_start(psc[:, :], row_of(T["pscale"], P)).then_inc(w_in, 16)
                sp.dma_start(bpot[:, :], row_of(T["b_pot"], P)).then_inc(w_in, 16)
                sp.dma_start(T["x1"], x_all[:, :, :]).then_inc(x1_out, 16)
                for e in range(E):
                    for c in range(C):
                        sp.dma_start(gate[:, c, e, :], T["gate"][e, c * P:(c + 1) * P].rearrange("p g h -> p (g h)")).then_inc(moe_w_in, 16)
                    sp.dma_start(lin[:, e, :, :], T["lin"][e].rearrange("(f p) d -> p f d", p=P)).then_inc(moe_w_in, 16)
                sp.wait_ge(rows_ready, 2)
                for k in range(2):
                    sp.dma_start(T["drow"][k].rearrange("c b (j n) -> (c b j) n", n=P), turned[0:2 * NT, k, :]).then_inc(rows_out, 16)
                sp.dma_start(T["crow"].rearrange("b (j n) -> (b j) n", n=P), turned[2 * NT:3 * NT, 0, :]).then_inc(rows_out, 16)
                sp.wait_ge(rows_out, 48)
                sp.wait_ge(x1_out, 16)

            @block.gpsimd
            def _(pool):
                st = Steps(pool, p_step)
                st.link(nc.gpsimd.memset(incl[:, :], 0.0))
                st.link(nc.gpsimd.memset(anti[:, :], 0.0))
                st.link(nc.gpsimd.memset(decay_mask[:, :], 0.1))
                nc.gpsimd.affine_select(out=incl[:, :], in_=incl[:, :], compare_op=ALU.is_ge, fill=1.0,
                                        base=-1, pattern=[[-1, P]], channel_multiplier=1).then_inc(c_ready, 1)
                nc.gpsimd.affine_select(out=anti[:, :], in_=anti[:, :], compare_op=ALU.not_equal, fill=1.0,
                                        base=1 - P, pattern=[[1, P]], channel_multiplier=1).then_inc(c_ready, 1)
                nc.gpsimd.affine_select(out=decay_mask[:, :], in_=decay_mask[:, :], compare_op=ALU.is_ge, fill=0.0,
                                        base=0, pattern=[[1, N]], channel_multiplier=-1).then_inc(c_ready, 1)
                for tile, pattern, first in ((pref, [[-1, E]], E), (steps128, [[P, NT]], 0), (tile_no, [[1, NS]], 0)):
                    nc.gpsimd.iota(tile[:, :], pattern=pattern, base=first, channel_multiplier=0,
                                   allow_small_or_imprecise_dtypes=True).then_inc(c_ready, 1)
                with pool.Fori(0, B) as b:
                    pool.wait_ge(var_ready, b + 1)
                    nc.gpsimd.tensor_tensor(rb1[:, :], vb[:, :], mhalf[:, 0:J], ALU.pow).then_inc(rs_ready, 1)
                    pool.wait_ge(var2_ready, b + 1)
                    nc.gpsimd.tensor_tensor(rs[:, :, ds(b * J, J)], var2[:, :, :], mhalf[:, 0:2 * J].rearrange("p (k j) -> p k j", k=2),
                                            ALU.pow).then_inc(rs2_ready, 1)

            @block.scalar
            def _(act):
                A = nc.scalar.activation
                act.sem_inc(yT_ready, 1)
                act.sem_inc(lg_copied, 1)
                act.sem_inc(y_kept, 1)
                with act.Fori(0, B) as b:
                    act.wait_ge(tp_ready, b + 2)
                    act.wait_ge(lg_done, b + 1)
                    A(yT[:, :, :], tp[:, :, :], ACT.Copy).then_inc(yT_ready, 1)
                    A(y_all[:, ds(b * J, J), :], y[:, :, :], ACT.Copy).then_inc(y_kept, 1)
                    act.wait_ge(lg_done, b + 2)
                    A(lg[:, ds(b * J, J), :], lgv, ACT.Copy).then_inc(lg_copied, 1)
                act.wait_ge(r_sub, 1)
                A(rb[:, :, :], ra[:, :, :], ACT.Exp).then_inc(r_exp, 1)
                act.wait_ge(sp_in, 1)
                A(small[:, 1, :], small[:, 0, :], ACT.Exp, scale=-1.0).then_inc(sp_exp, 1)
                act.wait_ge(sp_exp, 1)
                A(small[:, 2, :], small[:, 1, :], ACT.Ln, bias=1.0).then_inc(sp_ln, 1)
                act.wait_ge(rows_done, 1)
                A(turned[:, 0, :], cp[0:3 * NT, 0, 0:P], ACT.Copy).then_inc(rows_ready, 1)
                A(turned[0:2 * NT, 1, :], cp[0:2 * NT, 1, 0:P], ACT.Copy).then_inc(rows_ready, 1)

            @block.tensor
            def _(pe):
                M = nc.tensor.matmul
                pe.wait_ge(proj_ready, 2)
                for c in range(C):
                    M(cp[:, 0, 0:2], ones[:, :], proj[:, c, E:E + 2], start=(c == 0), stop=(c == C - 1))
                for c in range(C):
                    last = M(cp[:, 0, 2:4], lb[:, c, :], wpot[:, c, :], start=(c == 0), stop=(c == C - 1))
                last.then_inc(sums_done, 1)
                pe.sem_inc(lg_done, 1)
                pe.sem_inc(tp_ready, 1)
                with pe.Fori(0, B) as b:
                    pe.wait_ge(y_ready, b + 1)
                    pe.wait_ge(yT_ready, b + 1)
                    for j in range(J):
                        for c in range(C):
                            last = nc.tensor.transpose(tp[:, c, j * P:(j + 1) * P], y[:, j, c * P:(c + 1) * P], ident[:, :])
                    last.then_inc(tp_ready, 1)
                    pe.wait_ge(yT_ready, b + 2)
                    pe.wait_ge(lg_copied, b + 1)
                    for j in range(J):
                        for c in range(C):
                            last = M(lgv[:, j, :], yT[:, c, j * P:(j + 1) * P], proj[:, c, :], start=(c == 0), stop=(c == C - 1))
                    last.then_inc(lg_done, 1)
                pe.wait_ge(gam_ready, 1)
                M(cp[:, 0, 0:NT], incl[:, :], gam[:, :], start=True, stop=True)
                M(cp[:, 1, 0:NT], ones[:, :], gam[:, :], start=True, stop=True).then_inc(cum_done, 1)
                pe.wait_ge(oh_ready, 3)
                ohf = oh12[:, :, :].rearrange("p t e -> p (t e)")
                M(rkp[:, 0, 0:NT * E], strict[:, :], ohf, start=True, stop=True)
                M(rkp[:, 1, 0:NT * E], ones[:, :], ohf, start=True, stop=True).then_inc(rank_done, 1)
                pe.wait_ge(cols_ready, 1)
                M(cp[0:3 * NT, 0, 0:P], pot[:, :, :].rearrange("p c t -> p (c t)"), ident[:, :], start=True, stop=True)
                M(cp[0:2 * NT, 1, 0:P], pot[:, 0:2, :].rearrange("p c t -> p (c t)"), anti[:, :], start=True, stop=True).then_inc(rows_done, 1)

            @block.vector
            def _(ve):
                st = Steps(ve, v_step, (c_ready, 6))
                link = st.link
                V = nc.vector

                def moments(b):
                    for j in range(J):
                        la = V.bn_stats(stats[:, j, :], x_all[:, b * J + j, :])
                    link(la, apart=True)
                    for j in range(J):
                        la = V.bn_aggr(mvb[:, 0, j, :], stats[:, j, :])
                    link(la, apart=True)
                    V.tensor_scalar(vb[:, :], mvb[:, 0, :, 1], 1e-5, None, ALU.add).then_inc(var_ready, 1)

                moments(0)
                ve.wait_ge(w_in, 16 * NW)
                ve.wait_ge(c_ready, 6)
                for c in range(C):
                    V.tensor_scalar(proj[:, c, E:E + 2], wpot[:, c, :], pv[:, c, 1:2], None, ALU.mult)
                    V.tensor_scalar(lb[:, c, :], ones[:, :], pv[:, c, 2:3], None, ALU.mult)
                    last = V.tensor_scalar(proj[:, c, 0:E], proj[:, c, 0:E], pv[:, c, 0:1], None, ALU.mult)
                    last.then_inc(proj_ready, 1)
                ve.wait_ge(sums_done, 1)
                V.tensor_copy(consts2[:, 0:2], cp[:, 0, 0:2])
                link(V.tensor_tensor(consts2[:, 2:4], cp[:, 0, 2:4], bpot[:, :], ALU.add))

                def body(b, last):
                    ve.wait_ge(rs_ready, b + 1)
                    ve.wait_ge(tp_ready, b + 1)
                    ve.wait_ge(y_kept, b + 1)
                    for j in range(J):
                        la = V.tensor_scalar(y[:, j, :], x_all[:, ds(b * J + j, 1), :].squeeze(1), mvb[:, 0, j, 0:1],
                                             rb1[:, j:j + 1], ALU.subtract, ALU.mult)
                    la.then_inc(y_ready, 1)
                    wait_apart(ve, y_ready, b + 1, (c_ready, 6))
                    for j in range(J):
                        la = V.bn_stats(stats2[:, j, :], y[:, j, :])
                    link(la, apart=True)
                    for j in range(J):
                        la = V.bn_aggr(mvb[:, 1, j, :], stats2[:, j, :])
                    link(la, apart=True)
                    V.tensor_copy(mv[:, ds(b * J, J), :], mvb[:, 1, :, :])
                    link(V.tensor_tensor(msq[:, :], mvb[:, 1, :, 0], mvb[:, 1, :, 0], ALU.mult))
                    ve.wait_ge(rs2_ready, b + 1)
                    V.tensor_scalar(var2[:, 0, :], mvb[:, 1, :, 1], 1e-5, None, ALU.add)
                    V.scalar_tensor_tensor(out=var2[:, 1, :], in0=msq[:, :], scalar=1e-6, in1=mvb[:, 1, :, 1], op0=ALU.add,
                                           op1=ALU.add).then_inc(var2_ready, 1)
                    if not last:
                        moments(b + 1)

                ve.sem_inc(rs2_ready, 1)
                loop(ve, B, body, st, 5)
                mean = mv[:, :, 0]
                ve.wait_ge(rs2_ready, B + 1)
                ve.wait_ge(lg_copied, B + 1)
                for k in range(2):
                    link(V.scalar_tensor_tensor(out=small[:, 1 + k, :], in0=mean, scalar=consts2[:, k:k + 1], in1=lg[:, :, E + k],
                                                op0=ALU.mult, op1=ALU.subtract))
                    link(V.tensor_tensor(small[:, 3 + k, :], small[:, 1 + k, :], rs[:, 0, :], ALU.mult))
                    link(V.tensor_scalar(small[:, 5 + k, :], small[:, 3 + k, :], -1.0, consts2[:, 2 + k:3 + k], ALU.mult, ALU.add))
                V.tensor_scalar(pot[:, 0, :], small[:, 5, :], 2.0, None, ALU.add)
                link(V.tensor_scalar(small[:, 7, :], small[:, 6, :], -1.0, None, ALU.mult))
                V.tensor_tensor(small[:, 0, :], small[:, 6, :], small[:, 7, :], ALU.max).then_inc(sp_in, 1)
                link(V.tensor_scalar(small[:, 3, :], small[:, 6, :], 0.0, GAMMA_FLOOR, ALU.max, ALU.add))
                link(V.tensor_scalar(small[:, 4, :], rs[:, 1, :], D ** -0.5, None, ALU.mult))
                link(V.tensor_tensor(lg[:, :, 0:E], lg[:, :, 0:E], last_dim(small[:, 4, :], E), ALU.mult))
                link(V.tensor_reduce(small[:, 5, :], lg[:, :, 0:E], AX.X, ALU.max))
                V.tensor_tensor(ra[:, :, :], lg[:, :, 0:E], last_dim(small[:, 5, :], E), ALU.subtract).then_inc(r_sub, 1)
                ve.wait_ge(sp_ln, 1)
                V.tensor_tensor(gam[:, :], small[:, 2, :], small[:, 3, :], ALU.add).then_inc(gam_ready, 1)
                ve.wait_ge(gam_ready, 1)
                V.tensor_scalar(pot[:, 1, :], gam[:, :], -1.0, None, ALU.mult)
                ve.wait_ge(cum_done, 1)
                link(V.tensor_copy(small[:, 0, :], cp[:, 0, 0:NT]))
                link(V.tensor_copy(small[:, 1, :], cp[:, 1, 0:NT]))
                own, whole = (small[:, k, :].rearrange("p (b j) -> p b j", j=J) for k in (0, 1))
                for k in range(1, J):
                    for j in range(J - 1, k - 1, -1):
                        link(V.tensor_tensor(own[:, :, j], own[:, :, j], whole[:, :, j - k], ALU.add))
                link(V.tensor_scalar(ccol[:, :], small[:, 0, :], DT, None, ALU.mult))
                link(V.tensor_copy(dcol[:, :, :], pot[:, 0:2, :]))
                V.tensor_copy(pot[:, 2, :], ccol[:, :]).then_inc(cols_ready, 1)
                ve.wait_ge(r_exp, 1)
                link(V.tensor_reduce(small[:, 0, :], rb[:, :, :], AX.X, ALU.add))
                link(V.reciprocal(small[:, 1, :], small[:, 0, :]))
                link(V.tensor_tensor(rb[:, :, :], rb[:, :, :], last_dim(small[:, 1, :], E), ALU.mult))
                for k, oh in ((0, oh1), (1, oh2)):
                    if k == 1:
                        link(V.scalar_tensor_tensor(out=lg[:, :, 0:E], in0=oh1[:, :, :], scalar=-3e38, in1=lg[:, :, 0:E], op0=ALU.mult, op1=ALU.add))
                        link(V.tensor_reduce(small[:, 5, :], lg[:, :, 0:E], AX.X, ALU.max))
                    link(V.tensor_tensor(ra[:, :, :], lg[:, :, 0:E], last_dim(small[:, 5, :], E), ALU.is_equal))
                    link(V.tensor_tensor(oh12[:, :, :], ra[:, :, :], mid_dim(pref[:, :], NT), ALU.mult))
                    link(V.tensor_reduce(small[:, 6, :], oh12[:, :, :], AX.X, ALU.max))
                    V.tensor_tensor(oh[:, :, :], oh12[:, :, :], last_dim(small[:, 6, :], E), ALU.is_equal).then_inc(oh_ready, 1)
                    ve.wait_ge(oh_ready, k + 1)
                V.tensor_tensor(oh12[:, :, :], oh1[:, :, :], oh2[:, :, :], ALU.add).then_inc(oh_ready, 1)
                for k, oh in ((0, oh1), (1, oh2)):
                    link(V.tensor_tensor(ra[:, :, :], rb[:, :, :], oh[:, :, :], ALU.mult))
                    link(V.tensor_reduce(small[:, k, :], ra[:, :, :], AX.X, ALU.add))
                    link(V.tensor_tensor(ra[:, :, :], oh[:, :, :], mid_dim(psc[:, :], NT), ALU.mult))
                    link(V.tensor_reduce(small[:, 2 + k, :], ra[:, :, :], AX.X, ALU.add))
                link(V.tensor_tensor(small[:, 4, :], small[:, 0, :], small[:, 1, :], ALU.add))
                link(V.scalar_tensor_tensor(out=small[:, 5, :], in0=small[:, 4, :], scalar=0.0, in1=small[:, 4, :], op0=ALU.is_le, op1=ALU.add))
                link(V.reciprocal(small[:, 6, :], small[:, 5, :]))
                for k in range(2):
                    link(V.tensor_tensor(small[:, k, :], small[:, k, :], small[:, 6, :], ALU.mult))
                    link(V.tensor_tensor(weight1[:, k, :], small[:, k, :], small[:, 2 + k, :], ALU.mult))
                ve.wait_ge(rank_done, 1)
                before = rkp[:, 0, 0:NT * E].rearrange("p (t e) -> p t e", e=E)
                count = rkp[:, 1, 0:NT * E].rearrange("p (t e) -> p t e", e=E)
                link(V.tensor_copy(ra[:, :, :], count))
                a, z, k = ra, rb, 1
                while k < NT:
                    link(V.tensor_copy(z[:, 0:k, :], a[:, 0:k, :]))
                    link(V.tensor_tensor(z[:, k:NT, :], a[:, k:NT, :], a[:, 0:NT - k, :], ALU.add))
                    a, z, k = z, a, 2 * k
                total = base[:, 0, :]
                link(V.tensor_copy(total, a[:, NT - 1, :]))
                lgt = lg[:, :, 0:E]
                link(V.tensor_tensor(lgt, mid_dim(total, NT), last_dim(steps128[:, :], E), ALU.is_gt))
                link(V.tensor_reduce(base[:, 1, :], lgt.rearrange("p t e -> p e t"), AX.X, ALU.add))
                link(V.tensor_copy(base[:, 2, :], base[:, 1, :]))
                for e in range(1, E):
                    link(V.tensor_tensor(base[:, 2, e:e + 1], base[:, 2, e:e + 1], base[:, 2, e - 1:e], ALU.add))
                link(V.tensor_tensor(base[:, 3, :], base[:, 2, :], base[:, 1, :], ALU.subtract))
                link(V.tensor_scalar(base[:, 3, :], base[:, 3, :], float(P), None, ALU.mult))
                link(V.tensor_tensor(z[:, :, :], a[:, :, :], count, ALU.subtract))
                link(V.tensor_tensor(a[:, :, :], z[:, :, :], before, ALU.add))
                link(V.tensor_tensor(z[:, :, :], a[:, :, :], mid_dim(base[:, 3, :], NT), ALU.add))
                for k, oh in ((0, oh1), (1, oh2)):
                    link(V.tensor_tensor(a[:, :, :], z[:, :, :], oh[:, :, :], ALU.mult))
                    link(V.tensor_reduce(small[:, 6 + k, :], a[:, :, :], AX.X, ALU.add))
                    V.tensor_copy(slot1[:, k, :], small[:, 6 + k, :]).then_inc(slots_ready, 1)
                link(V.tensor_tensor(tcmp[:, :, :], last_dim(tile_no[0:1, :], E), mid_dim(base[0:1, 2, :], NS), ALU.is_ge))
                link(V.tensor_reduce(tile_no[0:1, :], tcmp[:, :, :], AX.X, ALU.add))
                link(V.tensor_scalar(tile_expert[0:1, 0:NS], tile_no[0:1, :], float(E - 1), None, ALU.min))
        clear(nc, used)


def phase_experts1_scan(nc, T, G):
    B, N, D = T["x"].shape
    E, HID = T["lin"].shape[0], T["lin"].shape[1]
    C, J, FT = D // P, N // P, HID // P
    NS = 2 * B * N // P + E - 1
    NT = B * J
    HW, F = T["w_out"].shape[0], T["w_ff1"].shape[1]
    y_all, ident, gate, lin, tile_expert, slot1 = (G[n] for n in ("y_all", "ident", "gate", "lin", "tile_expert", "slot1"))
    SCAN = 6
    SCAN_TRIPS = NS - 1
    AHEAD = N - SCAN * SCAN_TRIPS
    with ExitStack() as ctx:
        used = []

        def sb(name, shape, dt=F32):
            return ctx.enter_context(nc.sbuf_tensor(name, shape, dt))

        def sem(name):
            used.append(ctx.enter_context(nc.semaphore(name)))
            return used[-1]

        def bank(name, shape):
            return ctx.enter_context(nc.psum_tensor(name, shape, F32))

        xt = sb("xt4", [P, D])
        xT = sb("xT4", [P, C, P])
        gl = sb("gl", [P, HID])
        hid = sb("hid", [P, HID])
        hidT = sb("hidT", [P, FT, P])
        ysb = sb("ysb4", [P, D])
        bbk = sb("bbk", [P, D])
        dz = sb("dz", [2 * B, 2, N])
        z = sb("z", [2 * B, 2, N])
        sgn = sb("sgn", [2 * B, N // 2, 2])
        sq = sb("sq", [2 * B, 2])
        nrm = sb("nrm", [2 * B, 2])
        txp = bank("txp", [P, 4, P])
        gp = bank("gp", [P, 2, HID])
        htp = bank("htp", [P, FT, P])
        yp = bank("yp", [P, 512])

        xs_loaded, tx_done, xT_ready, g_done, gelu_ready, hid_ready = (
            sem(n) for n in ("xs_loaded", "tx_done", "xT4_ready", "g_done", "gelu_ready", "hid_ready"))
        ht_done, hidT_ready, y_done, y_copied, ys_out = (sem(n) for n in ("ht_done", "hidT_ready", "y4_done", "y4_copied", "ys_out"))
        scattered, next_in = sem("scattered1"), sem("next_in")
        d_in, z_ready, z_out, cf_step, b_in, b_added = (sem(n) for n in ("d_in", "zed_ready", "z_out", "cf_step", "bbk_in", "bbk_added"))

        with nc.Block() as block:
            @block.sync
            def _(sp):
                def load(i):
                    sp.dma_start(xt[:, :], T["xs"][ds(i * P, P), :]).then_inc(xs_loaded, 16)

                def store(i):
                    sp.wait_ge(y_copied, i + 2)
                    sp.dma_start(T["ys"][ds(i * P, P), :], ysb[:, :]).then_inc(ys_out, 16)

                sp.dma_start(bbk[:, :], row_of(T["b_bk"], P)).then_inc(b_in, 16)
                sp.dma_start(dz[0:B, :, :], T["drow"][0].rearrange("c b n -> b c n")).then_inc(d_in, 16)
                for j in range(J):
                    sp.dma_start(dz[B:2 * B, :, (J - 1 - j) * P:(J - j) * P],
                                 T["drow"][1].rearrange("c b n -> b c n")[:, :, j * P:(j + 1) * P]).then_inc(d_in, 16)
                for k in range(2):
                    sp.dma_start(G["wbk"][:, k, :], row_of(T["w_bk"][k], P)).then_inc(next_in, 16)
                for c in range(C):
                    for k, name in enumerate(("ln2_g", "ln2_b", "ln3_g", "ln3_b")):
                        sp.dma_start(G["cols"][:, c, k:k + 1], column(T[name][c * P:(c + 1) * P])).then_inc(next_in, 16)
                sp.dma_start(G["Wqkv"][:, :, :], T["w_qkv"].rearrange("(c p) n -> p c n", p=P)).then_inc(next_in, 16)
                for m in range(2 * HW // P):
                    sp.dma_start(G["bqk"][:, m:m + 1], column(T["b_qkv"][m * P:(m + 1) * P])).then_inc(next_in, 16)
                for f in range(F // P):
                    sp.dma_start(G["bf1"][:, f:f + 1], column(T["b_ff1"][f * P:(f + 1) * P])).then_inc(next_in, 16)
                for t, vector in ((G["bv"], T["b_qkv"][2 * HW:3 * HW]), (G["bout"], T["b_out"]), (G["bf2"], T["b_ff2"])):
                    sp.dma_start(t[:, :], row_of(vector, P)).then_inc(next_in, 16)
                sp.sem_inc(ys_out, 16)
                sp.wait_ge(scattered, 16 * 2 * NT)
                load(0)
                sp.wait_ge(tx_done, 1)
                load(1)
                sp.wait_ge(tx_done, 2)
                load(2)
                with sp.Fori(0, NS - 3) as k:
                    store(k)
                    sp.wait_ge(tx_done, k + 3)
                    load(k + 3)
                for i in range(NS - 3, NS):
                    store(i)
                sp.wait_ge(z_ready, 1)
                for way in range(2):
                    for c in range(2):
                        sp.dma_start(T["cf"][way, c], z[way * B:(way + 1) * B, c, :]).then_inc(z_out, 16)
                sp.wait_ge(z_out, 64)
                sp.wait_ge(next_in, 16 * (2 + 4 * C + 1 + 2 * HW // P + F // P + 3))
                sp.wait_ge(ys_out, 16 * (NS + 1))

            @block.gpsimd
            def _(pool):
                for t in range(NT):
                    for k in range(2):
                        nc.gpsimd.indirect_dma_start(
                            out=T["xs"], out_offset=bass.IndirectOffsetOnAxis(ap=slot1[:, k, t:t + 1], axis=0),
                            in_=y_all[:, t, :], in_offset=None, bounds_check=NS * P - 1, oob_is_err=False,
                        ).then_inc(scattered, 16)
                pool.wait_ge(b_in, 16)
                pool.wait_ge(scattered, 16 * 2 * NT)
                with pool.Fori(0, B) as b:
                    own = y_all[:, ds(b * J, J), :]
                    nc.gpsimd.tensor_tensor(own, own, mid_dim(bbk[:, :], J), ALU.add).then_inc(b_added, 1)
                pool.wait_ge(b_added, B)

            @block.scalar
            def _(act):
                A = nc.scalar.activation

                def turned_in():
                    A(xT[:, :, :], txp[:, 0:C, :], ACT.Copy).then_inc(xT_ready, 1)

                def outputs(i):
                    act.wait_ge(y_done, i + 1)
                    act.wait_ge(ys_out, i * 16 + 16)
                    A(ysb[:, :], yp[:, 0:D], ACT.Copy).then_inc(y_copied, 1)

                def body(i, first=False, last=False):
                    act.wait_ge(g_done, i * 2 + 1)
                    A(gl[:, :], gp[:, 0, :], ACT.Gelu_apprx_tanh).then_inc(gelu_ready, 1)
                    if not last:
                        act.wait_ge(tx_done, i + 2)
                        turned_in()
                    if not first:
                        outputs(i - 1)
                    act.wait_ge(ht_done, i + 1)
                    A(hidT[:, :, :], htp[:, :, :], ACT.Copy).then_inc(hidT_ready, 1)

                act.sem_inc(y_copied, 1)
                act.wait_ge(tx_done, 1)
                turned_in()
                body(0, first=True)
                with act.Fori(0, NS - 2) as k:
                    body(k + 1)
                body(NS - 1, last=True)
                outputs(NS - 1)

            @block.tensor
            def _(pe):
                M = nc.tensor.matmul

                def turn_in(i):
                    pe.wait_ge(xs_loaded, i * 16 + 16)
                    for c in range(C):
                        mm = nc.tensor.transpose(txp[:, c, :], xt[:, c * P:(c + 1) * P], ident[:, :])
                    mm.then_inc(tx_done, 1)

                def turn_hidden(i):
                    pe.wait_ge(hid_ready, i + 1)
                    pe.wait_ge(hidT_ready, i + 1)
                    for f in range(FT):
                        mm = nc.tensor.transpose(htp[:, f, :], hid[:, f * P:(f + 1) * P], ident[:, :])
                    mm.then_inc(ht_done, 1)

                def gates(i, e):
                    pe.wait_ge(xT_ready, i + 1)
                    for g in range(2):
                        for c in range(C):
                            mm = M(gp[:, g, :], xT[:, c, :], gate[:, c, ds(e, 1), g * HID:(g + 1) * HID].squeeze(1), start=(c == 0), stop=(c == C - 1))
                        mm.then_inc(g_done, 1)

                def outputs(i, e):
                    pe.wait_ge(hidT_ready, i + 2)
                    pe.wait_ge(y_copied, i + 1)
                    for f in range(FT):
                        mm = M(yp[:, 0:D], hidT[:, f, :], lin[:, ds(e, 1), f, :].squeeze(1), start=(f == 0), stop=(f == FT - 1))
                    mm.then_inc(y_done, 1)

                def expert(i):
                    return pe.value_load(tile_expert[0:1, ds(i, 1)], min_val=0, max_val=E - 1)

                pe.wait_ge(G["moe_w_in"], 16 * E * (C + 1))
                turn_in(0)
                pe.sem_inc(hidT_ready, 1)
                gates(0, expert(0))
                turn_in(1)
                with pe.Fori(0, NS - 2) as k:
                    e, e_next = expert(k), expert(k + 1)
                    turn_hidden(k)
                    gates(k + 1, e_next)
                    turn_in(k + 2)
                    outputs(k, e)
                turn_hidden(NS - 2)
                gates(NS - 1, expert(NS - 1))
                outputs(NS - 2, expert(NS - 2))
                turn_hidden(NS - 1)
                outputs(NS - 1, expert(NS - 1))

            @block.vector
            def _(ve):
                V = nc.vector
                st = Steps(ve, cf_step, (d_in, 16))
                link = st.link

                def scan(t):
                    last = z[:, :, ds(t - 1, 1)].squeeze(2)
                    link(V.scalar_tensor_tensor(out=sq[:, :], in0=last, scalar=-1.0, in1=last, op0=ALU.mult, op1=ALU.mult, accum_out=nrm[:, 0:1]))
                    link(V.reciprocal(nrm[:, 1:2], nrm[:, 0:1]))
                    link(V.scalar_tensor_tensor(out=z[:, :, ds(t, 1)].squeeze(2), in0=last, scalar=nrm[:, 1:2], in1=dz[:, :, ds(t, 1)].squeeze(2),
                                                op0=ALU.mult, op1=ALU.add))

                def product(i):
                    ve.wait_ge(gelu_ready, i + 1)
                    ve.wait_ge(g_done, i * 2 + 2)
                    V.tensor_tensor(hid[:, :], gl[:, :], gp[:, 1, :], ALU.mult).then_inc(hid_ready, 1)

                link(V.memset(sgn[:, :, 0:1], 1.0))
                link(V.memset(sgn[:, :, 1:2], -1.0))
                sign = sgn[:, :, :].rearrange("p n s -> p (n s)")
                ve.wait_ge(d_in, 16 * (1 + J))
                link(V.tensor_tensor(dz[:, 1, :], dz[:, 1, :], sign, ALU.mult))
                link(V.tensor_copy(z[:, :, 0], dz[:, :, 0]))
                for t in range(1, AHEAD % SCAN):
                    scan(t)
                with ve.Fori(0, AHEAD // SCAN) as i:
                    st.enter(i, 3 * SCAN)
                    for s in range(SCAN):
                        scan(i * SCAN + (AHEAD % SCAN + s))
                st.leave(AHEAD // SCAN)
                with ve.Fori(0, SCAN_TRIPS) as i:
                    st.enter(i, 3 * SCAN)
                    product(i)
                    for s in range(SCAN):
                        scan(i * SCAN + (AHEAD + s))
                st.leave(SCAN_TRIPS)
                V.tensor_tensor(z[:, 1, :], z[:, 1, :], sign, ALU.mult).then_inc(z_ready, 1)
                with ve.Fori(0, NS - SCAN_TRIPS) as k:
                    product(k + SCAN_TRIPS)
        clear(nc, used)


def phase_attention1(nc, T, G, out):
    B, N, D = T["x"].shape
    E = T["rw"].shape[1]
    C, J = D // P, N // P
    NT = B * J
    HW = T["w_out"].shape[0]
    HP = HW // P
    DH = P // 2
    F = T["w_ff1"].shape[1]
    FT = F // P
    NU = HP * J
    x_all, y_all, ident, anti = G["x_all"], G["y_all"], G["ident"], G["anti"]
    Wqkv, cols, bqk, bf1, bv, wbk, bout, bf2 = (G[n] for n in ("Wqkv", "cols", "bqk", "bf1", "bv", "wbk", "bout", "bf2"))
    mhalf, dcol, ccol, slot1, weight1, decay_mask = (G[n] for n in ("mhalf", "dcol", "ccol", "slot1", "weight1", "decay_mask"))
    with ExitStack() as ctx:
        def sb(name, shape, dt=F32):
            return ctx.enter_context(nc.sbuf_tensor(name, shape, dt))

        def sem(name):
            return ctx.enter_context(nc.semaphore(name))

        Wout = sb("Wout", [P, HP, D])
        Wf1h, Wf1l = sb("Wf1h", [P, C, F], F32R), sb("Wf1l", [P, C, F], F32R)
        Wf2h, Wf2l = sb("Wf2h", [P, FT, D], F32R), sb("Wf2l", [P, FT, D], F32R)
        place = x_all[:, :, :].rearrange("p t d -> p (t d)")
        assert NT * D == 4 * HP * N and C * F == HP * N and FT * D == J * HW
        qkT = place[:, 0:2 * HP * N].rearrange("p (m n) -> p m n", n=N)
        vt = place[:, 2 * HP * N:3 * HP * N].rearrange("p (j n) -> p j n", n=HW)
        hebT = place[:, 3 * HP * N:4 * HP * N].rearrange("p (m n) -> p m n", n=N)
        Wf2 = place[:, 2 * HP * N:3 * HP * N].rearrange("p (f n) -> p f n", n=D)
        Wf1 = place[:, 3 * HP * N:4 * HP * N].rearrange("p (c n) -> p c n", n=F)
        cbc = sb("cbc", [P, N])
        wd = sb("wd", [P, sum(N - c * P for c in range(J))])

        def weights(c):
            first = sum(N - k * P for k in range(c))
            return wd[:, first:first + N - c * P]

        xh2, xh3 = sb("xh2", [P, J, D]), sb("xh3", [P, J, D])
        xT2 = sb("xT2", [P, C, N])
        xT3h, xT3l = sb("xT3h", [P, C, N], F32R), sb("xT3l", [P, C, N], F32R)
        xT3 = xh3[:, :, :].rearrange("p j d -> p (j d)").rearrange("p (c n) -> p c n", n=N)
        stats5 = sb("stats5", [P, J, 6])
        mv5 = sb("mv5", [P, J, 2])
        rv = sb("rv", [P, 2, J])
        pm = sb("pm", [P, 2, 2, N])
        hid = sb("hid5", [P, 2, N])
        hTh, hTl = sb("hTh", [P, FT, N], F32R), sb("hTl", [P, FT, N], F32R)
        gt = sb("gt", [P, 2, J, D])
        ost = sb("ost", [P, J, D])
        fr = pm[0:2 * NT, 0, 0, 0:2 * P].rearrange("p (k n) -> p k n", n=P)
        gf = pm[:, 1, 0, 0:8 * NT].rearrange("p (k t) -> p k t", t=NT)
        fb = pm[:, 1, 1, 0:2 * NT]
        gcol = sb("gcol", [P, 2, NT])
        PA = ctx.enter_context(nc.psum_tensor("PA5", [P, 2, 512], F32))
        PS = ctx.enter_context(nc.psum_tensor("PS5", [P, 4, 512], F32))
        PO = ctx.enter_context(nc.psum_tensor("PO5", [P, 2, 512], F32))

        w_in, c_in, f_in = sem("w5_in"), sem("cbc_in"), sem("f_in")
        f_turned, fb_ready, fb_turned = (sem(n) for n in ("f_turned", "fb_ready", "fb_turned"))
        diff_ready, wexp_ready, wd_ready = (sem(n) for n in ("diff_ready", "wexp_ready", "wd_ready"))
        var_ready, rs_ready, xh2_ready, xh3_ready = (sem(n) for n in ("var5_ready", "rs5_ready", "xh2_ready", "xh3_ready"))
        t2_done, xT2_ready, t3_done, xT3_ready = (sem(n) for n in ("t2_done", "xT2_ready", "t3_done", "xT3_ready"))
        qk_done, qk_ready, v_done, v_ready = (sem(n) for n in ("qk5_done", "qk5_ready", "v5_done", "v5_ready"))
        s_done, p_ready, av_done, heb_ready = (sem(n) for n in ("s5_done", "p5_ready", "av5_done", "heb_ready"))
        wo_done, x3_ready, bout_added, h_done, hid_ready, high_ready, h_ready, f_done, moved = (
            sem(n) for n in ("wo5_done", "x3_ready", "bout_added", "h5_done", "hid5_ready", "high_ready", "h5_ready", "f5_done", "out_ready"))
        res_ready, gathered, moe_added, o_out = (sem(n) for n in ("res_ready", "gathered5", "moe_added", "o_out"))
        v_step, p_step = sem("v5_step"), sem("p5_step")
        w_high, w_low, xT3_full, xT3_high, x_in = (sem(n) for n in ("w_high", "w_low", "xT3_full", "xT3_high", "x5_in"))
        NW = 3

        with nc.Block() as block:
            @block.sync
            def _(sp):
                def load_c(b):
                    sp.dma_start(cbc[:, :], T["crow"][ds(b, 1), :].to_broadcast([P, N])).then_inc(c_in, 16)

                for k in range(2):
                    sp.dma_start(fr[:, k, :], T["cf"][k].rearrange("c b (j n) -> (c b j) n", n=P)).then_inc(f_in, 16)
                load_c(0)
                sp.dma_start(Wout[:, :, :], T["w_out"].rearrange("(c p) n -> p c n", p=P)).then_inc(w_in, 16)
                sp.dma_start(Wf1[:, :, :], T["w_ff1"].rearrange("(c p) n -> p c n", p=P)).then_inc(w_in, 16)
                sp.dma_start(Wf2[:, :, :], T["w_ff2"].rearrange("(c p) n -> p c n", p=P)).then_inc(w_in, 16)

                def body(b, last):
                    sp.wait_ge(o_out, b * 16 * J + 16 * J)
                    sp.dma_start(ost[:, :, :], T["x1"][:, ds(b * J, J), :]).then_inc(x_in, 16)
                    if not last:
                        sp.wait_ge(diff_ready, b + 1)
                        load_c(b + 1)
                    for j in range(J):
                        sp.wait_ge(moved, b * J + (j + 2))
                        sp.dma_start(out[ds(b, 1), j * P:(j + 1) * P, :].squeeze(0), ost[:, j, :]).then_inc(o_out, 16)
                sp.sem_inc(o_out, 16 * J)
                loop(sp, B, body)
                sp.wait_ge(o_out, 16 * (B * J + J))

            @block.gpsimd
            def _(pool):
                st = Steps(pool, p_step)
                Q = nc.gpsimd

                def gather(b):
                    for j in range(J):
                        for k in range(2):
                            t = b * J + j
                            Q.indirect_dma_start(out=gt[:, k, j, :], out_offset=None, in_=T["ys"],
                                                 in_offset=bass.IndirectOffsetOnAxis(ap=slot1[:, k, t:t + 1], axis=0),
                                                 bounds_check=T["ys"].shape[0] - 1, oob_is_err=False).then_inc(gathered, 16)

                def power(n):
                    pool.wait_ge(var_ready, n + 1)
                    Q.tensor_tensor(rv[:, 1, :], rv[:, 0, :], mhalf[:, 0:J], ALU.pow).then_inc(rs_ready, 1)

                def ahead(b):
                    power(2 * b - 1 if b else 0)
                    for c in range(J):
                        if c == 0:
                            pool.wait_ge(wexp_ready, b + 1)
                        Q.tensor_tensor(weights(c), weights(c), decay_mask[:, 0:N - c * P], ALU.mult).then_inc(wd_ready, 1)
                    pool.wait_ge(xh2_ready, b + 1)
                    own = y_all[:, b * J:(b + 1) * J, :]
                    Q.tensor_tensor(own, own, mid_dim(bout[:, :], J), ALU.add).then_inc(bout_added, 1)

                gather(0)
                ahead(0)
                for b in range(B):
                    if b + 1 < B:
                        ahead(b + 1)
                    power(2 * b + 2 if b + 1 < B else 2 * b + 1)
                    pool.wait_ge(xh3_ready, b + 1)
                    own = y_all[:, b * J:(b + 1) * J, :]
                    st.link(Q.tensor_tensor(own, own, mid_dim(bf2[:, :], J), ALU.add))
                    pool.wait_ge(x_in, b * 16 + 16)
                    Q.tensor_tensor(own, own, ost[:, :, :], ALU.add).then_inc(res_ready, 1)
                    if b + 1 < B:
                        pool.wait_ge(moe_added, b + 1)
                        gather(b + 1)

            @block.scalar
            def _(act):
                A = nc.scalar.activation

                def decays(b):
                    act.wait_ge(diff_ready, b + 1)
                    for c in range(J):
                        last = A(weights(c), weights(c), ACT.Exp, scale=-1.0)
                    last.then_inc(wexp_ready, 1)

                def project(b):
                    act.wait_ge(t2_done, b + 1)
                    for c in range(C):
                        last = A(xT2[:, c, :], PA[:, c, :], ACT.Identity, scale=cols[:, c, 0:1], bias=cols[:, c, 1:2])
                    last.then_inc(xT2_ready, 1)
                    for m in range(2 * HP):
                        act.wait_ge(qk_done, b * 2 * HP + (m + 1))
                        A(qkT[:, m, :], PS[:, m % 4, :], ACT.Identity, bias=bqk[:, m:m + 1]).then_inc(qk_ready, 1)

                act.wait_ge(f_turned, 1)
                A(fb, PS[:, 1, 0:2 * NT], ACT.Copy).then_inc(fb_ready, 1)
                act.wait_ge(w_in, 16 * NW)
                A(Wf1h[:, :, :], Wf1, ACT.Copy).then_inc(w_high, 1)
                A(Wf2h[:, :, :], Wf2, ACT.Copy).then_inc(w_high, 1)
                decays(0)
                project(0)

                def body(b, last):
                    for hp in range(HP):
                        act.wait_ge(av_done, b * NU + ((hp + 1) * J + 2))
                        A(hebT[:, hp, :], PO[:, hp % 2, :], ACT.Copy).then_inc(heb_ready, 1)
                    if not last:
                        decays(b + 1)
                        project(b + 1)
                    for c in range(C):
                        act.wait_ge(xT3_full, b * C + (c + 1))
                        A(xT3h[:, c, :], xT3[:, c, :], ACT.Copy).then_inc(xT3_high, 1)
                    for f in range(FT):
                        act.wait_ge(h_ready, b * FT + (f + 1))
                        act.wait_ge(h_done, b * FT + (f + 1))
                        A(hid[:, f % 2, :], PS[:, f % 4, :], ACT.Gelu_apprx_tanh, bias=bf1[:, f:f + 1]).then_inc(hid_ready, 1)
                        act.wait_ge(hid_ready, b * FT + (f + 1))
                        A(hTh[:, f, :], hid[:, f % 2, :], ACT.Copy).then_inc(high_ready, 1)
                loop(act, B, body)

            @block.tensor
            def _(pe):
                M = nc.tensor.matmul

                def turn(xh, done):
                    for c in range(C):
                        for j in range(J):
                            mm = nc.tensor.transpose(PA[:, c, j * P:(j + 1) * P], xh[:, j, c * P:(c + 1) * P], ident[:, :])
                    mm.then_inc(done, 1)

                def turn_next(b):
                    pe.wait_ge(xh2_ready, b + 1)
                    turn(xh2, t2_done)

                def project_qk(b):
                    pe.wait_ge(xT2_ready, b + 1)
                    for m in range(2 * HP):
                        if m < 4:
                            if not (isinstance(b, int) and b == 0):
                                pe.wait_ge(x3_ready, (b - 1) * J + (m + 1))
                        else:
                            pe.wait_ge(qk_ready, b * 2 * HP + (m - 3))
                        for c in range(C):
                            mm = M(PS[:, m % 4, :], Wqkv[:, c, m * P:(m + 1) * P], xT2[:, c, :], start=(c == 0), stop=(c == C - 1))
                        mm.then_inc(qk_done, 1)

                def project_v(b):
                    for j in range(J):
                        pe.wait_ge(qk_ready, b * 2 * HP + (2 * HP - J + j + 1))
                        for c in range(C):
                            mm = M(PS[:, j, 0:HW], xT2[:, c, j * P:(j + 1) * P], Wqkv[:, c, 2 * HW:3 * HW], start=(c == 0), stop=(c == C - 1))
                        mm.then_inc(v_done, 1)

                def scores(b, u):
                    hp, c = divmod(u, J)
                    if u == 0:
                        pe.wait_ge(v_ready, b * J + J)
                        pe.wait_ge(moved, b * J + 1)
                    elif u >= 2:
                        pe.wait_ge(p_ready, b * NU + (u - 1))
                    for e in range(2):
                        half = slice(e * DH, (e + 1) * DH)
                        mm = M(PS[:, 2 * (u % 2) + e, 0:N - c * P], qkT[half, HP + hp, c * P:(c + 1) * P], qkT[half, hp, c * P:N],
                               start=True, stop=True)
                    mm.then_inc(s_done, 1)

                def values(b, u):
                    hp, c = divmod(u, J)
                    if c == 0:
                        pe.wait_ge(heb_ready, b * HP + (hp + 1))
                    pe.wait_ge(p_ready, b * NU + (u + 1))
                    for e in range(2):
                        mm = M(PO[e * DH:(e + 1) * DH, hp % 2, c * P:N], vt[:, c, (2 * hp + e) * DH:(2 * hp + e + 1) * DH], pm[:, u % 2, e, 0:N - c * P],
                               start=(c == 0), stop=(c == J - 1))
                    mm.then_inc(av_done, 1)

                pe.wait_ge(f_in, 32)
                nc.tensor.transpose(PS[:, 0, 0:2 * NT], fr[:, 0, :], ident[0:2 * NT, 0:2 * NT])
                nc.tensor.transpose(PS[:, 1, 0:2 * NT], fr[:, 1, :], ident[0:2 * NT, 0:2 * NT]).then_inc(f_turned, 1)
                pe.wait_ge(fb_ready, 1)
                M(PS[:, 2, 0:2 * NT], anti[:, :], fb, start=True, stop=True).then_inc(fb_turned, 1)
                pe.sem_inc(heb_ready, 2)
                pe.sem_inc(moved, 1)
                pe.sem_inc(av_done, 2)
                turn_next(0)
                project_qk(0)
                project_v(0)
                pe.wait_ge(w_in, 16 * NW)
                pe.sem_inc(h_ready, 2)

                def body(b, last):
                    pe.wait_ge(qk_ready, b * 2 * HP + 2 * HP)
                    pe.wait_ge(v_ready, b * J + J)
                    scores(b, 0)
                    for u in range(NU):
                        if u + 1 < NU:
                            scores(b, u + 1)
                        values(b, u)
                    pe.wait_ge(heb_ready, b * HP + (HP + 2))
                    for j in range(J):
                        if j == J - 1 and not last:
                            turn_next(b + 1)
                        for hp in range(HP):
                            mm = M(PS[:, j, 0:D], hebT[:, hp, j * P:(j + 1) * P], Wout[:, hp, :], start=(hp == 0), stop=(hp == HP - 1))
                        mm.then_inc(wo_done, 1)
                    if not last:
                        project_qk(b + 1)
                    pe.wait_ge(xh3_ready, b + 1)
                    turn(xh3, t3_done)
                    if not last:
                        project_v(b + 1)
                    wait_apart(pe, xT3_ready, b * C + C, (w_low, 2))
                    for f in range(FT):
                        if f >= 4:
                            pe.wait_ge(hid_ready, b * FT + (f - 3))
                        elif not last:
                            pe.wait_ge(v_ready, b * J + (J + f + 1))
                        for n, (w, x) in enumerate(((Wf1h, xT3h), (Wf1l, xT3h), (Wf1h, xT3l))):
                            for c in range(C):
                                mm = M(PS[:, f % 4, :], w[:, c, f * P:(f + 1) * P], x[:, c, :], start=(n + c == 0), stop=(n + c == C + 1))
                        mm.then_inc(h_done, 1)
                    for j in range(J):
                        pe.wait_ge(hid_ready, b * FT + (FT - J + j + 1))
                        for f in range(FT):
                            if j == 0:
                                pe.wait_ge(h_ready, b * FT + (f + 3))
                            for n, (h, w) in enumerate(((hTh, Wf2h), (hTl, Wf2h), (hTh, Wf2l))):
                                mm = M(PS[:, j, 0:D], h[:, f, j * P:(j + 1) * P], w[:, f, :], start=(f + n == 0), stop=(f + n == FT + 1))
                        mm.then_inc(f_done, 1)
                loop(pe, B, body)

            @block.vector
            def _(ve):
                V = nc.vector
                st = Steps(ve, v_step, (fb_turned, 1))
                link = st.link

                def tile(t):
                    return y_all[:, ds(t, 1), :].squeeze(1)

                def norm(b, n, xh, done):
                    for j in range(J):
                        la = V.bn_stats(stats5[:, j, :], tile(b * J + j))
                    link(la, apart=True)
                    for j in range(J):
                        la = V.bn_aggr(mv5[:, j, :], stats5[:, j, :])
                    link(la)
                    V.tensor_scalar(rv[:, 0, :], mv5[:, :, 1], 1e-5, None, ALU.add).then_inc(var_ready, 1)
                    ve.wait_ge(rs_ready, n + 1)
                    for j in range(J):
                        la = V.tensor_scalar(xh[:, j, :], tile(b * J + j), mv5[:, j, 0:1], rv[:, 1, j:j + 1], ALU.subtract, ALU.mult)
                    la.then_inc(done, 1)

                def ahead(b, n):
                    for k in range(2):
                        for j in range(J):
                            la = V.scalar_tensor_tensor(out=tile(b * J + j), in0=wbk[:, k, :], scalar=gcol[:, k, ds(b * J + j, 1)], in1=tile(b * J + j),
                                                        op0=ALU.mult, op1=ALU.add)
                        link(la, apart=True)
                    norm(b, n, xh2, xh2_ready)
                    if not (isinstance(b, int) and b == 0):
                        ve.wait_ge(p_ready, b * NU)
                    ve.wait_ge(c_in, b * 16 + 16)
                    for c in range(J):
                        la = V.tensor_scalar(weights(c), cbc[:, c * P:N], ccol[:, ds(b * J + c, 1)], 0.0, ALU.subtract, ALU.max)
                    la.then_inc(diff_ready, 1)

                def values_in(b):
                    for j in range(J):
                        ve.wait_ge(v_done, b * J + (j + 1))
                        V.tensor_tensor(vt[:, j, :], PS[:, j, 0:HW], bv[:, :], ALU.add).then_inc(v_ready, 1)

                ve.wait_ge(fb_turned, 1)
                bwd = PS[:, 2, 0:2 * NT].rearrange("p (c b j) -> p c b j", c=2, j=J)
                link(V.tensor_tensor(gf[:, 0:2, :], PS[:, 0, 0:2 * NT].rearrange("p (c t) -> p c t", c=2), dcol[:, :, :], ALU.subtract))
                for c in range(2):
                    own = gf[:, c, :].rearrange("p (b j) -> p b j", j=J)
                    for j in range(J):
                        la = V.tensor_tensor(own[:, :, j], bwd[:, c, :, J - 1 - j], own[:, :, j], ALU.add)
                link(la)
                link(V.tensor_tensor(gf[:, 2:4, :], gf[:, 0:2, :], gf[:, 0:2, :], ALU.mult))
                link(V.tensor_tensor(gf[:, 4, :], gf[:, 2, :], gf[:, 3, :], ALU.add))
                link(V.reciprocal(gf[:, 5, :], gf[:, 4, :]))
                V.tensor_tensor(gcol[:, 0, :], gf[:, 0, :], gf[:, 5, :], ALU.mult)
                link(V.scalar_tensor_tensor(out=gcol[:, 1, :], in0=gf[:, 1, :], scalar=-1.0, in1=gf[:, 5, :], op0=ALU.mult, op1=ALU.mult))
                ahead(0, 0)
                for n, (raw, high, low) in enumerate(((Wf1, Wf1h, Wf1l), (Wf2, Wf2h, Wf2l))):
                    ve.wait_ge(w_high, n + 1)
                    V.tensor_tensor(low[:, :, :], raw, high[:, :, :], ALU.subtract).then_inc(w_low, 1)
                ve.wait_ge(w_low, 2)
                values_in(0)

                def body(b, last):
                    for u in range(NU):
                        c = u % J
                        n = N - c * P
                        if u == 0:
                            ve.wait_ge(wd_ready, b * J + J)
                        ve.wait_ge(av_done, b * NU + (u + 1))
                        ve.wait_ge(s_done, b * NU + (u + 1))
                        V.tensor_tensor(pm[:, u % 2, :, 0:n], PS[:, 2 * (u % 2):2 * (u % 2) + 2, 0:n], mid_dim(weights(c), 2), ALU.mult).then_inc(p_ready, 1)
                    if not last:
                        ahead(b + 1, 2 * b + 1)
                    ve.wait_ge(bout_added, b + 1)
                    for j in range(J):
                        ve.wait_ge(wo_done, b * J + (j + 1))
                        V.tensor_tensor(tile(b * J + j), PS[:, j, 0:D], tile(b * J + j), ALU.add).then_inc(x3_ready, 1)
                    wait_apart(ve, x3_ready, b * J + J, (fb_turned, 1))
                    norm(b, 2 * b + (1 if last else 2), xh3, xh3_ready)
                    ve.wait_ge(t3_done, b + 1)
                    for c in range(C):
                        V.tensor_scalar(xT3[:, c, :], PA[:, c, :], cols[:, c, 2:3], cols[:, c, 3:4], ALU.mult, ALU.add).then_inc(xT3_full, 1)
                    for c in range(C):
                        ve.wait_ge(xT3_high, b * C + (c + 1))
                        V.tensor_tensor(xT3l[:, c, :], xT3[:, c, :], xT3h[:, c, :], ALU.subtract).then_inc(xT3_ready, 1)
                    ve.wait_ge(res_ready, b + 1)
                    ve.wait_ge(gathered, b * 16 * 2 * J + 16 * 2 * J)
                    for k in range(2):
                        for j in range(J):
                            la = V.scalar_tensor_tensor(out=tile(b * J + j), in0=gt[:, k, j, :], scalar=weight1[:, k, ds(b * J + j, 1)], in1=tile(b * J + j),
                                                        op0=ALU.mult, op1=ALU.add)
                        if k == 1:
                            la.then_inc(moe_added, 1)
                            ve.wait_ge(moe_added, b + 1)
                        else:
                            link(la, apart=True)
                    if not last:
                        values_in(b + 1)
                    for f in range(FT):
                        ve.wait_ge(high_ready, b * FT + (f + 1))
                        V.tensor_tensor(hTl[:, f, :], hid[:, f % 2, :], hTh[:, f, :], ALU.subtract).then_inc(h_ready, 1)
                    for j in range(J):
                        ve.wait_ge(f_done, b * J + (j + 1))
                        V.tensor_tensor(ost[:, j, :], PS[:, j, 0:D], tile(b * J + j), ALU.add).then_inc(moved, 1)
                loop(ve, B, body, st, 7)


_NAMES = {"x": "L0_attn_x", "Wq": "L0_attn_Wq", "Wk": "L0_attn_Wk", "Wv": "L0_attn_Wv", "Wo": "L0_attn_Wo",
          "splat": "L0_attn_splat_positions", "sscale": "L0_attn_splat_scales", "simp": "L0_attn_splat_importance",
          "We": "L0_attn_We", "be": "L0_attn_be", "Wt": "L0_attn_Wt", "Wd": "L0_attn_Wd",
          "bd": "L0_attn_bd", "Wg": "L0_attn_Wg", "bg": "L0_attn_bg", "Wr": "L0_ffn_Wr", "W1": "L0_ffn_W1",
          "W2": "L0_ffn_W2", "ln1_g": "L1_attn_ln1_g", "ln1_b": "L1_attn_ln1_b", "ln2_g": "L1_attn_ln2_g",
          "ln2_b": "L1_attn_ln2_b", "ln3_g": "L1_attn_ln3_g", "ln3_b": "L1_attn_ln3_b", "w_pot": "L1_attn_w_pot",
          "b_pot": "L1_attn_b_pot", "w_bk": "L1_attn_w_bk", "b_bk": "L1_attn_b_bk", "w_qkv": "L1_attn_w_qkv",
          "b_qkv": "L1_attn_b_qkv", "w_out": "L1_attn_w_out", "b_out": "L1_attn_b_out", "w_ff1": "L1_attn_w_ff1",
          "b_ff1": "L1_attn_b_ff1", "w_ff2": "L1_attn_w_ff2", "b_ff2": "L1_attn_b_ff2",
          "rscale": "L1_ffn_router_scale", "rw": "L1_ffn_router_w", "lin": "L1_ffn_linear_w",
          "pscale": "L1_ffn_per_expert_scale"}


def kernel(**inputs):
    import numpy as _np
    import concourse.bacc as _bacc
    from concourse import mybir as _mybir
    from concourse.bass_utils import run_bass_kernel_spmd as _run

    nc = _bacc.Bacc("TRN2", target_bir_lowering=False, num_devices=1)
    laid = {short: _np.asarray(inputs[name]) for short, name in _NAMES.items()}
    laid["btT"] = _np.asarray(inputs["L0_attn_bt"]).T
    laid["gate"] = _np.asarray(inputs["L1_ffn_gating_w"]).transpose(0, 3, 1, 2)
    arrays, T = {}, {}
    for short, a in laid.items():
        a = _np.ascontiguousarray(a)
        arrays[f"in_{short}"] = a
        T[short] = nc.dram_tensor(f"in_{short}", a.shape, _mybir.dt.from_np(a.dtype), kind="ExternalInput").ap()
    shape = laid["x"].shape
    tokens, width = shape[0] * shape[1], shape[2]
    experts = laid["rw"].shape[1]
    rows2 = 2 * tokens + experts * P
    for name, rows in (("xe", tokens), ("ye", tokens), ("xs", rows2), ("ys", rows2 - P)):
        T[name] = nc.dram_tensor(f"scratch_{name}", (rows, width), F32, kind="Internal").ap()
    T["xnT"] = nc.dram_tensor("scratch_xnT", (shape[0], P, width // P, shape[1]), F32, kind="Internal").ap()
    T["inflT"] = nc.dram_tensor("scratch_inflT", (shape[0], laid["splat"].shape[0], shape[1]), F32, kind="Internal").ap()
    T["dec"] = nc.dram_tensor("scratch_dec", (shape[0], laid["splat"].shape[0], width), F32, kind="Internal").ap()
    T["parts"] = nc.dram_tensor("scratch_parts", (2, 3, width, shape[1]), BF16, kind="Internal").ap()
    T["drow"] = nc.dram_tensor("scratch_drow", (2, 2, shape[0], shape[1]), F32, kind="Internal").ap()
    T["crow"] = nc.dram_tensor("scratch_crow", (shape[0], shape[1]), F32, kind="Internal").ap()
    T["x1"] = nc.dram_tensor("scratch_x1", (P, tokens // P, width), F32, kind="Internal").ap()
    T["cf"] = nc.dram_tensor("scratch_cf", (2, 2, shape[0], shape[1]), F32, kind="Internal").ap()
    out = nc.dram_tensor("out_dram", shape, F32, kind="ExternalOutput").ap()
    build_program(nc, T, out)
    r = _run(nc, [arrays], core_ids=[0])
    return r.results[0]["out_dram"]
```
